# Optimizing a Trainium2 kernel written in Bass

```python
import numpy as np
import jax
import jax.numpy as jnp

def _softmax(x, axis=-1):
    return jax.nn.softmax(x, axis=axis)

def _gelu(x):
    return jax.nn.gelu(x, approximate=True)

def _silu(x):
    return jax.nn.silu(x)

def _sigmoid(x):
    return jax.nn.sigmoid(x)

def _layernorm(x, axis=-1, eps=1e-05):
    m = jnp.mean(x, axis=axis, keepdims=True)
    v = jnp.var(x, axis=axis, keepdims=True)
    return (x - m) / jnp.sqrt(v + eps)

def _scatter_add(tgt, idx, src, axis=0):
    return tgt.at[idx].add(src)

def _segment_sum(src, seg, n):
    return jax.ops.segment_sum(src, seg, n)
kernel_name = 'mk_gnn_ffn_d2_gnn_r32_921f54'

def setup_inputs(seed: int=0):
    np.random.seed(seed)
    _w = jnp.asarray

    def _rec_inputs():
        import jax
        import jax.numpy as jnp
        _gk = jax.random.key(seed)
        x = -0.0003713 + 1 * jax.random.normal(jax.random.fold_in(_gk, 1), (3125, 256), jnp.float32)
        src = jax.random.randint(jax.random.fold_in(_gk, 2), (50000,), 0, 3125, jnp.int32)
        dst = jnp.minimum((3125 * jax.random.uniform(jax.random.fold_in(_gk, 3), (50000,)) ** 2.0).astype(jnp.int32), 99999)
        _o = jnp.argsort(dst, stable=True)
        src = src[_o]
        dst = dst[_o]
        edge_type_8 = jax.random.randint(jax.random.fold_in(_gk, 12), (50000,), 0, 8, jnp.int32)
        node_type_4 = jax.random.randint(jax.random.fold_in(_gk, 13), (3125,), 0, 4, jnp.int32)
        return (x, src, dst, edge_type_8, node_type_4)
    x, src, dst, edge_type_8, node_type_4 = _rec_inputs()

    def _L0_gnn_setup():
        import jax, jax.numpy as jnp
        import numpy as np
        N = 50000
        E = 25000
        DIM = 256
        H = 8
        DH = DIM // H
        SCALE = DH ** (-0.5)
        key = jax.random.key(seed)
        ks = jax.random.split(key, 7)
        h = jax.random.normal(ks[0], (N, DIM), dtype=jnp.float32)
        src = jax.random.randint(ks[1], (E,), 0, N, dtype=jnp.int32)
        dst = jax.random.randint(ks[2], (E,), 0, N, dtype=jnp.int32)
        W_qkv = jax.random.normal(ks[3], (DIM, 3 * DIM), dtype=jnp.float32) * DIM ** (-0.5)
        b_qkv = jnp.zeros((3 * DIM,), dtype=jnp.float32)
        W_out = jax.random.normal(ks[4], (DIM, DIM), dtype=jnp.float32) * DIM ** (-0.5)
        b_out = jnp.zeros((DIM,), dtype=jnp.float32)
        return {'h': h, 'src': src, 'dst': dst, 'W_qkv': W_qkv, 'b_qkv': b_qkv, 'W_out': W_out, 'b_out': b_out}
    _L0_gnn_all = _L0_gnn_setup()
    _L0_gnn_in = {k: v for k, v in _L0_gnn_all.items() if k in ('W_qkv', 'b_qkv', 'W_out', 'b_out')}
    del _L0_gnn_all

    def _L0_ffn_setup():
        import jax, jax.numpy as jnp
        import numpy as np
        E = 8
        K = 2
        D = 256
        H = 512
        DOUT = 256
        EPS = 1e-05
        key = jax.random.key(seed)
        ks = jax.random.split(key, 9)
        s = 0.02
        return {'x': jax.random.normal(ks[0], (4, 256, D), jnp.float32), 'gamma': 1.0 + 0.05 * jax.random.normal(ks[1], (D,), jnp.float32), 'beta': 0.05 * jax.random.normal(ks[2], (D,), jnp.float32), 'Wr': 0.01 * jax.random.normal(ks[3], (D, E), jnp.float32), 'br': jnp.zeros((E,), jnp.float32), 'W1': s * jax.random.normal(ks[4], (E, D, H), jnp.float32), 'b1': s * jax.random.normal(ks[5], (E, H), jnp.float32), 'W2': s * jax.random.normal(ks[6], (E, H, DOUT), jnp.float32), 'b2': s * jax.random.normal(ks[7], (E, DOUT), jnp.float32)}
    _L0_ffn_all = _L0_ffn_setup()
    _L0_ffn_in = {k: v for k, v in _L0_ffn_all.items() if k in ('gamma', 'beta', 'Wr', 'br', 'W1', 'b1', 'W2', 'b2')}
    del _L0_ffn_all

    def _L1_gnn_setup():
        import jax, jax.numpy as jnp
        import numpy as np
        N_NODES = 625
        N_EDGES = 10000
        IN_DIM = 256
        OUT_DIM = 256
        N_HEADS = 4
        D_K = OUT_DIM // N_HEADS
        N_NTYPES = 4
        N_RELS = 8
        SQRT_DK = float(np.sqrt(D_K))

        def _typed_matmul(x, W, node_type):
            all_t = jnp.einsum('ni,tio->tno', x, W)
            return all_t[node_type, jnp.arange(x.shape[0])]
        key = jax.random.key(seed)
        ks = jax.random.split(key, 12)
        xav = lambda k, shape, fan: jax.random.normal(k, shape, jnp.float32) * (1.0 / np.sqrt(fan))
        return {'h': jax.random.normal(ks[0], (N_NODES, IN_DIM), jnp.float32), 'k_linears': xav(ks[1], (N_NTYPES, IN_DIM, OUT_DIM), IN_DIM), 'q_linears': xav(ks[2], (N_NTYPES, IN_DIM, OUT_DIM), IN_DIM), 'v_linears': xav(ks[3], (N_NTYPES, IN_DIM, OUT_DIM), IN_DIM), 'a_linears': xav(ks[4], (N_NTYPES, OUT_DIM, OUT_DIM), OUT_DIM), 'relation_att': xav(ks[5], (N_RELS, N_HEADS, D_K, D_K), D_K), 'relation_msg': xav(ks[6], (N_RELS, N_HEADS, D_K, D_K), D_K), 'relation_pri': jnp.ones((N_RELS, N_HEADS), jnp.float32), 'skip': jnp.ones((N_NTYPES,), jnp.float32), 'node_type': jax.random.randint(ks[7], (N_NODES,), 0, N_NTYPES), 'etype': jnp.sort(jax.random.randint(ks[8], (N_EDGES,), 0, N_RELS)), 'row_idx': jax.random.randint(ks[9], (N_EDGES,), 0, N_NODES), 'col_idx': jax.random.randint(ks[10], (N_EDGES,), 0, N_NODES)}
    _L1_gnn_all = _L1_gnn_setup()
    _L1_gnn_in = {k: v for k, v in _L1_gnn_all.items() if k in ('k_linears', 'q_linears', 'v_linears', 'a_linears', 'relation_att', 'relation_msg', 'relation_pri', 'skip')}
    del _L1_gnn_all

    def _L1_ffn_setup():
        import jax, jax.numpy as jnp
        import numpy as np
        B, N, D = (16, 128, 256)
        NUM_EXPERTS, TOP_K, HEADS = (4, 2, 4)
        N_EDGES = 32768
        LN_EPS = 1e-05

        def _layernorm(x, g, b):
            mu = x.mean(-1, keepdims=True)
            var = ((x - mu) ** 2).mean(-1, keepdims=True)
            return (x - mu) * jax.lax.rsqrt(var + LN_EPS) * g + b

        def _forward(x, edge_index, W_gat, att_src, att_dst, b_gat, ln_gamma, ln_beta, W1, b1, W2, b2):
            Bc, Nc, Dc = x.shape
            M = Bc * Nc
            x_flat = x.reshape(M, Dc)
            h = (x_flat @ W_gat).reshape(M, HEADS, NUM_EXPERTS)
            loops = jnp.arange(M, dtype=edge_index.dtype)
            src = jnp.concatenate([edge_index[0], loops])
            dst = jnp.concatenate([edge_index[1], loops])
            a_src = (h * att_src).sum(-1)
            a_dst = (h * att_dst).sum(-1)
            e = jax.nn.leaky_relu(a_src[src] + a_dst[dst], negative_slope=0.2)
            e_max = jax.ops.segment_max(e, dst, num_segments=M)
            ee = jnp.exp(e - e_max[dst])
            denom = jax.ops.segment_sum(ee, dst, num_segments=M)
            alpha = ee / (denom[dst] + 1e-16)
            msg = h[src] * alpha[:, :, None]
            agg = jax.ops.segment_sum(msg, dst, num_segments=M).reshape(M, HEADS * NUM_EXPERTS) + b_gat
            scores = _layernorm(agg, ln_gamma, ln_beta).reshape(M, HEADS, NUM_EXPERTS).mean(1)
            scores = scores.reshape(Bc, Nc, NUM_EXPERTS)
            topk_s, topk_i = jax.lax.top_k(scores, TOP_K)
            w = jax.nn.softmax(topk_s, axis=-1)
            out = jnp.zeros_like(x)
            for ei in range(NUM_EXPERTS):
                g = jnp.where(topk_i == ei, w, 0.0).sum(-1)
                hh = jax.nn.gelu(x @ W1[ei] + b1[ei], approximate=False)
                out = out + g[..., None] * (hh @ W2[ei] + b2[ei])
            return out
        key = jax.random.key(seed)
        ks = jax.random.split(key, 8)
        s = 0.05
        return {'x': jax.random.normal(ks[0], (B, N, D), jnp.float32), 'W_gat': jax.random.normal(ks[1], (D, HEADS * NUM_EXPERTS), jnp.float32) * s, 'att_src': jax.random.normal(ks[2], (HEADS, NUM_EXPERTS), jnp.float32) * s, 'att_dst': jax.random.normal(ks[3], (HEADS, NUM_EXPERTS), jnp.float32) * s, 'b_gat': jnp.zeros((HEADS * NUM_EXPERTS,), jnp.float32), 'ln_gamma': jnp.ones((HEADS * NUM_EXPERTS,), jnp.float32), 'ln_beta': jnp.zeros((HEADS * NUM_EXPERTS,), jnp.float32), 'W1': jax.random.normal(ks[4], (NUM_EXPERTS, D, 2 * D), jnp.float32) * s, 'b1': jnp.zeros((NUM_EXPERTS, 2 * D), jnp.float32), 'W2': jax.random.normal(ks[5], (NUM_EXPERTS, 2 * D, D), jnp.float32) * s, 'b2': jnp.zeros((NUM_EXPERTS, D), jnp.float32), 'edge_index': jax.random.randint(ks[6], (2, N_EDGES), 0, B * N, jnp.int32)}
    _L1_ffn_all = _L1_ffn_setup()
    _L1_ffn_in = {k: v for k, v in _L1_ffn_all.items() if k in ('W_gat', 'att_src', 'att_dst', 'b_gat', 'ln_gamma', 'ln_beta', 'W1', 'b1', 'W2', 'b2', 'edge_index')}
    del _L1_ffn_all
    return {'x': x, 'src': src, 'dst': dst, 'edge_type_8': edge_type_8, 'node_type_4': node_type_4, 'L0_gnn_W_qkv': _L0_gnn_in['W_qkv'], 'L0_gnn_b_qkv': _L0_gnn_in['b_qkv'], 'L0_gnn_W_out': _L0_gnn_in['W_out'], 'L0_gnn_b_out': _L0_gnn_in['b_out'], 'L0_ffn_gamma': _L0_ffn_in['gamma'], 'L0_ffn_beta': _L0_ffn_in['beta'], 'L0_ffn_Wr': _L0_ffn_in['Wr'], 'L0_ffn_br': _L0_ffn_in['br'], 'L0_ffn_W1': _L0_ffn_in['W1'], 'L0_ffn_b1': _L0_ffn_in['b1'], 'L0_ffn_W2': _L0_ffn_in['W2'], 'L0_ffn_b2': _L0_ffn_in['b2'], 'L1_gnn_k_linears': _L1_gnn_in['k_linears'], 'L1_gnn_q_linears': _L1_gnn_in['q_linears'], 'L1_gnn_v_linears': _L1_gnn_in['v_linears'], 'L1_gnn_a_linears': _L1_gnn_in['a_linears'], 'L1_gnn_relation_att': _L1_gnn_in['relation_att'], 'L1_gnn_relation_msg': _L1_gnn_in['relation_msg'], 'L1_gnn_relation_pri': _L1_gnn_in['relation_pri'], 'L1_gnn_skip': _L1_gnn_in['skip'], 'L1_ffn_W_gat': _L1_ffn_in['W_gat'], 'L1_ffn_att_src': _L1_ffn_in['att_src'], 'L1_ffn_att_dst': _L1_ffn_in['att_dst'], 'L1_ffn_b_gat': _L1_ffn_in['b_gat'], 'L1_ffn_ln_gamma': _L1_ffn_in['ln_gamma'], 'L1_ffn_ln_beta': _L1_ffn_in['ln_beta'], 'L1_ffn_W1': _L1_ffn_in['W1'], 'L1_ffn_b1': _L1_ffn_in['b1'], 'L1_ffn_W2': _L1_ffn_in['W2'], 'L1_ffn_b2': _L1_ffn_in['b2'], 'L1_ffn_edge_index': _L1_ffn_in['edge_index']}

def reference(x, src, dst, edge_type_8, node_type_4, L0_gnn_W_qkv, L0_gnn_b_qkv, L0_gnn_W_out, L0_gnn_b_out, L0_ffn_gamma, L0_ffn_beta, L0_ffn_Wr, L0_ffn_br, L0_ffn_W1, L0_ffn_b1, L0_ffn_W2, L0_ffn_b2, L1_gnn_k_linears, L1_gnn_q_linears, L1_gnn_v_linears, L1_gnn_a_linears, L1_gnn_relation_att, L1_gnn_relation_msg, L1_gnn_relation_pri, L1_gnn_skip, L1_ffn_W_gat, L1_ffn_att_src, L1_ffn_att_dst, L1_ffn_b_gat, L1_ffn_ln_gamma, L1_ffn_ln_beta, L1_ffn_W1, L1_ffn_b1, L1_ffn_W2, L1_ffn_b2, L1_ffn_edge_index):
    import jax
    import jax.numpy as jnp

    def _L0_gnn_ref(h, src, dst, W_qkv, b_qkv, W_out, b_out):
        import jax, jax.numpy as jnp
        import numpy as np
        N = 50000
        E = 25000
        DIM = 256
        H = 8
        DH = DIM // H
        SCALE = DH ** (-0.5)
        n = h.shape[0]
        qkv = (h @ W_qkv + b_qkv).reshape(n, 3, H, DH)
        q, k, v = (qkv[:, 0], qkv[:, 1], qkv[:, 2])
        score = jnp.einsum('ehd,ehd->eh', q[dst], k[src]) * SCALE
        mx = jax.ops.segment_max(score, dst, num_segments=n)
        ex = jnp.exp(score - mx[dst])
        denom = jax.ops.segment_sum(ex, dst, num_segments=n)
        attn = ex / denom[dst]
        msg = attn[:, :, None] * v[src]
        h_new = jax.ops.segment_sum(msg, dst, num_segments=n)
        h_out = jnp.transpose(h_new, (0, 2, 1)).reshape(n, DIM)
        return (h_out + h) @ W_out + b_out

    def _L0_ffn_ref(x, gamma, beta, Wr, br, W1, b1, W2, b2):
        import jax, jax.numpy as jnp
        import numpy as np
        E = 8
        K = 2
        D = 256
        H = 512
        DOUT = 256
        EPS = 1e-05
        mu = jnp.mean(x, axis=-1, keepdims=True)
        var = jnp.mean(jnp.square(x - mu), axis=-1, keepdims=True)
        xn = (x - mu) * jax.lax.rsqrt(var + EPS) * gamma + beta
        logits = jnp.einsum('bsd,de->bse', xn, Wr) + br
        top_vals, top_idx = jax.lax.top_k(logits, K)
        w = jax.nn.softmax(top_vals, axis=-1)
        w_full = jnp.einsum('bsk,bske->bse', w, jax.nn.one_hot(top_idx, E, dtype=w.dtype))
        y = jnp.zeros(x.shape[:-1] + (DOUT,), x.dtype)
        for e in range(E):
            h = jax.nn.gelu(jnp.einsum('bsd,dh->bsh', xn, W1[e]) + b1[e], approximate=False)
            y_e = jnp.einsum('bsh,hd->bsd', h, W2[e]) + b2[e]
            y = y + y_e * w_full[..., e, None]
        return y

    def _L1_gnn_ref(h, k_linears, q_linears, v_linears, a_linears, relation_att, relation_msg, relation_pri, skip, node_type, etype, row_idx, col_idx):
        import jax, jax.numpy as jnp
        import numpy as np
        N_NODES = 625
        N_EDGES = 10000
        IN_DIM = 256
        OUT_DIM = 256
        N_HEADS = 4
        D_K = OUT_DIM // N_HEADS
        N_NTYPES = 4
        N_RELS = 8
        SQRT_DK = float(np.sqrt(D_K))

        def _typed_matmul(x, W, node_type):
            all_t = jnp.einsum('ni,tio->tno', x, W)
            return all_t[node_type, jnp.arange(x.shape[0])]
        n = h.shape[0]
        k = _typed_matmul(h, k_linears, node_type).reshape(n, N_HEADS, D_K)
        q = _typed_matmul(h, q_linears, node_type).reshape(n, N_HEADS, D_K)
        v = _typed_matmul(h, v_linears, node_type).reshape(n, N_HEADS, D_K)
        q_att = jnp.einsum('nhd,rhde->rnhe', q, relation_att)
        v_msg = jnp.einsum('nhd,rhde->rnhe', v, relation_msg)
        aw_q_edge = q_att[etype, col_idx]
        msg_edge = v_msg[etype, row_idx]
        attn_score = jnp.sum(aw_q_edge * k[row_idx], axis=-1)
        score = attn_score * (relation_pri[etype] / SQRT_DK)
        m = jax.ops.segment_max(score, col_idx, num_segments=n)
        ex = jnp.exp(score - m[col_idx])
        denom = jax.ops.segment_sum(ex, col_idx, num_segments=n)
        alpha = ex / denom[col_idx]
        agg = jax.ops.segment_sum(alpha[..., None] * msg_edge, col_idx, num_segments=n)
        agg = agg.reshape(n, OUT_DIM)
        out = _typed_matmul(agg, a_linears, node_type)
        out = jax.nn.sigmoid(skip)[node_type][:, None] * out
        return out

    def _L1_ffn_ref(x, W_gat, att_src, att_dst, b_gat, ln_gamma, ln_beta, W1, b1, W2, b2, edge_index):
        import jax, jax.numpy as jnp
        import numpy as np
        B, N, D = (16, 128, 256)
        NUM_EXPERTS, TOP_K, HEADS = (4, 2, 4)
        N_EDGES = 32768
        LN_EPS = 1e-05

        def _layernorm(x, g, b):
            mu = x.mean(-1, keepdims=True)
            var = ((x - mu) ** 2).mean(-1, keepdims=True)
            return (x - mu) * jax.lax.rsqrt(var + LN_EPS) * g + b

        def _forward(x, edge_index, W_gat, att_src, att_dst, b_gat, ln_gamma, ln_beta, W1, b1, W2, b2):
            Bc, Nc, Dc = x.shape
            M = Bc * Nc
            x_flat = x.reshape(M, Dc)
            h = (x_flat @ W_gat).reshape(M, HEADS, NUM_EXPERTS)
            loops = jnp.arange(M, dtype=edge_index.dtype)
            src = jnp.concatenate([edge_index[0], loops])
            dst = jnp.concatenate([edge_index[1], loops])
            a_src = (h * att_src).sum(-1)
            a_dst = (h * att_dst).sum(-1)
            e = jax.nn.leaky_relu(a_src[src] + a_dst[dst], negative_slope=0.2)
            e_max = jax.ops.segment_max(e, dst, num_segments=M)
            ee = jnp.exp(e - e_max[dst])
            denom = jax.ops.segment_sum(ee, dst, num_segments=M)
            alpha = ee / (denom[dst] + 1e-16)
            msg = h[src] * alpha[:, :, None]
            agg = jax.ops.segment_sum(msg, dst, num_segments=M).reshape(M, HEADS * NUM_EXPERTS) + b_gat
            scores = _layernorm(agg, ln_gamma, ln_beta).reshape(M, HEADS, NUM_EXPERTS).mean(1)
            scores = scores.reshape(Bc, Nc, NUM_EXPERTS)
            topk_s, topk_i = jax.lax.top_k(scores, TOP_K)
            w = jax.nn.softmax(topk_s, axis=-1)
            out = jnp.zeros_like(x)
            for ei in range(NUM_EXPERTS):
                g = jnp.where(topk_i == ei, w, 0.0).sum(-1)
                hh = jax.nn.gelu(x @ W1[ei] + b1[ei], approximate=False)
                out = out + g[..., None] * (hh @ W2[ei] + b2[ei])
            return out
        return _forward(x, edge_index, W_gat, att_src, att_dst, b_gat, ln_gamma, ln_beta, W1, b1, W2, b2)
    x = x + _L0_gnn_ref(_layernorm(x, axis=-1), src, dst, L0_gnn_W_qkv, L0_gnn_b_qkv, L0_gnn_W_out, L0_gnn_b_out)
    x = x + _L0_ffn_ref(_layernorm(x, axis=-1)[None], L0_ffn_gamma, L0_ffn_beta, L0_ffn_Wr, L0_ffn_br, L0_ffn_W1, L0_ffn_b1, L0_ffn_W2, L0_ffn_b2)[0]
    x = x + _L1_gnn_ref(_layernorm(x, axis=-1), L1_gnn_k_linears, L1_gnn_q_linears, L1_gnn_v_linears, L1_gnn_a_linears, L1_gnn_relation_att, L1_gnn_relation_msg, L1_gnn_relation_pri, L1_gnn_skip, node_type_4, edge_type_8, src, dst)
    x = x + _L1_ffn_ref(_layernorm(x, axis=-1)[None], L1_ffn_W_gat, L1_ffn_att_src, L1_ffn_att_dst, L1_ffn_b_gat, L1_ffn_ln_gamma, L1_ffn_ln_beta, L1_ffn_W1, L1_ffn_b1, L1_ffn_W2, L1_ffn_b2, L1_ffn_edge_index)[0]
    return x

_drawn_inputs = setup_inputs


def setup_inputs(seed=0):
    import zlib

    import numpy as np

    out = dict(_drawn_inputs(seed))
    spreads = {'L0_gnn_b_qkv': (0.0, 0.1),
     'L0_gnn_b_out': (0.0, 0.1),
     'L0_ffn_br': (0.0, 0.1),
     'L1_gnn_relation_pri': (1.0, 0.2),
     'L1_gnn_skip': (1.0, 0.6),
     'L1_ffn_b_gat': (0.0, 0.1),
     'L1_ffn_ln_gamma': (1.0, 0.2),
     'L1_ffn_ln_beta': (0.0, 0.1),
     'L1_ffn_b1': (0.0, 0.1),
     'L1_ffn_b2': (0.0, 0.1)}
    factors = {'L0_ffn_gamma': 4.942,
     'L0_ffn_beta': 4.162,
     'L0_ffn_b1': 5.622,
     'L1_ffn_att_dst': 21.57,
     'L0_ffn_b2': 2.928}
    for name, (base, spread) in spreads.items():
        noise = np.random.default_rng([zlib.crc32(name.encode()), seed]).standard_normal(out[name].shape)
        drawn = base * np.exp(spread * noise) if base else spread * noise
        out[name] = jnp.asarray(drawn.astype(out[name].dtype))
    for name, factor in factors.items():
        out[name] = (out[name] * factor).astype(out[name].dtype)
    return out
```

```python
from contextlib import ExitStack, contextmanager

import numpy as np

import concourse.bass as bass
from concourse import mybir

P = 128
N, D = 3125, 256
NT = 25
NP = NT * P
GROUP = 5
E0 = 50000
ET = 392
ETP = 400
EP = ETP * P
CH, CG = 16, 25
STEPS = ET + NT - 1
SP_ = 512
U = 8
GE = 32768
GT = GE // P
H = 8
BIG = 1.0e30
LN_EPS = 1e-5

ALU = mybir.AluOpType
ACT = mybir.ActivationFunctionType
AX = mybir.AxisListType.X
F32, I32, BF = mybir.dt.float32, mybir.dt.int32, mybir.dt.bfloat16


class Chain:

    def __init__(self, eng, sem, start=0, base=None):
        self.eng, self.sem, self.n, self.base = eng, sem, start, base

    def mark(self, ins):
        ins.then_inc(self.sem, 1)
        self.n += 1

    def sync(self):
        self.eng.wait_ge(self.sem, self.n if self.base is None else self.base + self.n)

    def __call__(self, ins):
        self.mark(ins)
        self.sync()


class Kernel:

    def __init__(self, nc, io, out, ctx, dump):
        self.nc, self.io, self.out, self.ctx, self.dumpto = nc, io, out, ctx, dump
        self.nsem = 0

        self.sems = []

    def sem(self, name):
        self.nsem += 1
        self.sems.append(self.nc.alloc_semaphore(name=f"{name}_{self.nsem}"))
        return self.sems[-1]

    @contextmanager
    def block(self):
        with self.nc.Block() as block:
            yield block
        self.nc.clear_and_free_semaphores(self.sems)
        self.nc.all_engine_barrier()
        self.sems = []

    def sb(self, ctx, name, shape, dt=F32):
        self.nsem += 1
        return ctx.enter_context(self.nc.sbuf_tensor(f"{name}_{self.nsem}", shape, dt))

    def ps(self, ctx, name, shape=(P, 512), dt=F32):
        self.nsem += 1
        return ctx.enter_context(self.nc.psum_tensor(f"{name}_{self.nsem}", list(shape), dt))

    def dram(self, name, shape, dt=F32):
        return self.nc.dram_tensor(name, shape, dt, kind="Internal").ap()


def bc(ap, shape):
    return ap.to_broadcast(list(shape))


def row_bc(ap, parts):
    return ap.partition_broadcast(parts)


def setup(k):
    nc, ctx, io = k.nc, k.ctx, k.io
    k.x = k.sb(ctx, "x", [P, NT, D])
    k.ident = k.sb(ctx, "ident", [P, P])
    k.iota = k.sb(ctx, "iota", [P, P])
    k.pair0 = k.sb(ctx, "pair0", [P, ETP, 2], I32)
    k.pair1 = k.sb(ctx, "pair1", [P, ETP, 2], I32)
    k.step_src = k.sb(ctx, "step_src", [P, SP_], I32)
    k.step_rel = k.sb(ctx, "step_rel", [P, SP_], I32)
    k.step_loc = k.sb(ctx, "step_loc", [P, SP_])
    k.step_tile = k.sb(ctx, "step_tile", [P, 4], I32)
    k.step_block = k.sb(ctx, "step_block", [1, SP_], I32)
    k.gpair = k.sb(ctx, "gpair", [P, GT + 2 * U, 2], I32)
    k.mask_pos = k.sb(ctx, "mask_pos", [P, GT], I32)
    k.glo = k.sb(ctx, "glo", [P, GT])
    k.ghi = k.sb(ctx, "ghi", [P, GT])
    k.ntype = k.sb(ctx, "ntype", [P, NP])
    k.mean = k.sb(ctx, "mean", [P, NT])
    k.rstd = k.sb(ctx, "rstd", [P, NT])
    k.stats = k.sb(ctx, "stats", [P, NT, 6])
    k.tmp1 = k.sb(ctx, "tmp1", [P, NT])
    k.tmp2 = k.sb(ctx, "tmp2", [P, NT])
    k.eps = k.sb(ctx, "eps", [P, 1])

    k.q_d = k.dram("q_d", [NP, D])
    k.k_d = k.dram("k_d", [NP, D])
    k.v_d = k.dram("v_d", [NP, D])
    k.kr_d = k.dram("kr_d", [NP * 8, D])
    k.vr_d = k.dram("vr_d", [NP * 8, D])
    k.rec_d = k.dram("rec_d", [ETP, 3 * P])
    k.ex_d = k.dram("ex_d", [ETP, H * P])
    k.ends_d = k.dram("ends_d", [P, 4])
    k.full_d = k.dram("full_d", [8, 32])
    k.mask_d = k.dram("mask_d", [NP * NP, 1], BF)
    k.asrc_d = k.dram("asrc_d", [4, NP])
    k.gs_d = k.dram("gs_d", [NP, 20])
    k.gd_d = k.dram("gd_d", [NP, 8])


def structure(k):
    nc, io = k.nc, k.io
    with ExitStack() as c:
        rows = k.sb(c, "rows", [100, 3, 4, P], I32)
        rec = k.sb(c, "rec", [100, 4, 3, P])
        rel0 = k.sb(c, "rel0", [P, ETP], I32)
        src0 = k.sb(c, "src0", [P, ETP], I32)
        dst0 = k.sb(c, "dst0", [P, ETP], I32)
        gsrc = k.sb(c, "gsrc", [P, GT + 2 * U], I32)
        gdst = k.sb(c, "gdst", [P, GT + 2 * U], I32)
        dstf = k.sb(c, "dstf", [P, ETP])
        low = k.sb(c, "low", [P, NT - 1])
        cnt = k.sb(c, "cnt", [P, NT - 1])
        ones = k.sb(c, "ones", [P, P])
        scr = k.sb(c, "scr", [P, ETP])
        edge0 = k.sb(c, "edge0", [P, ET])
        sidx = k.sb(c, "sidx", [P, SP_ + 4])
        blk = k.sb(c, "blk", [P, SP_ + 4])
        got = k.sb(c, "got", [P, 4, 3 * P])
        nt_i = k.sb(c, "nt_i", [P, NP], I32)
        gd_f = k.sb(c, "gd_f", [P, GT])
        gs_f = k.sb(c, "gs_f", [P, GT])
        lo_i = k.sb(c, "lo_i", [P, GT], I32)
        pc = k.ps(c, "pc")
        pt = [k.ps(c, f"pt{i}") for i in range(4)]
        s_load, s_gload, s_const, s_v, s_cnt, s_rec, s_recd = [k.sem(x) for x in
            ("loaded", "gate_loaded", "const_done", "dve", "counts_summed", "rec_ready", "rec_stored")]
        s_step, s_got, s_tr = [k.sem(x) for x in ("steps_ready", "got", "turned")]
        with k.block() as block:

            @block.sync
            def _(sp):
                for j, name in enumerate(("src_rows", "rel_rows", "dst_rows")):
                    sp.dma_start(rows[:, j, :, :], io[name].rearrange("(p c) e -> p c e", c=4)).then_inc(s_load, 16)
                sp.dma_start(src0[:, :], io["src_t"]).then_inc(s_load, 16)
                sp.dma_start(dst0[:, :], io["dst_t"]).then_inc(s_load, 16)
                sp.dma_start(rel0[:, :], io["rel_t"]).then_inc(s_load, 16)
                sp.dma_start(nt_i[:, :], row_bc(io["ntype"], P)).then_inc(s_load, 16)
                sp.dma_start(gsrc[:, :], io["gsrc_t"]).then_inc(s_gload, 16)
                sp.dma_start(gdst[:, :], io["gdst_t"]).then_inc(s_gload, 16)
                sp.dma_start(k.x[:, :, :], io["x"].rearrange("(t p) d -> p t d", p=P)).then_inc(s_gload, 16)
                sp.wait_ge(s_rec, 1)
                sp.dma_start(k.rec_d.rearrange("(p c) f -> p c f", c=4),
                             rec[:, :, :, :].rearrange("p c j e -> p c (j e)")).then_inc(s_recd, 16)

            @block.gpsimd
            def _(g):
                g.memset(k.ident[:, :], 0.0).then_inc(s_const, 1)
                g.wait_ge(s_const, 1)
                g.affine_select(out=k.ident[:, :], in_=k.ident[:, :], compare_op=ALU.not_equal, fill=1.0,
                                base=0, pattern=[[-1, P]], channel_multiplier=1).then_inc(s_const, 1)
                g.iota(k.iota[:, :], [[1, P]], base=0, channel_multiplier=0,
                       allow_small_or_imprecise_dtypes=True).then_inc(s_const, 1)
                g.iota(edge0[:, :], [[P, ET]], base=0, channel_multiplier=0,
                       allow_small_or_imprecise_dtypes=True).then_inc(s_const, 1)
                g.iota(sidx[:, 0:SP_], [[1, SP_]], base=0, channel_multiplier=0,
                       allow_small_or_imprecise_dtypes=True).then_inc(s_const, 1)
                g.iota(sidx[:, SP_:], [[P, 4]], base=0, channel_multiplier=1,
                       allow_small_or_imprecise_dtypes=True).then_inc(s_const, 1)
                g.wait_ge(s_step, 1)
                g.wait_ge(s_recd, 16)
                for j in range(4):
                    g.indirect_dma_start(got[:, j, :], None, k.rec_d,
                                         bass.IndirectOffsetOnAxis(k.step_tile[:, j:j + 1], 0),
                                         bounds_check=ETP - 1, oob_is_err=True).then_inc(s_got, 16)

            @block.vector
            def _(e):
                done = Chain(e, s_v)
                done(e.memset(ones[:, :], 1.0))
                done(e.memset(k.eps[:, :], LN_EPS))
                e.wait_ge(s_load, 16 * 7)
                done(e.tensor_copy(rec[:, :, 0, :], rows[:, 0, :, :]))
                done(e.tensor_copy(rec[:, :, 2, :], rows[:, 2, :, :]))
                done(e.scalar_tensor_tensor(rec[:, :, 1, :], rec[:, :, 0, :], 8.0, rows[:, 1, :, :],
                                            ALU.mult, ALU.add))
                e.sem_inc(s_rec, 1)
                done(e.scalar_tensor_tensor(k.pair1[:, :, 1], src0[:, :], 8.0, rel0[:, :], ALU.mult, ALU.add))
                done(e.tensor_copy(k.pair1[:, :, 0], dst0[:, :]))
                done(e.tensor_copy(k.pair0[:, :, 0], dst0[:, :]))
                done(e.tensor_copy(k.pair0[:, :, 1], src0[:, :]))
                done(e.tensor_copy(k.ntype[:, :], nt_i[:, :]))
                done(e.tensor_copy(dstf[:, :], dst0[:, :]))
                for b in range(NT - 1):
                    done(e.tensor_scalar(scr[:, 0:ET], dstf[:, 0:ET], float(P * (b + 1)), 0.0, ALU.is_lt, ALU.add,
                                         accum_out=low[:, b:b + 1]))
                e.sem_inc(s_cnt, 1)
                e.wait_ge(s_tr, 1)
                done(e.tensor_copy(low[:, :], pc[:, 0:NT - 1]))
                e.wait_ge(s_const, 6)
                for b in range(NT - 1):
                    done(e.tensor_scalar(scr[:, 0:ET], edge0[:, :], low[:, b:b + 1], 0.0, ALU.is_le, ALU.add,
                                         accum_out=cnt[:, b:b + 1]))
                done(e.memset(blk[:, :], 0.0))
                for b in range(NT - 1):
                    done(e.tensor_scalar(cnt[:, b:b + 1], cnt[:, b:b + 1], float(b), None, ALU.add))
                    done(e.scalar_tensor_tensor(blk[:, :], sidx[:, :], cnt[:, b:b + 1], blk[:, :],
                                                ALU.is_ge, ALU.add))
                done(e.tensor_copy(k.step_block[:, :], blk[0:1, 0:SP_]))
                done(e.tensor_tensor(sidx[:, SP_:], sidx[:, SP_:], blk[:, SP_:], ALU.subtract))
                done(e.tensor_scalar(sidx[:, SP_:], sidx[:, SP_:], float(ETP - 1), None, ALU.min))
                done(e.tensor_copy(k.step_tile[:, :], sidx[:, SP_:]))
                e.sem_inc(s_step, 1)
                for j in range(4):
                    e.wait_ge(s_tr, 2 + j)
                    cols = slice(P * j, P * j + P)
                    done(e.tensor_copy(k.step_src[:, cols], pt[j][:, 0:P]))
                    done(e.tensor_copy(k.step_rel[:, cols], pt[j][:, P:2 * P]))
                    done(e.scalar_tensor_tensor(k.step_loc[:, cols], blk[:, cols], -float(P), pt[j][:, 2 * P:3 * P],
                                                ALU.mult, ALU.add))
                e.wait_ge(s_gload, 16 * 3)
                done(e.tensor_copy(k.gpair[:, :, 0], gdst[:, :]))
                done(e.tensor_copy(k.gpair[:, :, 1], gsrc[:, :]))
                done(e.tensor_scalar(lo_i[:, :], gdst[:, 0:GT], P - 1, None, ALU.bitwise_and))
                done(e.tensor_copy(k.glo[:, :], lo_i[:, :]))
                done(e.tensor_copy(gd_f[:, :], gdst[:, 0:GT]))
                done(e.tensor_tensor(k.ghi[:, :], gd_f[:, :], k.glo[:, :], ALU.subtract))
                done(e.tensor_scalar(k.ghi[:, :], k.ghi[:, :], 1.0 / P, None, ALU.mult))
                done(e.tensor_copy(gs_f[:, :], gsrc[:, 0:GT]))
                done(e.scalar_tensor_tensor(k.mask_pos[:, :], gd_f[:, :], float(NP), gs_f[:, :], ALU.mult, ALU.add))

            @block.tensor
            def _(pe):
                pe.wait_ge(s_cnt, 1)
                pe.matmul(pc[:, 0:NT - 1], ones[:, :], low[:, :], start=True, stop=True).then_inc(s_tr, 1)
                pe.wait_ge(s_const, 2)
                pe.wait_ge(s_got, 64)
                for j in range(4):
                    for r in range(3):
                        ins = pe.transpose(pt[j][:, r * P:(r + 1) * P], got[:, j, r * P:(r + 1) * P], k.ident[:, :])
                    ins.then_inc(s_tr, 1)


def ln_stats(k, x):
    nc = k.nc
    s_v, s_var, s_std = k.sem("ln_dve"), k.sem("ln_var"), k.sem("ln_std")
    with k.block() as block:

        @block.vector
        def _(e):
            with e.Fori(0, NT // GROUP) as i:
                for j in range(GROUP):
                    e.bn_stats(k.stats[:, bass.ds(i * GROUP + j, 1), :].rearrange("p a b -> p (a b)"),
                               x[:, bass.ds(i * GROUP + j, 1), :].rearrange("p a b -> p (a b)")).then_inc(s_v, 1)
            done = Chain(e, s_v, start=NT)
            done.sync()
            me, mo = k.stats[:, :, 1], k.stats[:, :, 4]
            ve, vo = k.stats[:, :, 2], k.stats[:, :, 5]
            done(e.tensor_tensor(k.mean[:, :], me, mo, ALU.add))
            done(e.tensor_scalar(k.mean[:, :], k.mean[:, :], 0.5, None, ALU.mult))
            done(e.tensor_tensor(k.tmp1[:, :], me, mo, ALU.subtract))
            done(e.tensor_tensor(k.tmp1[:, :], k.tmp1[:, :], k.tmp1[:, :], ALU.mult))
            done(e.tensor_tensor(k.tmp2[:, :], ve, vo, ALU.add))
            done(e.tensor_scalar(k.tmp2[:, :], k.tmp2[:, :], 1.0 / D, None, ALU.mult))
            e.scalar_tensor_tensor(k.tmp1[:, :], k.tmp1[:, :], 0.25, k.tmp2[:, :], ALU.mult,
                                   ALU.add).then_inc(s_var, 1)
            e.wait_ge(s_std, 1)
            e.reciprocal(k.rstd[:, :], k.tmp2[:, :]).then_inc(s_var, 1)
            e.wait_ge(s_var, 2)

        @block.scalar
        def _(a):
            a.wait_ge(s_var, 1)
            a.activation(k.tmp2[:, :], k.tmp1[:, :], ACT.Sqrt, bias=k.eps[:, 0:1]).then_inc(s_std, 1)


def tile_of(t3, t, n=1):
    return t3[:, bass.ds(t, n), :].rearrange("p a b -> p (a b)")


def held(j):
    return 0 if j == 0 else 1


def project0(k):
    nc, io = k.nc, k.io
    with ExitStack() as c:
        w = k.sb(c, "wqkv", [P, 2, 3 * D])
        b = k.sb(c, "bqkv", [P, 3 * D])
        xn = k.sb(c, "xn", [P, GROUP, D])
        xt = k.sb(c, "xt", [P, GROUP, 2, P])
        stage = k.sb(c, "stage", [P, GROUP, 3 * D])
        pt = [k.ps(c, f"pt{i}") for i in range(2)]
        pa = [k.ps(c, f"pa{i}") for i in range(2)]
        pb = [k.ps(c, f"pb{i}") for i in range(2)]
        s_w, s_xn, s_tr, s_xt, s_mm, s_out = [k.sem(x) for x in
            ("w_loaded", "xn_ready", "turned", "xt_ready", "qkv_ready", "staged")]
        s_sto = [k.sem(f"stored{j}") for j in range(GROUP)]
        dst = [x.rearrange("(t p) d -> p t d", p=P) for x in (k.q_d, k.k_d, k.v_d)]
        with k.block() as block:

            @block.sync
            def _(sp):
                sp.dma_start(w[:, :, :], io["W_qkv"].rearrange("(c p) n -> p c n", p=P)).then_inc(s_w, 16)
                sp.dma_start(b[:, :], row_bc(io["b_qkv"], P)).then_inc(s_w, 16)
                with sp.Fori(0, NT // GROUP) as i:
                    for j in range(GROUP):
                        sp.wait_ge(s_out, i * GROUP + j + 1)
                        for n in range(3):
                            sp.dma_start(dst[n][:, bass.ds(i * GROUP + j, 1), :].rearrange("p a b -> p (a b)"),
                                         stage[:, j, n * D:(n + 1) * D]).then_inc(s_sto[j], 16)
                for j in range(GROUP):
                    sp.wait_ge(s_sto[j], 48 * (NT // GROUP))

            @block.vector
            def _(e):
                e.wait_ge(s_w, 32)

                def norm(i, j, first):
                    t = i * GROUP + j
                    if not first:
                        e.wait_ge(s_tr, t - GROUP + 1)
                    e.tensor_scalar(xn[:, j, :], tile_of(k.x, t), k.mean[:, bass.ds(t, 1)],
                                    k.rstd[:, bass.ds(t, 1)], ALU.subtract, ALU.mult).then_inc(s_xn, 1)

                def emit(i, j, first):
                    t = i * GROUP + j
                    e.wait_ge(s_mm, t + 1)
                    if not first:
                        e.wait_ge(s_sto[j], i * 48)
                    e.tensor_tensor(stage[:, j, 0:512], pa[j % 2][:, :], b[:, 0:512], ALU.add).then_inc(s_va, 1)
                    e.wait_ge(s_va, t + 1)
                    e.tensor_tensor(stage[:, j, 512:768], pb[j % 2][:, 0:256], b[:, 512:768],
                                    ALU.add).then_inc(s_out, 1)

                s_va = k.sem("first_half")

                def turn(i, first):
                    for j in range(GROUP):
                        norm(i, j, first)
                    for j in range(GROUP):
                        emit(i, j, first)
                turn(0, True)
                with e.Fori(1, NT // GROUP) as i:
                    turn(i, False)

            @block.scalar
            def _(a):
                def turn(i, first):
                    for j in range(GROUP):
                        t = i * GROUP + j
                        a.wait_ge(s_tr, t + 1)
                        if not first:
                            a.wait_ge(s_mm, t - GROUP + 1)
                        a.activation(xt[:, j, :, :], pt[j % 2][:, 0:256].rearrange("p (c n) -> p c n", c=2),
                                     ACT.Copy).then_inc(s_xt, 1)
                turn(0, True)
                with a.Fori(1, NT // GROUP) as i:
                    turn(i, False)

            @block.tensor
            def _(pe):
                pe.wait_ge(s_w, 32)

                def turn(i, first):
                    for j in range(GROUP):
                        t = i * GROUP + j
                        pe.wait_ge(s_xn, t + 1)
                        if not first or j >= 2:
                            pe.wait_ge(s_xt, t - held(j))
                        for c_ in range(2):
                            ins = pe.transpose(pt[j % 2][:, c_ * P:(c_ + 1) * P], xn[:, j, c_ * P:(c_ + 1) * P],
                                               k.ident[:, :])
                        ins.then_inc(s_tr, 1)
                    for j in range(GROUP):
                        t = i * GROUP + j
                        pe.wait_ge(s_xt, t + 1)
                        if not first or j >= 2:
                            pe.wait_ge(s_out, t - held(j))
                        for half, (out, lo, hi) in enumerate(((pa[j % 2][:, :], 0, 512), (pb[j % 2][:, 0:256], 512, 768))):
                            for c_ in range(2):
                                ins = pe.matmul(out, xt[:, j, c_, :], w[:, c_, lo:hi], start=(c_ == 0), stop=(c_ == 1))
                        ins.then_inc(s_mm, 1)
                turn(0, True)
                with pe.Fori(1, NT // GROUP) as i:
                    turn(i, False)


def edge_scores(k, score, pair, q_d, k_d, k_rows, heads):
    nc = k.nc
    with ExitStack() as c:
        qv = k.sb(c, "qv", [P, U, D])
        kv = k.sb(c, "kv", [P, U, D])
        prod = k.sb(c, "prod", [P, 2, D])
        idx = k.sb(c, "idx", [P, U, 2], I32)
        s_first, s_idx, s_prod, s_sum = [k.sem(x) for x in ("score_first", "idx_ready", "product", "summed")]
        s_let = k.sem("fetch_let")
        s_g = [k.sem(f"rows_in{j}") for j in range(U)]
        with k.block() as block:

            @block.gpsimd
            def _(g):
                with g.Fori(0, ET // U) as i:
                    for j in range(U):
                        g.wait_ge(s_idx, i * U + j + 1)
                        g.sem_inc(s_let, 1)
                        g.indirect_dma_start(qv[:, j, :], None, q_d, bass.IndirectOffsetOnAxis(idx[:, j, 0:1], 0),
                                             bounds_check=NP - 1, oob_is_err=True).then_inc(s_g[j], 16)
                        g.indirect_dma_start(kv[:, j, :], None, k_d, bass.IndirectOffsetOnAxis(idx[:, j, 1:2], 0),
                                             bounds_check=k_rows - 1, oob_is_err=True).then_inc(s_g[j], 16)

            @block.vector
            def _(e):
                e.memset(score[:, :, :], 0.0).then_inc(s_first, 1)
                e.tensor_copy(idx[:, :, :], pair[:, 0:U, :]).then_inc(s_first, 1)
                e.wait_ge(s_first, 2)
                e.sem_inc(s_idx, U)
                e.sem_inc(s_sum, 2)
                with e.Fori(0, ET // U) as i:
                    for j in range(U):
                        t = i * U + j
                        e.wait_ge(s_g[j], i * 32 + 32)
                        e.wait_ge(s_sum, t + 1)
                        e.tensor_tensor(prod[:, j % 2, :], qv[:, j, :], kv[:, j, :], ALU.mult).then_inc(s_prod, 1)
                        e.wait_ge(s_prod, t + 1)
                        e.tensor_copy(idx[:, j, :], tile_of(pair, t + U)).then_inc(s_idx, 1)
                        e.tensor_reduce(score[:, bass.ds(t, 1), 0:heads].rearrange("p a h -> p (a h)"),
                                        prod[:, j % 2, :].rearrange("p (h d) -> p h d", h=heads),
                                        AX, ALU.add).then_inc(s_sum, 1)


def softmax_numerators(k, score, ex, scale):
    nc, io = k.nc, k.io
    L = CG * P
    with ExitStack() as c:
        sc = k.sb(c, "sc", [P, CG, P])
        key = k.sb(c, "key", [P, L])
        st = k.sb(c, "st", [P, CG, P])
        st2 = st[:, :, :].rearrange("p g e -> p (g e)")
        new = k.sb(c, "new", [P, L + 1], BF)
        top = k.sb(c, "top", [P, L])
        far = k.sb(c, "far", [P, L], BF)
        ends = k.sb(c, "ends", [P, 4])
        full = k.sb(c, "full", [P, 2])
        e8 = k.sb(c, "e8", [8, CH, 4])
        m8 = k.sb(c, "m8", [8, 2 * CH])
        n8 = k.sb(c, "n8", [8, 2 * CH + 1])
        k8 = k.sb(c, "k8", [8, 2 * CH])
        got = k.sb(c, "got", [P, 4, H * P])
        pt = [k.ps(c, f"pt{i}") for i in range(7)]
        s_key, s_t, s_st, s_v, s_ends, s_e8, s_m8, s_full = [k.sem(x) for x in
            ("keys_in", "turned", "st_ready", "dve", "ends_out", "ends_in", "full_ready", "full_in")]
        s_sc = k.sem("scores_sorted")
        s_dif, s_ex, s_exd, s_got, s_b, s_bk = [k.sem(x) for x in
            ("shifted", "exp_ready", "exp_stored", "got", "step_turned", "step_kept")]
        with k.block() as block:

            @block.sync
            def _(sp):
                for h in range(H):
                    sp.dma_start(key[h * CH:(h + 1) * CH, :].bitcast(I32), io["dst_flat"].rearrange("(a f) -> a f", a=CH)
                                 ).then_inc(s_key, 16)
                sp.wait_ge(s_ends, 1)
                sp.dma_start(k.ends_d, ends[:, :]).then_inc(s_e8, 16)
                sp.wait_ge(s_e8, 16)
                sp.dma_start(e8[:, :, :], k.ends_d.rearrange("(h a) f -> h a f", a=CH)).then_inc(s_e8, 16)
                sp.wait_ge(s_m8, 1)
                sp.dma_start(k.full_d, m8[:, :]).then_inc(s_full, 16)
                sp.wait_ge(s_full, 16)
                sp.dma_start(full[:, :], k.full_d.rearrange("h (a f) -> (h a) f", f=2)).then_inc(s_full, 16)
                sp.wait_ge(s_ex, 1)
                for h in range(H):
                    sp.dma_start(k.ex_d.rearrange("(a g) (h e) -> h a g e", a=CH, h=H)[h],
                                 st[h * CH:(h + 1) * CH, :, :]).then_inc(s_exd, 16)

            @block.tensor
            def _(pe):
                pe.wait_ge(s_sc, 1)
                for g in range(CG):
                    ins = pe.transpose(pt[g // 4][:, (g % 4) * P:(g % 4 + 1) * P],
                                       sc[:, g, :], k.ident[:, :])
                    if g % 4 == 3 or g == CG - 1:
                        ins.then_inc(s_t, 1)
                pe.wait_ge(s_st, 7)
                for n in range(8):
                    j, half = n // 2, n % 2
                    pe.wait_ge(s_got, 64)
                    if n >= 7:
                        pe.wait_ge(s_bk, n - 6)
                    for h in range(4):
                        hh = half * 4 + h
                        ins = pe.transpose(pt[n % 7][:, h * P:(h + 1) * P], got[:, j, hh * P:(hh + 1) * P],
                                           k.ident[:, :])
                    ins.then_inc(s_b, 1)

            @block.gpsimd
            def _(g):
                g.wait_ge(s_exd, 16 * H)
                for j in range(4):
                    g.indirect_dma_start(got[:, j, :], None, k.ex_d,
                                         bass.IndirectOffsetOnAxis(k.step_tile[:, j:j + 1], 0),
                                         bounds_check=ETP - 1, oob_is_err=True).then_inc(s_got, 16)

            @block.scalar
            def _(a):
                for g in range(7):
                    n = min(4, CG - 4 * g)
                    a.wait_ge(s_t, g + 1)
                    a.activation(st[:, 4 * g:4 * g + n, :],
                                 pt[g][:, 0:n * P].rearrange("p (g e) -> p g e", e=P), ACT.Copy).then_inc(s_st, 1)
                a.wait_ge(s_dif, 1)
                a.activation(st2, top[:, :], ACT.Exp, scale=scale).then_inc(s_ex, 1)
                for n in range(8):
                    j, half = n // 2, n % 2
                    a.wait_ge(s_b, n + 1)
                    a.activation(ex[:, j * P:(j + 1) * P, half * 4:half * 4 + 4].rearrange("p s h -> p h s"),
                                 pt[n % 7][:, :].rearrange("p (h s) -> p h s", h=4), ACT.Copy).then_inc(s_bk, 1)

            @block.vector
            def _(e):
                done = Chain(e, s_v)

                def segment_max(vals, restart, out, n):
                    done(e.tensor_tensor_scan(vals[1], restart[:, 0:n], vals[0], -BIG, ALU.add, ALU.max))
                    done(e.tensor_tensor_scan(out[:, ::-1], restart[:, 1:n + 1][:, ::-1], vals[1][:, ::-1], -BIG,
                                              ALU.add, ALU.max))

                done(e.tensor_copy(sc[:, :, :].rearrange("p g (h a) -> p a g h", h=H),
                                   score[:, :, :].rearrange("p (a g) h -> p a g h", g=CG)))
                e.sem_inc(s_sc, 1)
                e.wait_ge(s_key, 16 * H)
                done(e.memset(new[:, :], -BIG))
                keyf = got[:, :, :].rearrange("p a b -> p (a b)")[:, 0:L]
                done(e.tensor_copy(keyf, key[:, :].bitcast(I32)))
                done(e.tensor_tensor(top[:, 1:L], keyf[:, 1:L], keyf[:, 0:L - 1], ALU.not_equal))
                done(e.tensor_scalar(new[:, 1:L], top[:, 1:L], -BIG, None, ALU.mult))
                e.wait_ge(s_st, 7)
                segment_max((st2, key[:, :]), new, top, L)
                done(e.tensor_copy(ends[:, 0:1], top[:, 0:1]))
                done(e.tensor_copy(ends[:, 1:2], top[:, L - 1:L]))
                done(e.tensor_copy(ends[:, 2:3], keyf[:, 0:1]))
                done(e.tensor_copy(ends[:, 3:4], keyf[:, L - 1:L]))
                e.sem_inc(s_ends, 1)
                done(e.tensor_scalar(far[:, :], keyf, keyf[:, 0:1], -BIG, ALU.not_equal, ALU.mult))
                done(e.tensor_scalar(key[:, :], keyf, keyf[:, L - 1:L], -BIG, ALU.not_equal, ALU.mult))
                e.wait_ge(s_e8, 32)
                done(e.tensor_copy(m8[:, :].rearrange("p (a f) -> p a f", f=2), e8[:, :, 0:2]))
                done(e.tensor_copy(k8[:, :].rearrange("p (a f) -> p a f", f=2), e8[:, :, 2:4]))
                done(e.memset(n8[:, :], -BIG))
                done(e.tensor_tensor(n8[:, 1:2 * CH], k8[:, 1:], k8[:, 0:2 * CH - 1], ALU.not_equal))
                done(e.tensor_scalar(n8[:, 1:2 * CH], n8[:, 1:2 * CH], -BIG, None, ALU.mult))
                segment_max((m8[:, :], k8[:, :]), n8, m8, 2 * CH)
                e.sem_inc(s_m8, 1)
                e.wait_ge(s_full, 32)
                done(e.scalar_tensor_tensor(top[:, :], far[:, :], full[:, 0:1], top[:, :], ALU.add, ALU.max))
                done(e.scalar_tensor_tensor(top[:, :], key[:, :], full[:, 1:2], top[:, :], ALU.add, ALU.max))
                e.tensor_tensor(top[:, :], st2, top[:, :], ALU.subtract).then_inc(s_dif, 1)
                e.wait_ge(s_bk, 8)


def edge_messages(k, ex, acc, v_d, v_idx, v_rows, heads):
    nc = k.nc
    W = D + H
    with ExitStack() as c:
        vv = k.sb(c, "vv", [P, U, D])
        msg = k.sb(c, "msg", [P, 2, D])
        pick = k.sb(c, "pick", [P, 2, P])
        idx = k.sb(c, "idx", [P, U], I32)
        pm = [k.ps(c, f"pm{i}") for i in range(2)]
        s_first, s_idx, s_msg, s_pick, s_mm, s_acc = [k.sem(x) for x in
            ("msg_first", "idx_ready", "msg_ready", "pick_ready", "summed", "added")]
        s_let = k.sem("fetch_let")
        s_g = [k.sem(f"rows_in{j}") for j in range(U)]
        with k.block() as block:

            @block.gpsimd
            def _(g):
                with g.Fori(0, STEPS // U) as i:
                    for j in range(U):
                        g.wait_ge(s_idx, i * U + j + 1)
                        g.sem_inc(s_let, 1)
                        g.indirect_dma_start(vv[:, j, :], None, v_d, bass.IndirectOffsetOnAxis(idx[:, j:j + 1], 0),
                                             bounds_check=v_rows - 1, oob_is_err=True).then_inc(s_g[j], 16)

            @block.vector
            def _(e):
                e.memset(acc[:, :, :], 0.0).then_inc(s_first, 1)
                e.tensor_copy(idx[:, :], v_idx[:, 0:U]).then_inc(s_first, 1)
                e.wait_ge(s_first, 2)
                e.sem_inc(s_idx, U)
                e.sem_inc(s_mm, 2)

                def add(s, j, block_of):
                    e.wait_ge(s_mm, s + 3)
                    e.wait_ge(s_acc, s + 1)
                    to = acc[:, bass.ds(block_of, 1), :].rearrange("p a w -> p (a w)")
                    e.tensor_tensor(to, to, pm[j % 2][:, 0:W], ALU.add).then_inc(s_acc, 1)

                e.sem_inc(s_acc, 1)
                with e.Fori(0, STEPS // U) as i:
                    node = [e.value_load(k.step_block[0:1, bass.ds(i * U + j, 1)], min_val=0, max_val=NT - 1)
                            for j in range(U)]
                    for j in range(U):
                        s = i * U + j
                        e.wait_ge(s_mm, s + 1)
                        e.tensor_scalar(pick[:, j % 2, :], k.iota[:, :], k.step_loc[:, bass.ds(s, 1)], None,
                                        ALU.is_equal).then_inc(s_pick, 1)
                        e.wait_ge(s_g[j], i * 16 + 16)
                        e.tensor_tensor(msg[:, j % 2, :].rearrange("p (h d) -> p h d", h=heads),
                                        vv[:, j, :].rearrange("p (h d) -> p h d", h=heads),
                                        bc(ex[:, bass.ds(s, 1), 0:heads].rearrange("p a h -> p (a h)").unsqueeze(2),
                                           (P, heads, D // heads)), ALU.mult).then_inc(s_msg, 1)
                        e.wait_ge(s_msg, s + 1)
                        e.tensor_copy(idx[:, j:j + 1], v_idx[:, bass.ds(s + U, 1)]).then_inc(s_idx, 1)
                        if j:
                            add(s - 1, j - 1, node[j - 1])
                    add(i * U + U - 1, U - 1, node[U - 1])
                e.wait_ge(s_acc, STEPS + 1)

            @block.tensor
            def _(pe):
                with pe.Fori(0, STEPS // U) as i:
                    for j in range(U):
                        s = i * U + j
                        pe.wait_ge(s_pick, s + 1)
                        pe.wait_ge(s_msg, s + 1)
                        if j >= 2:
                            pe.wait_ge(s_acc, s)
                        else:
                            pe.wait_ge(s_acc, i * U + 1)
                        pe.matmul(pm[j % 2][:, 0:D], pick[:, j % 2, :], msg[:, j % 2, :], start=True, stop=True)
                        pe.matmul(pm[j % 2][:, D:W], pick[:, j % 2, :],
                                  ex[:, bass.ds(s, 1), :].rearrange("p a h -> p (a h)"), start=True, stop=True
                                  ).then_inc(s_mm, 1)


def reciprocal_sums(k, e, s_v, acc, rden):
    done = Chain(e, s_v)
    done(e.tensor_scalar(rden[:, :, :], acc[:, :, D:], 1e-30, None, ALU.max))
    done(e.reciprocal(rden[:, :, :], rden[:, :, :]))


def finish0(k, acc):
    nc, io = k.nc, k.io
    with ExitStack() as c:
        w = k.sb(c, "wout", [P, 2, D])
        b = k.sb(c, "bout", [P, D])
        rden = k.sb(c, "rden", [P, NT, H])
        hn = k.sb(c, "hn", [P, GROUP, D])
        xn = k.sb(c, "xn", [P, GROUP, D])
        xt = k.sb(c, "xt", [P, GROUP, 2, P])
        pt = [k.ps(c, f"pt{i}") for i in range(2)]
        py = [k.ps(c, f"py{i}") for i in range(2)]
        s_w, s_v, s_a, s_b, s_hn, s_tr, s_xt, s_mm, s_y, s_x = [k.sem(x) for x in
            ("w_loaded", "dve", "normed", "scaled", "h_ready", "turned", "xt_ready", "product", "biased", "x_ready")]
        with k.block() as block:

            @block.sync
            def _(sp):
                sp.dma_start(w[:, :, :], io["W_out"].rearrange("(c p) n -> p c n", p=P)).then_inc(s_w, 16)
                sp.dma_start(b[:, :], row_bc(io["b_out"], P)).then_inc(s_w, 16)

            @block.vector
            def _(e):
                e.wait_ge(s_w, 32)
                reciprocal_sums(k, e, s_v, acc, rden)

                def turn(i, first):
                    for j in range(GROUP):
                        t = i * GROUP + j
                        if not first:
                            e.wait_ge(s_tr, t - GROUP + 1)
                        e.tensor_scalar(xn[:, j, :], tile_of(k.x, t), k.mean[:, bass.ds(t, 1)],
                                        k.rstd[:, bass.ds(t, 1)], ALU.subtract, ALU.mult).then_inc(s_a, 1)
                        e.tensor_tensor(hn[:, j, :].rearrange("p (d h) -> p h d", h=H),
                                        tile_of(acc, t)[:, 0:D].rearrange("p (h d) -> p h d", h=H),
                                        bc(tile_of(rden, t).unsqueeze(2), (P, H, D // H)), ALU.mult).then_inc(s_b, 1)
                        e.wait_ge(s_a, t + 1)
                        e.wait_ge(s_b, t + 1)
                        e.tensor_tensor(hn[:, j, :], hn[:, j, :], xn[:, j, :], ALU.add).then_inc(s_hn, 1)
                    for j in range(GROUP):
                        t = i * GROUP + j
                        e.wait_ge(s_mm, t + 1)
                        e.tensor_tensor(xn[:, j, :], py[j % 2][:, 0:D], b[:, :], ALU.add).then_inc(s_y, 1)
                        e.wait_ge(s_y, t + 1)
                        e.tensor_tensor(tile_of(k.x, t), tile_of(k.x, t), xn[:, j, :], ALU.add).then_inc(s_x, 1)
                turn(0, True)
                with e.Fori(1, NT // GROUP) as i:
                    e.wait_ge(s_x, i * GROUP)
                    turn(i, False)
                e.wait_ge(s_x, NT)

            @block.scalar
            def _(a):
                def turn(i, first):
                    for j in range(GROUP):
                        t = i * GROUP + j
                        a.wait_ge(s_tr, t + 1)
                        if not first:
                            a.wait_ge(s_mm, t - GROUP + 1)
                        a.activation(xt[:, j, :, :], pt[j % 2][:, 0:256].rearrange("p (c n) -> p c n", c=2),
                                     ACT.Copy).then_inc(s_xt, 1)
                turn(0, True)
                with a.Fori(1, NT // GROUP) as i:
                    turn(i, False)

            @block.tensor
            def _(pe):
                pe.wait_ge(s_w, 32)

                def turn(i, first):
                    for j in range(GROUP):
                        t = i * GROUP + j
                        pe.wait_ge(s_hn, t + 1)
                        if not first or j >= 2:
                            pe.wait_ge(s_xt, t - held(j))
                        for h in range(2):
                            ins = pe.transpose(pt[j % 2][:, h * P:(h + 1) * P], hn[:, j, h * P:(h + 1) * P],
                                               k.ident[:, :])
                        ins.then_inc(s_tr, 1)
                    for j in range(GROUP):
                        t = i * GROUP + j
                        pe.wait_ge(s_xt, t + 1)
                        if not first or j >= 2:
                            pe.wait_ge(s_y, t - held(j))
                        for h in range(2):
                            ins = pe.matmul(py[j % 2][:, 0:D], xt[:, j, h, :], w[:, h, :], start=(h == 0), stop=(h == 1))
                        ins.then_inc(s_mm, 1)
                turn(0, True)
                with pe.Fori(1, NT // GROUP) as i:
                    turn(i, False)


def normalize(k, x, out):
    nc = k.nc
    s_v = k.sem("normed")
    with k.block() as block:

        @block.vector
        def _(e):
            with e.Fori(0, NT // GROUP) as i:
                for j in range(GROUP):
                    t = i * GROUP + j
                    e.tensor_scalar(tile_of(out, t), tile_of(x, t), k.mean[:, bass.ds(t, 1)],
                                    k.rstd[:, bass.ds(t, 1)], ALU.subtract, ALU.mult).then_inc(s_v, 1)
            e.wait_ge(s_v, NT)


def columns(k, x, xnt, router, w_router, R, affine):
    nc, io = k.nc, k.io
    with ExitStack() as c:
        wr = k.sb(c, "wr", [P, 2, R])
        gb = k.sb(c, "gb", [P, 2, 2])
        xn = k.sb(c, "xn", [P, GROUP, D])
        xt = k.sb(c, "xt", [P, GROUP, 2, P])
        pt = [k.ps(c, f"pt{i}") for i in range(2)]
        pr = [k.ps(c, f"pr{i}") for i in range(2)]
        s_w, s_xn, s_tr, s_xt, s_mm, s_r, s_cp = [k.sem(x) for x in
            ("w_loaded", "xn_ready", "turned", "xt_ready", "routed", "router_kept", "xt_kept")]
        n_w = 1 + 2 * bool(affine)
        with k.block() as block:

            @block.sync
            def _(sp):
                sp.dma_start(wr[:, :, :], io[w_router].rearrange("(c p) n -> p c n", p=P)).then_inc(s_w, 16)
                if affine:
                    for n, name in enumerate(affine):
                        sp.dma_start(gb[:, n, :], io[name].rearrange("p c -> p c")).then_inc(s_w, 16)

            @block.vector
            def _(e):
                def turn(i, first):
                    for j in range(GROUP):
                        t = i * GROUP + j
                        if not first:
                            e.wait_ge(s_tr, t - GROUP + 1)
                        e.tensor_scalar(xn[:, j, :], tile_of(x, t), k.mean[:, bass.ds(t, 1)],
                                        k.rstd[:, bass.ds(t, 1)], ALU.subtract, ALU.mult).then_inc(s_xn, 1)
                    for j in range(GROUP):
                        t = i * GROUP + j
                        e.wait_ge(s_mm, t + 1)
                        e.tensor_copy(tile_of(router, t), pr[j % 2][:, 0:R]).then_inc(s_r, 1)
                turn(0, True)
                with e.Fori(1, NT // GROUP) as i:
                    turn(i, False)
                e.wait_ge(s_r, NT)

            @block.scalar
            def _(a):
                a.wait_ge(s_w, 16 * n_w)

                def turn(i, first):
                    for j in range(GROUP):
                        t = i * GROUP + j
                        a.wait_ge(s_tr, t + 1)
                        if not first:
                            a.wait_ge(s_mm, t - GROUP + 1)
                        for h in range(2):
                            src = pt[j % 2][:, h * P:(h + 1) * P]
                            for n, to in enumerate((xt[:, j, h, :], xnt[:, h, bass.ds(t * P, P)])):
                                if affine:
                                    ins = a.activation(to, src, ACT.Identity, bias=gb[:, 1, h:h + 1],
                                                       scale=gb[:, 0, h:h + 1])
                                else:
                                    ins = a.activation(to, src, ACT.Copy)
                        ins.then_inc(s_xt, 1)
                turn(0, True)
                with a.Fori(1, NT // GROUP) as i:
                    turn(i, False)

            @block.tensor
            def _(pe):
                pe.wait_ge(s_w, 16 * n_w)

                def turn(i, first):
                    for j in range(GROUP):
                        t = i * GROUP + j
                        pe.wait_ge(s_xn, t + 1)
                        if not first or j >= 2:
                            pe.wait_ge(s_xt, t - held(j))
                        for h in range(2):
                            ins = pe.transpose(pt[j % 2][:, h * P:(h + 1) * P], xn[:, j, h * P:(h + 1) * P],
                                               k.ident[:, :])
                        ins.then_inc(s_tr, 1)
                    for j in range(GROUP):
                        t = i * GROUP + j
                        pe.wait_ge(s_xt, t + 1)
                        if not first or j >= 2:
                            pe.wait_ge(s_r, t - held(j))
                        for h in range(2):
                            ins = pe.matmul(pr[j % 2][:, 0:R], xt[:, j, h, :], wr[:, h, :], start=(h == 0),
                                            stop=(h == 1))
                        ins.then_inc(s_mm, 1)
                turn(0, True)
                with pe.Fori(1, NT // GROUP) as i:
                    turn(i, False)


def top2_gates(k, score, gate, E, b_router=None):
    nc, io = k.nc, k.io
    with ExitStack() as c:
        b = k.sb(c, "b", [P, E])
        work = k.sb(c, "work", [P, NT, E])
        cand = k.sb(c, "cand", [P, NT, E])
        one = [k.sb(c, f"one{i}", [P, NT, E]) for i in range(2)]
        m = [k.sb(c, f"m{i}", [P, NT]) for i in range(2)]
        pick = k.sb(c, "pick", [P, NT])
        ww = [k.sb(c, f"ww{i}", [P, NT]) for i in range(2)]
        s_b, s_v, s_d, s_e = [k.sem(x) for x in ("b_loaded", "dve", "gap_ready", "exp_ready")]
        wide = lambda a: bc(a[:, :].unsqueeze(2), (P, NT, E))
        iota = bc(k.iota[:, 0:E].unsqueeze(1), (P, NT, E))
        with k.block() as block:

            if b_router:
                @block.sync
                def _(sp):
                    sp.dma_start(b[:, :], row_bc(io[b_router], P)).then_inc(s_b, 16)

            @block.vector
            def _(e):
                done = Chain(e, s_v)
                if b_router:
                    e.wait_ge(s_b, 16)
                    done(e.tensor_tensor(score[:, :, :], score[:, :, :], bc(b[:, :].unsqueeze(1), (P, NT, E)), ALU.add))
                done(e.tensor_copy(work[:, :, :], score[:, :, :]))
                for n in range(2):
                    done(e.tensor_reduce(m[n][:, :], work[:, :, :], AX, ALU.max))
                    done(e.tensor_tensor(cand[:, :, :], work[:, :, :], wide(m[n]), ALU.is_lt))
                    done(e.scalar_tensor_tensor(cand[:, :, :], cand[:, :, :], 99.0, iota, ALU.mult, ALU.add))
                    done(e.tensor_reduce(pick[:, :], cand[:, :, :], AX, ALU.min))
                    done(e.tensor_tensor(one[n][:, :, :], cand[:, :, :], wide(pick), ALU.is_equal))
                    if n == 0:
                        done(e.scalar_tensor_tensor(work[:, :, :], one[0][:, :, :], -BIG, work[:, :, :],
                                                    ALU.mult, ALU.add))
                done(e.tensor_tensor(m[1][:, :], m[1][:, :], m[0][:, :], ALU.subtract))
                e.sem_inc(s_d, 1)
                e.wait_ge(s_e, 1)
                done(e.tensor_scalar(ww[0][:, :], ww[1][:, :], 1.0, None, ALU.add))
                done(e.reciprocal(ww[0][:, :], ww[0][:, :]))
                done(e.tensor_tensor(ww[1][:, :], ww[1][:, :], ww[0][:, :], ALU.mult))
                done(e.tensor_tensor(one[0][:, :, :], one[0][:, :, :], wide(ww[0]), ALU.mult))
                done(e.tensor_tensor(one[1][:, :, :], one[1][:, :, :], wide(ww[1]), ALU.mult))
                done(e.tensor_tensor(gate[:, :, :], one[0][:, :, :], one[1][:, :, :], ALU.add))

            @block.scalar
            def _(a):
                a.wait_ge(s_d, 1)
                a.activation(ww[1][:, :], m[1][:, :], ACT.Exp).then_inc(s_e, 1)


def mark_mask(k, block, c, s_cleared, s_neg):
    idx = k.sb(c, "idx", [P, 2], I32)
    zero1 = k.sb(c, "zero1", [P, 1], BF)
    s_i, s_mark, s_let, s_z = [k.sem(x) for x in ("pos_ready", "marked", "scatter_let", "zero_ready")]

    @block.gpsimd
    def _(g):
        g.memset(zero1[:, :], 0.0).then_inc(s_z, 1)
        g.wait_ge(s_z, 1)
        g.wait_ge(s_cleared, 16 * NT)

        def scatter(b):
            g.sem_inc(s_let, 1)
            g.indirect_dma_start(k.mask_d, bass.IndirectOffsetOnAxis(idx[:, b:b + 1], 0), zero1[:, :], None,
                                 bounds_check=NP * NP - 1, oob_is_err=True).then_inc(s_mark, 16)
        for b in range(2):
            g.tensor_copy(idx[:, b:b + 1], k.mask_pos[:, b:b + 1]).then_inc(s_i, 1)
        g.wait_ge(s_i, 2)
        scatter(0)
        with g.Fori(0, GT // 2 - 1) as i:
            for b in range(2):
                g.wait_ge(s_mark, i * 32 + 16 * b + 16)
                scatter(1 - b)
                g.tensor_copy(idx[:, b:b + 1], k.mask_pos[:, bass.ds(i * 2 + b + 2, 1)]).then_inc(s_i, 1)
                g.wait_ge(s_i, i * 2 + b + 3)
        g.wait_ge(s_mark, 16 * (GT - 1))
        scatter(1)
        g.wait_ge(s_mark, 16 * GT)


def experts(k, xnt, gate, E, names, mask=False):
    nc, io = k.nc, k.io
    F = 512
    FC = F // P
    W1, b1, W2, b2 = names
    with ExitStack() as c:
        w1 = k.sb(c, "w1", [P, E, 2, F])
        w2 = k.sb(c, "w2", [P, E, FC, D])
        b1s = k.sb(c, "b1s", [P, E, FC])
        b2s = k.sb(c, "b2s", [P, E, D])
        ht = k.sb(c, "ht", [P, 2, FC, P])
        y = k.sb(c, "y", [P, 2, D])
        ph = [k.ps(c, f"ph{i}") for i in range(2)]
        py = [k.ps(c, f"py{i}") for i in range(2)]
        s_w, s_h, s_g, s_y, s_b, s_x = [k.sem(x) for x in
            ("w_loaded", "hidden", "gelu_ready", "product", "biased", "x_ready")]
        s_neg, s_cleared = k.sem("neg_ready"), k.sem("mask_cleared")
        neg = k.sb(c, "neg", [P, NP // 4], BF)
        with k.block() as block:
            if mask:
                mark_mask(k, block, c, s_cleared, s_neg)

            @block.sync
            def _(sp):
                sp.dma_start(w1[:, :, :, :], io[W1].rearrange("e (c p) f -> p e c f", p=P)).then_inc(s_w, 16)
                sp.dma_start(w2[:, :, :, :], io[W2].rearrange("e (c p) d -> p e c d", p=P)).then_inc(s_w, 16)
                sp.dma_start(b1s[:, :, :], io[b1]).then_inc(s_w, 16)
                sp.dma_start(b2s[:, :, :].rearrange("p e d -> p (e d)"),
                             row_bc(io[b2].rearrange("e d -> (e d)"), P)).then_inc(s_w, 16)
                if mask:
                    sp.wait_ge(s_neg, 1)
                    clear = k.mask_d.rearrange("(t p n f) o -> t p n (f o)", p=P, n=4, f=NP // 4)
                    for t in range(NT):
                        sp.dma_start(clear[t], bc(neg[:, :].unsqueeze(1), (P, 4, NP // 4))).then_inc(s_cleared, 16)

            @block.tensor
            def _(pe):
                pe.wait_ge(s_w, 64)

                def hidden(i, n, first):
                    if not first:
                        pe.wait_ge(s_g, i * E + n - 1)
                    for f in range(FC):
                        for h in range(2):
                            ins = pe.matmul(ph[n % 2][:, f * P:(f + 1) * P], w1[:, n, h, f * P:(f + 1) * P],
                                            xnt[:, h, bass.ds(i * P, P)], start=(h == 0), stop=(h == 1))
                    ins.then_inc(s_h, 1)

                def output(i, n, first):
                    pe.wait_ge(s_g, i * E + n + 1)
                    if not first:
                        pe.wait_ge(s_b, i * E + n - 1)
                    for f in range(FC):
                        ins = pe.matmul(py[n % 2][:, 0:D], ht[:, n % 2, f, :], w2[:, n, f, :], start=(f == 0),
                                        stop=(f == FC - 1))
                    ins.then_inc(s_y, 1)

                def turn(i, first):
                    hidden(i, 0, first)
                    for n in range(E):
                        if n + 1 < E:
                            hidden(i, n + 1, first and n + 1 < 2)
                        output(i, n, first and n < 2)
                turn(0, True)
                with pe.Fori(1, NT) as i:
                    turn(i, False)

            @block.scalar
            def _(a):
                a.wait_ge(s_w, 64)

                def turn(i, first):
                    for n in range(E):
                        a.wait_ge(s_h, i * E + n + 1)
                        if not (first and n < 2):
                            a.wait_ge(s_y, i * E + n - 1)
                        for f in range(FC):
                            ins = a.activation(ht[:, n % 2, f, :], ph[n % 2][:, f * P:(f + 1) * P], ACT.Gelu,
                                               bias=b1s[:, n, f:f + 1])
                        ins.then_inc(s_g, 1)
                turn(0, True)
                with a.Fori(1, NT) as i:
                    turn(i, False)

            @block.vector
            def _(e):
                e.memset(neg[:, :], -BIG).then_inc(s_neg, 1)
                e.wait_ge(s_w, 64)
                e.sem_inc(s_x, 1)
                with e.Fori(0, NT) as i:
                    for n in range(E):
                        e.wait_ge(s_y, i * E + n + 1)
                        e.tensor_tensor(y[:, n % 2, :], py[n % 2][:, 0:D], b2s[:, n, :], ALU.add).then_inc(s_b, 1)
                        e.wait_ge(s_b, i * E + n + 1)
                        e.wait_ge(s_x, i * E + n + 1)
                        e.scalar_tensor_tensor(tile_of(k.x, i), y[:, n % 2, :],
                                               tile_of(gate, i)[:, n:n + 1], tile_of(k.x, i),
                                               ALU.mult, ALU.add).then_inc(s_x, 1)
                e.wait_ge(s_x, NT * E + 1)


def project1(k):
    nc, io = k.nc, k.io
    T, R = 4, 8
    with ExitStack() as c:
        w = k.sb(c, "wkvq", [P, 3, T, 2, D])
        rel = k.sb(c, "rel", [P, 2, 2, R, P])
        pri = k.sb(c, "pri", [P, R, 4])
        xn = k.sb(c, "xn", [P, GROUP, D])
        xm = k.sb(c, "xm", [P, 2, T, 2, P])
        kvt = k.sb(c, "kvt", [P, 2, 4, P])
        stage = k.sb(c, "stage", [P, 2, 2, R, D])
        stq = k.sb(c, "stq", [P, 2, D])
        pt = [k.ps(c, f"pt{i}") for i in range(2)]
        pk = k.ps(c, "pk")
        pq = k.ps(c, "pq")
        po = [k.ps(c, f"po{i}") for i in range(4)]
        s_w, s_z, s_blk, s_v, s_xn, s_tr, s_xm, s_kv, s_q, s_kvt, s_qs = [k.sem(x) for x in
            ("w_loaded", "rel_zero", "rel_loaded", "dve", "xn_ready", "turned", "masked", "kv_ready", "q_ready",
             "kvt_ready", "q_kept")]
        s_o, s_od, s_oa, s_rel = [k.sem(x) for x in ("out_ready", "out_kept_dve", "out_kept_act", "rel_scaled")]
        s_st = [k.sem(f"stored{j}") for j in range(2)]
        q_to = k.q_d.rearrange("(t p) d -> p t d", p=P)
        kv_to = [x.rearrange("(t p r) d -> p t (r d)", p=P, r=R) for x in (k.kr_d, k.vr_d)]
        with k.block() as block:

            @block.sync
            def _(sp):
                for n, name in enumerate(("k_linears", "v_linears", "q_linears")):
                    sp.dma_start(w[:, n, :, :, :], io[name].rearrange("t (c p) o -> p t c o", p=P)).then_inc(s_w, 16)
                sp.dma_start(pri[:, :, :].rearrange("p r h -> p (r h)"), row_bc(io["pri"], P)).then_inc(s_w, 16)
                sp.wait_ge(s_z, 1)
                for n, name in enumerate(("att_t", "msg")):
                    for h in range(4):
                        o = (h % 2) * 64
                        sp.dma_start(rel[o:o + 64, n, h // 2, :, o:o + 64], io[name][h]).then_inc(s_blk, 16)

                def turn(i, first):
                    for j in range(GROUP):
                        t = i * GROUP + j
                        sp.wait_ge(s_od, (t + 1) * 4)
                        sp.wait_ge(s_oa, (t + 1) * 4)
                        sp.wait_ge(s_qs, t + 1)
                        for n in range(2):
                            sp.dma_start(kv_to[n][:, bass.ds(t, 1), :].rearrange("p a f -> p (a f)"),
                                         stage[:, j % 2, n, :, :].rearrange("p r d -> p (r d)")
                                         ).then_inc(s_st[j % 2], 16)
                        sp.dma_start(q_to[:, bass.ds(t, 1), :].rearrange("p a f -> p (a f)"),
                                     stq[:, j % 2, :]).then_inc(s_st[j % 2], 16)
                with sp.Fori(0, NT // GROUP) as i:
                    turn(i, False)
                sp.wait_ge(s_st[0], 48 * 3 * (NT // GROUP))
                sp.wait_ge(s_st[1], 48 * 2 * (NT // GROUP))

            def free_stage(eng, i, j, first):
                uses = (3, 2)[j % 2]
                if not first or j >= 2:
                    eng.wait_ge(s_st[j % 2], i * (48 * uses) + 48 * (j // 2))

            def mask(e, j, t, n):
                return e.scalar_tensor_tensor(
                    xm[:, j % 2, n, :, :], bc(k.ntype[:, bass.ds(t * P, P)].unsqueeze(1), (P, 2, P)), float(n),
                    pt[j % 2][:, 0:2 * P].rearrange("p (c n) -> p c n", c=2), ALU.is_equal, ALU.mult)

            def stage_half(j, m):
                return stage[:, j % 2, m // 4, (m % 2) * 4:(m % 2) * 4 + 4, (m // 2 % 2) * P:(m // 2 % 2 + 1) * P]

            @block.vector
            def _(e):
                done = Chain(e, s_v)
                e.memset(rel[:, :, :, :, :], 0.0).then_inc(s_z, 1)
                e.wait_ge(s_w, 64)
                e.wait_ge(s_blk, 16 * 8)
                done(e.tensor_scalar(pri[:, :, :], pri[:, :, :], 0.125, None, ALU.mult))
                for h in range(4):
                    o = (h % 2) * 64
                    blk = rel[o:o + 64, 0, h // 2, :, o:o + 64]
                    done(e.tensor_tensor(blk, blk, bc(pri[o:o + 64, :, h:h + 1], (64, R, 64)), ALU.mult))
                e.sem_inc(s_rel, 1)

                def norm(i, j, first):
                    t = i * GROUP + j
                    if not first:
                        e.wait_ge(s_tr, t - GROUP + 1)
                    e.tensor_scalar(xn[:, j, :], tile_of(k.x, t), k.mean[:, bass.ds(t, 1)],
                                    k.rstd[:, bass.ds(t, 1)], ALU.subtract, ALU.mult).then_inc(s_xn, 1)

                def turn(i, first):
                    for j in range(GROUP):
                        norm(i, j, first)
                    for j in range(GROUP):
                        t = i * GROUP + j
                        e.wait_ge(s_tr, t + 1)
                        if not first or j >= 2:
                            e.wait_ge(s_q, t - held(j))
                        for n in range(T):
                            ins = mask(e, j, t, n)
                            ins.then_inc(s_xm, 1)
                        free_stage(e, i, j, first)
                        for m in range(0, 8, 2):
                            e.wait_ge(s_o, t * 8 + m + 1)
                            e.tensor_copy(stage_half(j, m), po[m % 4][:, :].rearrange("p (r d) -> p r d", r=4)
                                          ).then_inc(s_od, 1)
                turn(0, True)
                with e.Fori(1, NT // GROUP) as i:
                    turn(i, False)

            @block.scalar
            def _(a):
                def turn(i, first):
                    for j in range(GROUP):
                        t = i * GROUP + j
                        free_stage(a, i, j, first)
                        a.wait_ge(s_kv, t + 1)
                        a.activation(kvt[:, j % 2, :, :], pk[:, :].rearrange("p (m n) -> p m n", m=4),
                                     ACT.Copy).then_inc(s_kvt, 1)
                        a.wait_ge(s_q, t + 1)
                        a.activation(stq[:, j % 2, :], pq[:, 0:D], ACT.Copy).then_inc(s_qs, 1)
                        for m in range(1, 8, 2):
                            a.wait_ge(s_o, t * 8 + m + 1)
                            a.activation(stage_half(j, m), po[m % 4][:, :].rearrange("p (r d) -> p r d", r=4),
                                         ACT.Copy).then_inc(s_oa, 1)
                turn(0, True)
                with a.Fori(1, NT // GROUP) as i:
                    turn(i, False)

            @block.tensor
            def _(pe):
                pe.wait_ge(s_w, 64)
                pe.wait_ge(s_rel, 1)

                def turned(i, j, first):
                    t = i * GROUP + j
                    pe.wait_ge(s_xn, t + 1)
                    if not first or j >= 2:
                        pe.wait_ge(s_xm, (t - held(j)) * T)
                    for h in range(2):
                        ins = pe.transpose(pt[j % 2][:, h * P:(h + 1) * P], xn[:, j, h * P:(h + 1) * P],
                                           k.ident[:, :])
                    ins.then_inc(s_tr, 1)

                def turn(i, first):
                    turned(i, 0, first)
                    for j in range(GROUP):
                        t = i * GROUP + j
                        if j + 1 < GROUP:
                            turned(i, j + 1, first)
                        pe.wait_ge(s_xm, (t + 1) * T)
                        if not first or j:
                            pe.wait_ge(s_kvt, t)
                            pe.wait_ge(s_qs, t)
                        for m in range(4):
                            for n in range(T):
                                for h in range(2):
                                    ins = pe.matmul(pk[:, m * P:(m + 1) * P],
                                                    w[:, m // 2, n, h, (m % 2) * P:(m % 2 + 1) * P],
                                                    xm[:, j % 2, n, h, :], start=(n == 0 and h == 0),
                                                    stop=(n == T - 1 and h == 1))
                        ins.then_inc(s_kv, 1)
                        for n in range(T):
                            for h in range(2):
                                ins = pe.matmul(pq[:, 0:D], xm[:, j % 2, n, h, :], w[:, 2, n, h, :],
                                                start=(n == 0 and h == 0), stop=(n == T - 1 and h == 1))
                        ins.then_inc(s_q, 1)
                        pe.wait_ge(s_kvt, t + 1)
                        for m in range(8):
                            mine = s_od if m % 2 == 0 else s_oa
                            if m >= 4:
                                pe.wait_ge(mine, t * 4 + m // 2 - 1)
                            elif not first or j:
                                pe.wait_ge(mine, t * 4 - 1 + m // 2)
                            pe.matmul(po[m % 4][:, :], kvt[:, j % 2, m // 2, :],
                                      rel[:, m // 4, m // 2 % 2, (m % 2) * 4:(m % 2) * 4 + 4, :]
                                      .rearrange("p r d -> p (r d)"), start=True, stop=True).then_inc(s_o, 1)
                turn(0, True)
                with pe.Fori(1, NT // GROUP) as i:
                    turn(i, False)


def finish1(k, acc):
    nc, io = k.nc, k.io
    T = 4
    with ExitStack() as c:
        w = k.sb(c, "wa", [P, T, 2, D])
        skip = k.sb(c, "skip", [P, T])
        rden = k.sb(c, "rden", [P, NT, H])
        hn = k.sb(c, "hn", [P, GROUP, D])
        xm = k.sb(c, "xm", [P, GROUP, T, 2, P])
        pt = [k.ps(c, f"pt{i}") for i in range(2)]
        py = [k.ps(c, f"py{i}") for i in range(2)]
        s_w, s_v, s_sig, s_wr, s_hn, s_tr, s_xm, s_mm, s_x = [k.sem(x) for x in
            ("w_loaded", "dve", "sigmoid", "w_ready", "h_ready", "turned", "masked", "product", "x_ready")]
        with k.block() as block:

            @block.sync
            def _(sp):
                sp.dma_start(w[:, :, :, :], io["a_linears"].rearrange("t (c p) o -> p t c o", p=P)).then_inc(s_w, 16)
                sp.dma_start(skip[:, :], row_bc(io["skip"], P)).then_inc(s_w, 16)

            @block.scalar
            def _(a):
                a.wait_ge(s_w, 32)
                a.activation(skip[:, :], skip[:, :], ACT.Sigmoid).then_inc(s_sig, 1)

            @block.vector
            def _(e):
                done = Chain(e, s_v)
                reciprocal_sums(k, e, k.sem("sums"), acc, rden)
                e.wait_ge(s_w, 32)
                e.wait_ge(s_sig, 1)
                for n in range(T):
                    done(e.tensor_scalar(w[:, n, :, :], w[:, n, :, :], skip[:, n:n + 1], None, ALU.mult))
                e.sem_inc(s_wr, 1)

                def turn(i, first):
                    for j in range(GROUP):
                        t = i * GROUP + j
                        if not first:
                            e.wait_ge(s_tr, t - GROUP + 1)
                        e.tensor_tensor(hn[:, j, :].rearrange("p (h d) -> p h d", h=4),
                                        tile_of(acc, t)[:, 0:D].rearrange("p (h d) -> p h d", h=4),
                                        bc(tile_of(rden, t)[:, 0:4].unsqueeze(2), (P, 4, D // 4)),
                                        ALU.mult).then_inc(s_hn, 1)
                    for j in range(GROUP):
                        t = i * GROUP + j
                        e.wait_ge(s_tr, t + 1)
                        if not first:
                            e.wait_ge(s_mm, t - GROUP + 1)
                        for n in range(T):
                            e.scalar_tensor_tensor(
                                xm[:, j, n, :, :], bc(k.ntype[:, bass.ds(t * P, P)].unsqueeze(1), (P, 2, P)), float(n),
                                pt[j % 2][:, 0:2 * P].rearrange("p (c n) -> p c n", c=2), ALU.is_equal,
                                ALU.mult).then_inc(s_xm, 1)
                    for j in range(GROUP):
                        t = i * GROUP + j
                        e.wait_ge(s_mm, t + 1)
                        e.tensor_tensor(tile_of(k.x, t), tile_of(k.x, t), py[j % 2][:, 0:D], ALU.add).then_inc(s_x, 1)
                turn(0, True)
                with e.Fori(1, NT // GROUP) as i:
                    turn(i, False)
                e.wait_ge(s_x, NT)

            @block.tensor
            def _(pe):
                pe.wait_ge(s_wr, 1)

                def turn(i, first):
                    for j in range(GROUP):
                        t = i * GROUP + j
                        pe.wait_ge(s_hn, t + 1)
                        if not first or j >= 2:
                            pe.wait_ge(s_xm, (t - held(j)) * T)
                        for h in range(2):
                            ins = pe.transpose(pt[j % 2][:, h * P:(h + 1) * P], hn[:, j, h * P:(h + 1) * P],
                                               k.ident[:, :])
                        ins.then_inc(s_tr, 1)
                    for j in range(GROUP):
                        t = i * GROUP + j
                        pe.wait_ge(s_xm, (t + 1) * T)
                        if not first or j >= 2:
                            pe.wait_ge(s_x, t - held(j))
                        for n in range(T):
                            for h in range(2):
                                ins = pe.matmul(py[j % 2][:, 0:D], xm[:, j, n, h, :], w[:, n, h, :],
                                                start=(n == 0 and h == 0), stop=(n == T - 1 and h == 1))
                        ins.then_inc(s_mm, 1)
                turn(0, True)
                with pe.Fori(1, NT // GROUP) as i:
                    turn(i, False)


def leaky(e, done, out, x):
    done(e.scalar_tensor_tensor(out, x, 0.2, x, ALU.mult, ALU.max))


def gate_tables(k, h16, gs, gd):
    nc, io = k.nc, k.io
    with ExitStack() as c:
        att = k.sb(c, "att", [P, 2, 16])
        prod = k.sb(c, "prod", [P, 2, NT, 16])
        arow = k.sb(c, "arow", [4, NP])
        every = k.sb(c, "every", [P, 4, NP])
        mask = k.sb(c, "mask", [P, GROUP, NP], BF)
        scr = k.sb(c, "scr", [P, NP], BF)
        mx = k.sb(c, "mx", [P, 2, GROUP * 4])
        most = k.sb(c, "most", [P, NT * 4])
        pt = [k.ps(c, f"pt{i}") for i in range(7)]
        s_w, s_v, s_t, s_tk, s_row, s_all, s_mx, s_cp = [k.sem(x) for x in
            ("w_loaded", "dve", "turned", "row_kept", "row_ready", "row_spread", "maxima", "maxima_kept")]
        s_let = k.sem("mask_let")
        s_as, s_gd, s_out = k.sem("asrc_ready"), k.sem("gd_ready"), k.sem("stored")
        s_m = [k.sem(f"mask_in{j}") for j in range(GROUP)]
        rows = k.mask_d.rearrange("(t p f) o -> p t (f o)", p=P, f=NP)
        with k.block() as block:

            @block.sync
            def _(sp):
                sp.dma_start(att[:, 0, :], row_bc(io["att_src"], P)).then_inc(s_w, 16)
                sp.dma_start(att[:, 1, :], row_bc(io["att_dst"], P)).then_inc(s_w, 16)
                for j in range(GROUP):
                    sp.dma_start(mask[:, j, :], rows[:, j, :]).then_inc(s_m[j], 16)
                sp.wait_ge(s_tk, 7)
                sp.dma_start(k.asrc_d, arow[:, :]).then_inc(s_row, 16)
                sp.wait_ge(s_row, 16)
                sp.dma_start(every[:, :, :].rearrange("p h n -> p (h n)"),
                             row_bc(k.asrc_d.rearrange("h n -> (h n)"), P)).then_inc(s_all, 16)
                sp.dma_start(k.gs_d.rearrange("(t p) f -> p t f", p=P), gs[:, :, :]).then_inc(s_out, 16)
                with sp.Fori(1, NT // GROUP) as i:
                    for j in range(GROUP):
                        sp.wait_ge(s_mx, (i * GROUP + j - GROUP) * 4 + 4)
                        sp.dma_start(mask[:, j, :], rows[:, bass.ds(i * GROUP + j, 1), :].rearrange("p a f -> p (a f)")
                                     ).then_inc(s_m[j], 16)
                sp.wait_ge(s_gd, 1)
                sp.dma_start(k.gd_d.rearrange("(t p) f -> p t f", p=P), gd[:, :, :]).then_inc(s_out, 16)
                sp.wait_ge(s_out, 32)

            @block.tensor
            def _(pe):
                pe.wait_ge(s_as, 1)
                for t in range(NT):
                    ins = pe.transpose(pt[t // 4][0:4, (t % 4) * P:(t % 4 + 1) * P], gs[:, t, 0:4], k.ident[:, :])
                    if t % 4 == 3 or t == NT - 1:
                        ins.then_inc(s_t, 1)

            @block.scalar
            def _(a):
                for g in range(7):
                    n = min(4, NT - 4 * g)
                    a.wait_ge(s_t, g + 1)
                    a.activation(arow[:, g * 4 * P:(g * 4 + n) * P], pt[g][0:4, 0:n * P], ACT.Copy).then_inc(s_tk, 1)

            @block.vector
            def _(e):
                done = Chain(e, s_v)
                e.wait_ge(s_w, 32)
                for n, out in enumerate((gs, gd)):
                    done(e.tensor_tensor(prod[:, n, :, :], h16[:, :, :], bc(att[:, n:n + 1, :], (P, NT, 16)), ALU.mult))
                    done(e.tensor_reduce(out[:, :, 0:4], prod[:, n, :, :].rearrange("p t (h x) -> p t h x", x=4),
                                         AX, ALU.add))
                done(e.tensor_copy(gs[:, :, 4:20], h16[:, :, :]))
                e.sem_inc(s_as, 1)
                e.wait_ge(s_all, 16)
                with e.Fori(0, NT // GROUP) as i:
                    for j in range(GROUP):
                        e.wait_ge(s_m[j], i * 16 + 16)
                        e.sem_inc(s_let, 1)
                        for h in range(4):
                            e.tensor_tensor_reduce(scr[:, :], mask[:, j, :], every[:, h, :], 1.0, -BIG, ALU.add,
                                                   ALU.max, mx[:, 0, j * 4 + h:j * 4 + h + 1]).then_inc(s_mx, 1)
                            e.wait_ge(s_mx, (i * GROUP + j) * 4 + h + 1)
                            e.sem_inc(s_let, 1)
                    e.wait_ge(s_mx, (i + 1) * (GROUP * 4))
                    e.tensor_copy(most[:, bass.ds(i * (GROUP * 4), GROUP * 4)], mx[:, 0, :]).then_inc(s_cp, 1)
                    e.wait_ge(s_cp, i + 1)
                m3 = most[:, :].rearrange("p (t h) -> p t h", h=4)
                done(e.tensor_tensor(m3, m3, gs[:, :, 0:4], ALU.max))
                done(e.tensor_tensor(m3, m3, gd[:, :, 0:4], ALU.add))
                leaky(e, done, gd[:, :, 4:8], m3)
                e.sem_inc(s_gd, 1)


def gate_sums(k, gs, gd, score):
    nc, io = k.nc, k.io
    B = 8
    C = NT * 20
    with ExitStack() as c:
        idx = k.sb(c, "idx", [P, 2, B, 2], I32)
        rs = k.sb(c, "rs", [P, 2, B, 20])
        rd = k.sb(c, "rd", [P, 2, B, 8])
        ev = k.sb(c, "ev", [P, 2, B, 4])
        f = k.sb(c, "f", [P, 2, B, 20])
        lo = k.sb(c, "lo", [P, 2, B, P])
        hi = k.sb(c, "hi", [P, 2, B, NT])
        wide = k.sb(c, "wide", [P, 2, C])
        zero = k.sb(c, "zero", [P, C])
        agg = k.sb(c, "agg", [P, NT, 20])
        own = k.sb(c, "own", [P, NT, 20])
        nrm = k.sb(c, "nrm", [P, NT, 16])
        sq = k.sb(c, "sq", [P, NT, 16])
        m1 = k.sb(c, "m1", [P, NT])
        v1 = k.sb(c, "v1", [P, NT])
        par = k.sb(c, "par", [P, 3, 16])
        pa = k.ps(c, "pa")
        s_w, s_first, s_idx, s_v, s_e, s_ex, s_hot, s_mm, s_own, s_ownx, s_var, s_std = [k.sem(x) for x in
            ("w_loaded", "first", "idx_ready", "dve", "gap_ready", "exp_ready", "wide_ready", "summed", "loop_gap",
             "loop_exp", "var_ready", "std_ready")]
        s_let = k.sem("fetch_let")
        s_g = [k.sem(f"rows_in{b}") for b in range(2)]
        with k.block() as block:

            @block.sync
            def _(sp):
                for n, name in enumerate(("b_gat", "ln_gamma", "ln_beta")):
                    sp.dma_start(par[:, n, :], row_bc(io[name], P)).then_inc(s_w, 16)

            @block.gpsimd
            def _(g):
                with g.Fori(0, GT // (2 * B)) as i:
                    for b in range(2):
                        g.wait_ge(s_idx, i * 2 + b + 1)
                        g.sem_inc(s_let, 1)
                        for j in range(B):
                            g.indirect_dma_start(rd[:, b, j, :], None, k.gd_d,
                                                 bass.IndirectOffsetOnAxis(idx[:, b, j, 0:1], 0),
                                                 bounds_check=NP - 1, oob_is_err=True).then_inc(s_g[b], 16)
                            g.indirect_dma_start(rs[:, b, j, :], None, k.gs_d,
                                                 bass.IndirectOffsetOnAxis(idx[:, b, j, 1:2], 0),
                                                 bounds_check=NP - 1, oob_is_err=True).then_inc(s_g[b], 16)

            @block.scalar
            def _(a):
                a.wait_ge(s_own, 1)
                a.activation(own[:, :, 0:4], own[:, :, 0:4], ACT.Exp).then_inc(s_ownx, 1)
                with a.Fori(0, GT // (2 * B)) as i:
                    for b in range(2):
                        a.wait_ge(s_e, i * 2 + b + 1)
                        a.activation(f[:, b, :, 0:4], ev[:, b, :, :], ACT.Exp).then_inc(s_ex, 1)
                a.wait_ge(s_var, 1)
                a.activation(v1[:, :], v1[:, :], ACT.Sqrt, bias=k.eps[:, 0:1]).then_inc(s_std, 1)

            @block.tensor
            def _(pe):
                pe.wait_ge(s_first, 1)
                pe.matmul(pa[:, 0:C], zero[:, 0:P], zero[:, :], start=True, stop=False, skip_group_check=True)
                with pe.Fori(0, GT // (2 * B)) as i:
                    for b in range(2):
                        for j in range(B):
                            pe.wait_ge(s_hot, (i * 2 + b) * B + j + 1)
                            pe.matmul(pa[:, 0:C], lo[:, b, j, :], wide[:, j % 2, :], start=False, stop=False,
                                      skip_group_check=True).then_inc(s_mm, 1)
                pe.matmul(pa[:, 0:C], zero[:, 0:P], zero[:, :], start=False, stop=True,
                          skip_group_check=True).then_inc(s_mm, 1)

            @block.vector
            def _(e):
                e.memset(zero[:, :], 0.0).then_inc(s_v, 1)
                e.tensor_copy(idx[:, :, :, :], k.gpair[:, 0:2 * B, :].rearrange("p (a b) f -> p a b f", a=2)
                              ).then_inc(s_v, 1)
                done = Chain(e, s_v, start=2)
                done.sync()
                e.sem_inc(s_first, 1)
                e.sem_inc(s_idx, 2)
                e.sem_inc(s_mm, 2 * B)
                done(e.tensor_tensor(own[:, :, 0:4], gs[:, :, 0:4], gd[:, :, 0:4], ALU.add))
                leaky(e, done, own[:, :, 0:4], own[:, :, 0:4])
                done(e.tensor_tensor(own[:, :, 0:4], own[:, :, 0:4], gd[:, :, 4:8], ALU.subtract))
                e.sem_inc(s_own, 1)
                e.wait_ge(s_ownx, 1)
                for x in range(4):
                    done(e.tensor_tensor(own[:, :, 4 + x:20:4], gs[:, :, 4 + x:20:4], own[:, :, 0:4], ALU.mult))
                base = done.n
                with e.Fori(0, GT // (2 * B)) as i:
                    per = 2 * 9
                    loop = Chain(e, s_v, base=i * per + base)
                    for b in range(2):
                        T0 = (i * 2 + b) * B
                        e.wait_ge(s_g[b], i * (32 * B) + 32 * B)
                        loop(e.tensor_tensor(ev[:, b, :, :], rs[:, b, :, 0:4], rd[:, b, :, 0:4], ALU.add))
                        leaky(e, loop, ev[:, b, :, :], ev[:, b, :, :])
                        loop(e.tensor_tensor(ev[:, b, :, :], ev[:, b, :, :], rd[:, b, :, 4:8], ALU.subtract))
                        e.sem_inc(s_e, 1)
                        e.wait_ge(s_mm, T0 + B)
                        loop(e.tensor_tensor(lo[:, b, :, :], bc(k.iota[:, :].unsqueeze(1), (P, B, P)),
                                             bc(k.glo[:, bass.ds(T0, B)].unsqueeze(2), (P, B, P)), ALU.is_equal))
                        loop(e.tensor_tensor(hi[:, b, :, :], bc(k.iota[:, 0:NT].unsqueeze(1), (P, B, NT)),
                                             bc(k.ghi[:, bass.ds(T0, B)].unsqueeze(2), (P, B, NT)), ALU.is_equal))
                        e.wait_ge(s_ex, i * 2 + b + 1)
                        for x in range(4):
                            loop(e.tensor_tensor(f[:, b, :, 4 + x:20:4], rs[:, b, :, 4 + x:20:4], f[:, b, :, 0:4],
                                                 ALU.mult))
                        e.tensor_copy(idx[:, b, :, :], k.gpair[:, bass.ds(T0 + 2 * B, B), :]).then_inc(s_idx, 1)
                        for j in range(B):
                            e.wait_ge(s_mm, T0 + j + 2 * B - 1)
                            e.tensor_tensor(wide[:, j % 2, :].rearrange("p (n f) -> p n f", n=NT),
                                            bc(hi[:, b, j, :].unsqueeze(2), (P, NT, 20)),
                                            bc(f[:, b, j:j + 1, :], (P, NT, 20)), ALU.mult).then_inc(s_hot, 1)
                    assert loop.n == per, loop.n
                done = Chain(e, s_v, start=base + per * (GT // (2 * B)))
                e.wait_ge(s_mm, GT + 2 * B + 1)
                done(e.tensor_tensor(agg[:, :, :], pa[:, 0:C].rearrange("p (n f) -> p n f", n=NT), own[:, :, :], ALU.add))
                done(e.tensor_scalar(own[:, :, 0:4], agg[:, :, 0:4], 1e-16, None, ALU.add))
                done(e.reciprocal(own[:, :, 0:4], own[:, :, 0:4]))
                for x in range(4):
                    done(e.tensor_tensor(nrm[:, :, x::4], agg[:, :, 4 + x:20:4], own[:, :, 0:4], ALU.mult))
                e.wait_ge(s_w, 48)
                done(e.tensor_tensor(nrm[:, :, :], nrm[:, :, :], bc(par[:, 0:1, :], (P, NT, 16)), ALU.add))
                done(e.tensor_reduce(m1[:, :], nrm[:, :, :], AX, ALU.add))
                done(e.tensor_scalar(m1[:, :], m1[:, :], 1.0 / 16, None, ALU.mult))
                done(e.tensor_tensor(nrm[:, :, :], nrm[:, :, :], bc(m1[:, :].unsqueeze(2), (P, NT, 16)), ALU.subtract))
                done(e.tensor_tensor(sq[:, :, :], nrm[:, :, :], nrm[:, :, :], ALU.mult))
                done(e.tensor_reduce(v1[:, :], sq[:, :, :], AX, ALU.add))
                done(e.tensor_scalar(v1[:, :], v1[:, :], 1.0 / 16, None, ALU.mult))
                e.sem_inc(s_var, 1)
                e.wait_ge(s_std, 1)
                done(e.reciprocal(v1[:, :], v1[:, :]))
                done(e.tensor_tensor(nrm[:, :, :], nrm[:, :, :], bc(v1[:, :].unsqueeze(2), (P, NT, 16)), ALU.mult))
                done(e.tensor_tensor(nrm[:, :, :], nrm[:, :, :], bc(par[:, 1:2, :], (P, NT, 16)), ALU.mult))
                done(e.tensor_tensor(nrm[:, :, :], nrm[:, :, :], bc(par[:, 2:3, :], (P, NT, 16)), ALU.add))
                done(e.tensor_reduce(score[:, :, :], nrm[:, :, :].rearrange("p t (h x) -> p t x h", x=4), AX, ALU.add))
                done(e.tensor_scalar(score[:, :, :], score[:, :, :], 0.25, None, ALU.mult))


def store_x(k, to):
    nc = k.nc
    s_o = k.sem("stored")
    with k.block() as block:

        @block.sync
        def _(sp):
            sp.dma_start(to[0:(NT - 1) * P, :].rearrange("(t p) d -> p t d", p=P), k.x[:, 0:NT - 1, :]).then_inc(s_o, 16)
            sp.dma_start(to[(NT - 1) * P:, :], k.x[0:to.shape[0] - (NT - 1) * P, NT - 1, :]).then_inc(s_o, 16)
            sp.wait_ge(s_o, 32)


def build(nc, io, out, dumps=None, upto=99):
    with ExitStack() as ctx:
        k = Kernel(nc, io, out, ctx, dumps)
        setup(k)
        structure(k)
        for layer in range(2):
            ln_stats(k, k.x)
            with ExitStack() as c:
                if layer == 0:
                    project0(k)
                    args = (k.pair0, k.q_d, k.k_d, NP, 8)
                    vargs = (k.v_d, k.step_src, NP, 8)
                    scale = 32 ** -0.5
                else:
                    project1(k)
                    args = (k.pair1, k.q_d, k.kr_d, NP * 8, 4)
                    vargs = (k.vr_d, k.step_rel, NP * 8, 4)
                    scale = 1.0
                ex = k.sb(c, "ex", [P, SP_, H])
                with ExitStack() as c2:
                    score = k.sb(c2, "score", [P, ETP, H])
                    edge_scores(k, score, *args)
                    softmax_numerators(k, score, ex, scale)
                acc = k.sb(c, "acc", [P, NT, D + H])
                edge_messages(k, ex, acc, *vargs)
                (finish0, finish1)[layer](k, acc)
            if dumps:
                store_x(k, dumps[2 * layer])
            if upto <= 2 * layer + 1:
                return
            with ExitStack() as c:
                E, R = ((8, 8), (4, 16))[layer]
                gate = k.sb(c, "gate", [P, NT, E])
                ln_stats(k, k.x)
                xnt = k.sb(c, "xnt", [P, 2, NP])
                with ExitStack() as c2:
                    router = k.sb(c2, "router", [P, NT, R])
                    if layer == 0:
                        with ExitStack() as c3:
                            xn = k.sb(c3, "xn", [P, NT, D])
                            normalize(k, k.x, xn)
                            ln_stats(k, xn)
                            columns(k, xn, xnt, router, "Wr", R, ("gamma", "beta"))
                        top2_gates(k, router, gate, E, "br")
                    else:
                        columns(k, k.x, xnt, router, "W_gat", R, None)
                        gs = k.sb(c2, "gs", [P, NT, 20])
                        gd = k.sb(c2, "gd", [P, NT, 8])
                        score = k.sb(c2, "score", [P, NT, E])
                        gate_tables(k, router, gs, gd)
                        gate_sums(k, gs, gd, score)
                        top2_gates(k, score, gate, E)
                experts(k, xnt, gate, E, [f"{x}_{layer}" for x in ("W1", "b1", "W2", "b2")],
                        mask=layer == 0)
            if dumps:
                store_x(k, dumps[2 * layer + 1])
            if upto <= 2 * layer + 2:
                return
        store_x(k, out)


def kernel(x, src, dst, edge_type_8, node_type_4, L0_gnn_W_qkv, L0_gnn_b_qkv, L0_gnn_W_out, L0_gnn_b_out,
           L0_ffn_gamma, L0_ffn_beta, L0_ffn_Wr, L0_ffn_br, L0_ffn_W1, L0_ffn_b1, L0_ffn_W2, L0_ffn_b2,
           L1_gnn_k_linears, L1_gnn_q_linears, L1_gnn_v_linears, L1_gnn_a_linears, L1_gnn_relation_att,
           L1_gnn_relation_msg, L1_gnn_relation_pri, L1_gnn_skip, L1_ffn_W_gat, L1_ffn_att_src, L1_ffn_att_dst,
           L1_ffn_b_gat, L1_ffn_ln_gamma, L1_ffn_ln_beta, L1_ffn_W1, L1_ffn_b1, L1_ffn_W2, L1_ffn_b2,
           L1_ffn_edge_index, _dump=False, _upto=99):
    import concourse.bacc as bacc
    from concourse.bass_utils import run_bass_kernel_spmd

    a = np.ascontiguousarray

    def pad(v, n, fill):
        v = np.asarray(v)
        out = np.full((n,) + v.shape[1:], fill, v.dtype)
        out[:len(v)] = v
        return out

    last = NP - 1
    s, d, r = pad(src, EP, last), pad(dst, EP, last), pad(edge_type_8, EP, 0)
    g = np.asarray(L1_ffn_edge_index)

    def tiles(v, extra=0):
        v = np.asarray(v).reshape(-1, P).T
        return a(np.concatenate([v, np.zeros((P, extra), v.dtype)], 1)) if extra else a(v)

    def by_chunk(v):
        v = np.asarray(v)
        v = v.reshape(v.shape[:-1] + (-1, P))
        return a(np.moveaxis(v, -1, 0))

    data = {
        "x": pad(x, NP, 0), "src_rows": s.reshape(ETP, P), "rel_rows": r.reshape(ETP, P),
        "dst_rows": d.reshape(ETP, P), "src_t": tiles(s), "dst_t": tiles(d), "rel_t": tiles(r), "dst_flat": d,
        "ntype": pad(node_type_4, NP, 0), "gsrc_t": tiles(g[0], 2 * U), "gdst_t": tiles(g[1], 2 * U),
        "W_qkv": L0_gnn_W_qkv, "b_qkv": L0_gnn_b_qkv, "W_out": L0_gnn_W_out, "b_out": L0_gnn_b_out,
        "gamma": by_chunk(L0_ffn_gamma), "beta": by_chunk(L0_ffn_beta), "Wr": L0_ffn_Wr, "br": L0_ffn_br,
        "W1_0": L0_ffn_W1, "b1_0": by_chunk(L0_ffn_b1), "W2_0": L0_ffn_W2, "b2_0": L0_ffn_b2,
        "k_linears": L1_gnn_k_linears, "q_linears": L1_gnn_q_linears, "v_linears": L1_gnn_v_linears,
        "a_linears": L1_gnn_a_linears,
        "att_t": np.transpose(np.asarray(L1_gnn_relation_att), (1, 3, 0, 2)),
        "msg": np.transpose(np.asarray(L1_gnn_relation_msg), (1, 2, 0, 3)),
        "pri": np.asarray(L1_gnn_relation_pri).reshape(-1), "skip": L1_gnn_skip, "W_gat": L1_ffn_W_gat,
        "att_src": np.asarray(L1_ffn_att_src).reshape(-1), "att_dst": np.asarray(L1_ffn_att_dst).reshape(-1),
        "b_gat": L1_ffn_b_gat, "ln_gamma": L1_ffn_ln_gamma, "ln_beta": L1_ffn_ln_beta,
        "W1_1": L1_ffn_W1, "b1_1": by_chunk(L1_ffn_b1), "W2_1": L1_ffn_W2, "b2_1": L1_ffn_b2,
    }
    nc = bacc.Bacc("TRN2", target_bir_lowering=False, num_devices=1)
    arrays, io = {}, {}
    for name, v in data.items():
        v = a(np.asarray(v))
        arrays["in_" + name] = v
        io[name] = nc.dram_tensor("in_" + name, list(v.shape), mybir.dt.from_np(v.dtype), kind="ExternalInput").ap()
    out = nc.dram_tensor("out", [N, D], F32, kind="ExternalOutput").ap()
    if _dump:
        dumps = [nc.dram_tensor(f"dump{i}", [N, D], F32, kind="ExternalOutput").ap() for i in range(4)]
        build(nc, io, out, dumps, _upto)
        return nc, arrays
    build(nc, io, out)
    res = run_bass_kernel_spmd(nc, [arrays], core_ids=[0])
    return res.results[0]["out"]
```

```python
from contextlib import ExitStack, contextmanager

import numpy as np

import concourse.bass as bass
from concourse import mybir

P = 128
N, D = 3125, 256
NT = 25
NP = NT * P
GROUP = 5
E0 = 50000
ET = 392
ETP = 400
EP = ETP * P
CH, CG = 16, 25
STEPS = ET + NT - 1
SP_ = 512
U = 8
Q = 4
LAG = 8
GE = 32768
GT = GE // P
H = 8
BIG = 1.0e30
LN_EPS = 1e-5

ALU = mybir.AluOpType
ACT = mybir.ActivationFunctionType
AX = mybir.AxisListType.X
F32, I32, BF = mybir.dt.float32, mybir.dt.int32, mybir.dt.bfloat16


class Chain:

    def __init__(self, eng, sem, start=0, base=None):
        self.eng, self.sem, self.n, self.base = eng, sem, start, base

    def mark(self, ins):
        ins.then_inc(self.sem, 1)
        self.n += 1

    def sync(self):
        self.eng.wait_ge(self.sem, self.n if self.base is None else self.base + self.n)

    def __call__(self, ins):
        self.mark(ins)
        self.sync()


class Kernel:

    def __init__(self, nc, io, out, ctx, dump):
        self.nc, self.io, self.out, self.ctx, self.dumpto = nc, io, out, ctx, dump
        self.nsem = 0

        self.sems = []

    def sem(self, name):
        self.nsem += 1
        self.sems.append(self.nc.alloc_semaphore(name=f"{name}_{self.nsem}"))
        return self.sems[-1]

    @contextmanager
    def block(self):
        with self.nc.Block() as block:
            yield block
        self.nc.clear_and_free_semaphores(self.sems)
        self.nc.all_engine_barrier()
        self.sems = []

    def sb(self, ctx, name, shape, dt=F32):
        self.nsem += 1
        return ctx.enter_context(self.nc.sbuf_tensor(f"{name}_{self.nsem}", shape, dt))

    def ps(self, ctx, name, shape=(P, 512), dt=F32):
        self.nsem += 1
        return ctx.enter_context(self.nc.psum_tensor(f"{name}_{self.nsem}", list(shape), dt))

    def dram(self, name, shape, dt=F32):
        return self.nc.dram_tensor(name, shape, dt, kind="Internal").ap()


def bc(ap, shape):
    return ap.to_broadcast(list(shape))


def row_bc(ap, parts):
    return ap.partition_broadcast(parts)


def setup(k):
    nc, ctx, io = k.nc, k.ctx, k.io
    k.x = k.sb(ctx, "x", [P, NT, D])
    k.ident = k.sb(ctx, "ident", [P, P])
    k.iota = k.sb(ctx, "iota", [P, P])
    k.step_src = k.sb(ctx, "step_src", [P, SP_], I32)
    k.step_rel = k.sb(ctx, "step_rel", [P, SP_], I32)
    k.step_loc = k.sb(ctx, "step_loc", [P, SP_])
    k.step_tile = k.sb(ctx, "step_tile", [P, 4], I32)
    k.step_block = k.sb(ctx, "step_block", [1, LAG + SP_], I32)
    k.step_etile = k.sb(ctx, "step_etile", [1, LAG + SP_], I32)
    k.pcol = k.sb(ctx, "pcol", [P, 1])
    k.gpair = k.sb(ctx, "gpair", [P, GT + 2 * U, 2], I32)
    k.mask_pos = k.sb(ctx, "mask_pos", [P, GT], I32)
    k.glo = k.sb(ctx, "glo", [P, GT])
    k.ghi = k.sb(ctx, "ghi", [P, GT])
    k.ntype = k.sb(ctx, "ntype", [P, NP])
    k.mean = k.sb(ctx, "mean", [P, NT])
    k.rstd = k.sb(ctx, "rstd", [P, NT])
    k.stats = k.sb(ctx, "stats", [P, NT, 6])
    k.tmp1 = k.sb(ctx, "tmp1", [P, NT])
    k.tmp2 = k.sb(ctx, "tmp2", [P, NT])
    k.eps = k.sb(ctx, "eps", [P, 1])

    k.loc_d = k.dram("loc_d", [SP_, P])
    k.k_d = k.dram("k_d", [NP, D])
    k.v_d = k.dram("v_d", [NP, D])
    k.kr_d = k.dram("kr_d", [NP * 8, D])
    k.vr_d = k.dram("vr_d", [NP * 8, D])
    k.rec_d = k.dram("rec_d", [ETP, 3 * P])
    k.ex_d = k.dram("ex_d", [ETP, H * P])
    k.ends_d = k.dram("ends_d", [P, 4])
    k.full_d = k.dram("full_d", [8, 32])
    k.mask_d = k.dram("mask_d", [NP * NP, 1], BF)
    k.asrc_d = k.dram("asrc_d", [4, NP])
    k.gs_d = k.dram("gs_d", [NP, 20])
    k.gd_d = k.dram("gd_d", [NP, 8])


def structure(k):
    nc, io = k.nc, k.io
    with ExitStack() as c:
        rows = k.sb(c, "rows", [100, 3, 4, P], I32)
        rec = k.sb(c, "rec", [100, 4, 3, P])
        locr = k.sb(c, "locr", [P, 4, P])
        brow = k.sb(c, "brow", [1, SP_])
        dst0 = k.sb(c, "dst0", [P, ETP], I32)
        gsrc = k.sb(c, "gsrc", [P, GT + 2 * U], I32)
        gdst = k.sb(c, "gdst", [P, GT + 2 * U], I32)
        dstf = k.sb(c, "dstf", [P, ETP])
        low = k.sb(c, "low", [P, NT - 1])
        cnt = k.sb(c, "cnt", [P, NT - 1])
        ones = k.sb(c, "ones", [P, P])
        scr = k.sb(c, "scr", [P, ETP])
        edge0 = k.sb(c, "edge0", [P, ET])
        sidx = k.sb(c, "sidx", [P, SP_ + 4])
        blk = k.sb(c, "blk", [P, SP_ + 4])
        got = k.sb(c, "got", [P, 4, 3 * P])
        nt_i = k.sb(c, "nt_i", [P, NP], I32)
        gd_f = k.sb(c, "gd_f", [P, GT])
        gs_f = k.sb(c, "gs_f", [P, GT])
        lo_i = k.sb(c, "lo_i", [P, GT], I32)
        pc = k.ps(c, "pc")
        pt = [k.ps(c, f"pt{i}") for i in range(4)]
        s_load, s_gload, s_const, s_v, s_cnt, s_rec, s_recd = [k.sem(x) for x in
            ("loaded", "gate_loaded", "const_done", "dve", "counts_summed", "rec_ready", "rec_stored")]
        s_step, s_got, s_tr, s_loc, s_locd = [k.sem(x) for x in ("steps_ready", "got", "turned", "loc_ready", "loc_stored")]
        with k.block() as block:

            @block.sync
            def _(sp):
                for j, name in enumerate(("src_rows", "rel_rows", "dst_rows")):
                    sp.dma_start(rows[:, j, :, :], io[name].rearrange("(p c) e -> p c e", c=4)).then_inc(s_load, 16)
                sp.dma_start(dst0[:, :], io["dst_t"]).then_inc(s_load, 16)
                sp.dma_start(nt_i[:, :], row_bc(io["ntype"], P)).then_inc(s_load, 16)
                sp.dma_start(gsrc[:, :], io["gsrc_t"]).then_inc(s_gload, 16)
                sp.dma_start(gdst[:, :], io["gdst_t"]).then_inc(s_gload, 16)
                sp.dma_start(k.x[:, :, :], io["x"].rearrange("(t p) d -> p t d", p=P)).then_inc(s_gload, 16)
                sp.wait_ge(s_rec, 1)
                sp.dma_start(k.rec_d.rearrange("(p c) f -> p c f", c=4),
                             rec[:, :, :, :].rearrange("p c j e -> p c (j e)")).then_inc(s_recd, 16)
                sp.wait_ge(s_loc, 1)
                sp.dma_start(k.loc_d.rearrange("(j p) e -> p j e", p=P), locr[:, :, :]).then_inc(s_locd, 16)
                sp.wait_ge(s_locd, 16)

            @block.gpsimd
            def _(g):
                g.memset(k.ident[:, :], 0.0).then_inc(s_const, 1)
                g.wait_ge(s_const, 1)
                g.affine_select(out=k.ident[:, :], in_=k.ident[:, :], compare_op=ALU.not_equal, fill=1.0,
                                base=0, pattern=[[-1, P]], channel_multiplier=1).then_inc(s_const, 1)
                g.iota(k.iota[:, :], [[1, P]], base=0, channel_multiplier=0,
                       allow_small_or_imprecise_dtypes=True).then_inc(s_const, 1)
                g.iota(k.pcol[:, :], [[1, 1]], base=0, channel_multiplier=1,
                       allow_small_or_imprecise_dtypes=True).then_inc(s_const, 1)
                g.iota(edge0[:, :], [[P, ET]], base=0, channel_multiplier=0,
                       allow_small_or_imprecise_dtypes=True).then_inc(s_const, 1)
                g.iota(sidx[:, 0:SP_], [[1, SP_]], base=0, channel_multiplier=0,
                       allow_small_or_imprecise_dtypes=True).then_inc(s_const, 1)
                g.iota(sidx[:, SP_:], [[P, 4]], base=0, channel_multiplier=1,
                       allow_small_or_imprecise_dtypes=True).then_inc(s_const, 1)
                g.wait_ge(s_step, 1)
                g.wait_ge(s_recd, 16)
                for j in range(4):
                    g.indirect_dma_start(got[:, j, :], None, k.rec_d,
                                         bass.IndirectOffsetOnAxis(k.step_tile[:, j:j + 1], 0),
                                         bounds_check=ETP - 1, oob_is_err=True).then_inc(s_got, 16)

            @block.vector
            def _(e):
                done = Chain(e, s_v)
                done(e.memset(ones[:, :], 1.0))
                done(e.memset(k.eps[:, :], LN_EPS))
                e.wait_ge(s_load, 16 * 5)
                done(e.tensor_copy(rec[:, :, 0, :], rows[:, 0, :, :]))
                done(e.tensor_copy(rec[:, :, 2, :], rows[:, 2, :, :]))
                done(e.scalar_tensor_tensor(rec[:, :, 1, :], rec[:, :, 0, :], 8.0, rows[:, 1, :, :],
                                            ALU.mult, ALU.add))
                e.sem_inc(s_rec, 1)
                done(e.tensor_copy(k.ntype[:, :], nt_i[:, :]))
                done(e.tensor_copy(dstf[:, :], dst0[:, :]))
                for b in range(NT - 1):
                    done(e.tensor_scalar(scr[:, 0:ET], dstf[:, 0:ET], float(P * (b + 1)), 0.0, ALU.is_lt, ALU.add,
                                         accum_out=low[:, b:b + 1]))
                e.sem_inc(s_cnt, 1)
                e.wait_ge(s_tr, 1)
                done(e.tensor_copy(low[:, :], pc[:, 0:NT - 1]))
                e.wait_ge(s_const, 7)
                for b in range(NT - 1):
                    done(e.tensor_scalar(scr[:, 0:ET], edge0[:, :], low[:, b:b + 1], 0.0, ALU.is_le, ALU.add,
                                         accum_out=cnt[:, b:b + 1]))
                done(e.memset(blk[:, :], 0.0))
                for b in range(NT - 1):
                    done(e.tensor_scalar(cnt[:, b:b + 1], cnt[:, b:b + 1], float(b), None, ALU.add))
                    done(e.scalar_tensor_tensor(blk[:, :], sidx[:, :], cnt[:, b:b + 1], blk[:, :],
                                                ALU.is_ge, ALU.add))
                done(e.memset(k.step_block[:, :], 0))
                done(e.memset(k.step_etile[:, :], 0))
                done(e.tensor_copy(k.step_block[:, LAG:], blk[0:1, 0:SP_]))
                done(e.tensor_tensor(brow[:, :], sidx[0:1, 0:SP_], blk[0:1, 0:SP_], ALU.subtract))
                done(e.tensor_copy(k.step_etile[:, LAG:], brow[:, :]))
                done(e.tensor_tensor(sidx[:, SP_:], sidx[:, SP_:], blk[:, SP_:], ALU.subtract))
                done(e.tensor_scalar(sidx[:, SP_:], sidx[:, SP_:], float(ETP - 1), None, ALU.min))
                done(e.tensor_copy(k.step_tile[:, :], sidx[:, SP_:]))
                e.sem_inc(s_step, 1)
                e.wait_ge(s_got, 64)
                for j in range(4):
                    done(e.scalar_tensor_tensor(locr[:, j, :], bc(blk[:, SP_ + j:SP_ + j + 1], (P, P)), -float(P),
                                                got[:, j, 2 * P:3 * P], ALU.mult, ALU.add))
                e.sem_inc(s_loc, 1)
                for j in range(4):
                    e.wait_ge(s_tr, 2 + j)
                    cols = slice(P * j, P * j + P)
                    done(e.tensor_copy(k.step_src[:, cols], pt[j][:, 0:P]))
                    done(e.tensor_copy(k.step_rel[:, cols], pt[j][:, P:2 * P]))
                    done(e.scalar_tensor_tensor(k.step_loc[:, cols], blk[:, cols], -float(P), pt[j][:, 2 * P:3 * P],
                                                ALU.mult, ALU.add))
                e.wait_ge(s_gload, 16 * 3)
                done(e.tensor_copy(k.gpair[:, :, 0], gdst[:, :]))
                done(e.tensor_copy(k.gpair[:, :, 1], gsrc[:, :]))
                done(e.tensor_scalar(lo_i[:, :], gdst[:, 0:GT], P - 1, None, ALU.bitwise_and))
                done(e.tensor_copy(k.glo[:, :], lo_i[:, :]))
                done(e.tensor_copy(gd_f[:, :], gdst[:, 0:GT]))
                done(e.tensor_tensor(k.ghi[:, :], gd_f[:, :], k.glo[:, :], ALU.subtract))
                done(e.tensor_scalar(k.ghi[:, :], k.ghi[:, :], 1.0 / P, None, ALU.mult))
                done(e.tensor_copy(gs_f[:, :], gsrc[:, 0:GT]))
                done(e.scalar_tensor_tensor(k.mask_pos[:, :], gd_f[:, :], float(NP), gs_f[:, :], ALU.mult, ALU.add))

            @block.tensor
            def _(pe):
                pe.wait_ge(s_cnt, 1)
                pe.matmul(pc[:, 0:NT - 1], ones[:, :], low[:, :], start=True, stop=True).then_inc(s_tr, 1)
                pe.wait_ge(s_const, 2)
                pe.wait_ge(s_got, 64)
                for j in range(4):
                    for r in range(3):
                        ins = pe.transpose(pt[j][:, r * P:(r + 1) * P], got[:, j, r * P:(r + 1) * P], k.ident[:, :])
                    ins.then_inc(s_tr, 1)


def ln_stats(k, x):
    nc = k.nc
    s_v, s_var, s_std = k.sem("ln_dve"), k.sem("ln_var"), k.sem("ln_std")
    with k.block() as block:

        @block.vector
        def _(e):
            with e.Fori(0, NT // GROUP) as i:
                for j in range(GROUP):
                    e.bn_stats(k.stats[:, bass.ds(i * GROUP + j, 1), :].rearrange("p a b -> p (a b)"),
                               x[:, bass.ds(i * GROUP + j, 1), :].rearrange("p a b -> p (a b)")).then_inc(s_v, 1)
            done = Chain(e, s_v, start=NT)
            done.sync()
            me, mo = k.stats[:, :, 1], k.stats[:, :, 4]
            ve, vo = k.stats[:, :, 2], k.stats[:, :, 5]
            done(e.tensor_tensor(k.mean[:, :], me, mo, ALU.add))
            done(e.tensor_scalar(k.mean[:, :], k.mean[:, :], 0.5, None, ALU.mult))
            done(e.tensor_tensor(k.tmp1[:, :], me, mo, ALU.subtract))
            done(e.tensor_tensor(k.tmp1[:, :], k.tmp1[:, :], k.tmp1[:, :], ALU.mult))
            done(e.tensor_tensor(k.tmp2[:, :], ve, vo, ALU.add))
            done(e.tensor_scalar(k.tmp2[:, :], k.tmp2[:, :], 1.0 / D, None, ALU.mult))
            e.scalar_tensor_tensor(k.tmp1[:, :], k.tmp1[:, :], 0.25, k.tmp2[:, :], ALU.mult,
                                   ALU.add).then_inc(s_var, 1)
            e.wait_ge(s_std, 1)
            e.reciprocal(k.rstd[:, :], k.tmp2[:, :]).then_inc(s_var, 1)
            e.wait_ge(s_var, 2)

        @block.scalar
        def _(a):
            a.wait_ge(s_var, 1)
            a.activation(k.tmp2[:, :], k.tmp1[:, :], ACT.Sqrt, bias=k.eps[:, 0:1]).then_inc(s_std, 1)


def tile_of(t3, t, n=1):
    return t3[:, bass.ds(t, n), :].rearrange("p a b -> p (a b)")


def held(j):
    return 0 if j == 0 else 1


def project0(k, qres):
    nc, io = k.nc, k.io
    with ExitStack() as c:
        w = k.sb(c, "wqkv", [P, 2, 3 * D])
        b = k.sb(c, "bqkv", [P, 3 * D])
        xn = k.sb(c, "xn", [P, GROUP, D])
        xt = k.sb(c, "xt", [P, GROUP, 2, P])
        stage = k.sb(c, "stage", [P, GROUP, 2 * D])
        pt = [k.ps(c, f"pt{i}") for i in range(2)]
        pa = [k.ps(c, f"pa{i}") for i in range(2)]
        pb = [k.ps(c, f"pb{i}") for i in range(2)]
        s_w, s_xn, s_tr, s_xt, s_mm, s_out = [k.sem(x) for x in
            ("w_loaded", "xn_ready", "turned", "xt_ready", "qkv_ready", "staged")]
        s_sto = [k.sem(f"stored{j}") for j in range(GROUP)]
        dst = [x.rearrange("(t p) d -> p t d", p=P) for x in (k.k_d, k.v_d)]
        with k.block() as block:

            @block.sync
            def _(sp):
                sp.dma_start(w[:, :, :], io["W_qkv"].rearrange("(c p) n -> p c n", p=P)).then_inc(s_w, 16)
                sp.dma_start(b[:, :], row_bc(io["b_qkv"], P)).then_inc(s_w, 16)
                with sp.Fori(0, NT // GROUP) as i:
                    for j in range(GROUP):
                        sp.wait_ge(s_out, i * GROUP + j + 1)
                        for n in range(2):
                            sp.dma_start(dst[n][:, bass.ds(i * GROUP + j, 1), :].rearrange("p a b -> p (a b)"),
                                         stage[:, j, n * D:(n + 1) * D]).then_inc(s_sto[j], 16)
                for j in range(GROUP):
                    sp.wait_ge(s_sto[j], 32 * (NT // GROUP))

            @block.vector
            def _(e):
                e.wait_ge(s_w, 32)

                def norm(i, j, first):
                    t = i * GROUP + j
                    if not first:
                        e.wait_ge(s_tr, t - GROUP + 1)
                    e.tensor_scalar(xn[:, j, :], tile_of(k.x, t), k.mean[:, bass.ds(t, 1)],
                                    k.rstd[:, bass.ds(t, 1)], ALU.subtract, ALU.mult).then_inc(s_xn, 1)

                def emit(i, j, first):
                    t = i * GROUP + j
                    e.wait_ge(s_mm, t + 1)
                    if not first:
                        e.wait_ge(s_sto[j], i * 32)
                    e.tensor_tensor(tile_of(qres, t), pb[j % 2][:, 0:256], b[:, 0:256], ALU.add).then_inc(s_va, 1)
                    e.wait_ge(s_va, t + 1)
                    e.tensor_tensor(stage[:, j, :], pa[j % 2][:, :], b[:, 256:768], ALU.add).then_inc(s_out, 1)

                s_va = k.sem("first_half")

                def turn(i, first):
                    for j in range(GROUP):
                        norm(i, j, first)
                    for j in range(GROUP):
                        emit(i, j, first)
                turn(0, True)
                with e.Fori(1, NT // GROUP) as i:
                    turn(i, False)

            @block.scalar
            def _(a):
                def turn(i, first):
                    for j in range(GROUP):
                        t = i * GROUP + j
                        a.wait_ge(s_tr, t + 1)
                        if not first:
                            a.wait_ge(s_mm, t - GROUP + 1)
                        a.activation(xt[:, j, :, :], pt[j % 2][:, 0:256].rearrange("p (c n) -> p c n", c=2),
                                     ACT.Copy).then_inc(s_xt, 1)
                turn(0, True)
                with a.Fori(1, NT // GROUP) as i:
                    turn(i, False)

            @block.tensor
            def _(pe):
                pe.wait_ge(s_w, 32)

                def turn(i, first):
                    for j in range(GROUP):
                        t = i * GROUP + j
                        pe.wait_ge(s_xn, t + 1)
                        if not first or j >= 2:
                            pe.wait_ge(s_xt, t - held(j))
                        for c_ in range(2):
                            ins = pe.transpose(pt[j % 2][:, c_ * P:(c_ + 1) * P], xn[:, j, c_ * P:(c_ + 1) * P],
                                               k.ident[:, :])
                        ins.then_inc(s_tr, 1)
                    for j in range(GROUP):
                        t = i * GROUP + j
                        pe.wait_ge(s_xt, t + 1)
                        if not first or j >= 2:
                            pe.wait_ge(s_out, t - held(j))
                        for half, (out, lo, hi) in enumerate(((pb[j % 2][:, 0:256], 0, 256), (pa[j % 2][:, :], 256, 768))):
                            for c_ in range(2):
                                ins = pe.matmul(out, xt[:, j, c_, :], w[:, c_, lo:hi], start=(c_ == 0), stop=(c_ == 1))
                        ins.then_inc(s_mm, 1)
                turn(0, True)
                with pe.Fori(1, NT // GROUP) as i:
                    turn(i, False)


def registers(k, eng, table, first, name):
    k.nsem += 1
    regs = [eng.alloc_register(f"{name}{k.nsem}_{j}") for j in range(U)]

    def load(at):
        k.nc.reg_load(regs, table[0:1, bass.ds(at, U)])
        return [eng.snap(r, min_val=0, max_val=first) for r in regs]
    return load


def edge_scores(k, score, qres, idx_all, k_d, k_rows, heads):
    nc = k.nc
    TURNS = STEPS // U
    with ExitStack() as c:
        loc = k.sb(c, "loc", [P, 2, Q * P])
        hot = k.sb(c, "hot", [P, 2, Q * P])
        kv = k.sb(c, "kv", [P, 2, Q, D])
        prod = k.sb(c, "prod", [P, 2, Q * D])
        part = k.sb(c, "part", [P, 2, Q, heads])
        idx = k.sb(c, "idx", [P, 2, Q], I32)
        pq = [k.ps(c, f"pq{i}", [P, Q * D]) for i in range(2)]
        s_first, s_idx, s_hot, s_q, s_prod, s_part, s_add, s_let = [k.sem(x) for x in
            ("score_first", "idx_ready", "hot_ready", "q_picked", "product", "part_ready", "added", "fetch_let")]
        s_g = [k.sem(f"rows_in{b}") for b in range(2)]
        s_l = [k.sem(f"loc_in{b}") for b in range(2)]
        with k.block() as block:

            @block.gpsimd
            def _(g):
                with g.Fori(0, TURNS) as i:
                    for b in range(2):
                        g.wait_ge(s_idx, i * 2 + b + 1)
                        g.sem_inc(s_let, 1)
                        for r in range(Q):
                            g.indirect_dma_start(kv[:, b, r, :], None, k_d,
                                                 bass.IndirectOffsetOnAxis(idx[:, b, r:r + 1], 0),
                                                 bounds_check=k_rows - 1, oob_is_err=True).then_inc(s_g[b], 16)

            @block.sync
            def _(sp):
                def fetch(n, b):
                    sp.dma_start(loc[:, b, :], row_bc(k.loc_d.rearrange("s e -> (s e)")[bass.ds(n * (Q * P), Q * P)], P)
                                 ).then_inc(s_l[b], 16)
                for b in range(2):
                    fetch(b, b)
                with sp.Fori(1, TURNS) as i:
                    for b in range(2):
                        sp.wait_ge(s_hot, i * 2 + b - 1)
                        fetch(i * 2 + b, b)

            @block.tensor
            def _(pe):
                load = registers(k, pe, k.step_block, NT - 1, "node")
                with pe.Fori(0, TURNS) as i:
                    node = load(i * U + LAG)
                    for b in range(2):
                        n = i * 2 + b
                        pe.wait_ge(s_hot, n + 1)
                        pe.wait_ge(s_prod, n + 1)
                        for r in range(Q):
                            ins = pe.matmul(pq[b][:, r * D:(r + 1) * D], hot[:, b, r * P:(r + 1) * P],
                                            tile_of(qres, node[b * Q + r]), start=True, stop=True)
                        ins.then_inc(s_q, 1)

            @block.vector
            def _(e):
                e.memset(score[:, :, :], 0.0).then_inc(s_first, 1)
                e.tensor_copy(idx[:, :, :], idx_all[:, 0:U].rearrange("p (b r) -> p b r", b=2)).then_inc(s_first, 1)
                e.wait_ge(s_first, 2)
                e.sem_inc(s_idx, 2)
                for x in (s_q, s_prod, s_part):
                    e.sem_inc(x, 2)
                e.sem_inc(s_add, 1)

                def pick(n, b, i):
                    e.wait_ge(s_l[b], i * 16 + 16)
                    e.wait_ge(s_q, n + 1)
                    e.tensor_scalar(hot[:, b, :], loc[:, b, :], k.pcol[:, 0:1], None, ALU.is_equal).then_inc(s_hot, 1)

                def multiply(n, b, turns):
                    e.wait_ge(s_q, n + 3)
                    e.wait_ge(s_g[b], turns * (16 * Q))
                    e.wait_ge(s_part, n + 1)
                    e.tensor_tensor(prod[:, b, :], pq[b][:, :], kv[:, b, :, :].rearrange("p r d -> p (r d)"),
                                    ALU.mult).then_inc(s_prod, 1)

                def reduce(n, b):
                    e.wait_ge(s_prod, n + 3)
                    e.tensor_copy(idx[:, b, :], idx_all[:, bass.ds(n * Q + 2 * Q, Q)]).then_inc(s_idx, 1)
                    e.tensor_reduce(part[:, b, :, :], prod[:, b, :].rearrange("p (r h d) -> p r h d", r=Q, h=heads),
                                    AX, ALU.add).then_inc(s_part, 1)

                def add(n, b, tiles):
                    e.wait_ge(s_part, n + 3)
                    for r in range(Q):
                        to = score[:, bass.ds(tiles[r], 1), 0:heads].rearrange("p a h -> p (a h)")
                        e.wait_ge(s_add, n * Q + r + 1)
                        e.tensor_tensor(to, to, part[:, b, r, :], ALU.add).then_inc(s_add, 1)

                load = registers(k, e, k.step_etile, ETP - 1, "etile")
                pick(0, 0, 0)
                pick(1, 1, 0)
                multiply(0, 0, 1)
                reduce(0, 0)
                with e.Fori(1, TURNS) as i:
                    tiles = load(i * U)
                    n = i * 2
                    pick(n, 0, i)
                    multiply(n - 1, 1, i)
                    add(n - 2, 0, tiles[0:Q])
                    reduce(n - 1, 1)
                    pick(n + 1, 1, i)
                    multiply(n, 0, i + 1)
                    add(n - 1, 1, tiles[Q:])
                    reduce(n, 0)
                n = 2 * TURNS
                tiles = load(n * Q)
                multiply(n - 1, 1, TURNS)
                add(n - 2, 0, tiles[0:Q])
                reduce(n - 1, 1)
                add(n - 1, 1, tiles[Q:])
                e.wait_ge(s_add, n * Q + 1)


def softmax_numerators(k, score, ex, scale):
    nc, io = k.nc, k.io
    L = CG * P
    with ExitStack() as c:
        sc = k.sb(c, "sc", [P, CG, P])
        key = k.sb(c, "key", [P, L])
        st = k.sb(c, "st", [P, CG, P])
        st2 = st[:, :, :].rearrange("p g e -> p (g e)")
        new = k.sb(c, "new", [P, L + 1], BF)
        top = k.sb(c, "top", [P, L])
        far = k.sb(c, "far", [P, L], BF)
        ends = k.sb(c, "ends", [P, 4])
        full = k.sb(c, "full", [P, 2])
        e8 = k.sb(c, "e8", [8, CH, 4])
        m8 = k.sb(c, "m8", [8, 2 * CH])
        n8 = k.sb(c, "n8", [8, 2 * CH + 1])
        k8 = k.sb(c, "k8", [8, 2 * CH])
        got = k.sb(c, "got", [P, 4, H * P])
        pt = [k.ps(c, f"pt{i}") for i in range(7)]
        s_key, s_t, s_st, s_v, s_ends, s_e8, s_m8, s_full = [k.sem(x) for x in
            ("keys_in", "turned", "st_ready", "dve", "ends_out", "ends_in", "full_ready", "full_in")]
        s_sc = k.sem("scores_sorted")
        s_dif, s_ex, s_exd, s_got, s_b, s_bk = [k.sem(x) for x in
            ("shifted", "exp_ready", "exp_stored", "got", "step_turned", "step_kept")]
        with k.block() as block:

            @block.sync
            def _(sp):
                for h in range(H):
                    sp.dma_start(key[h * CH:(h + 1) * CH, :].bitcast(I32), io["dst_flat"].rearrange("(a f) -> a f", a=CH)
                                 ).then_inc(s_key, 16)
                sp.wait_ge(s_ends, 1)
                sp.dma_start(k.ends_d, ends[:, :]).then_inc(s_e8, 16)
                sp.wait_ge(s_e8, 16)
                sp.dma_start(e8[:, :, :], k.ends_d.rearrange("(h a) f -> h a f", a=CH)).then_inc(s_e8, 16)
                sp.wait_ge(s_m8, 1)
                sp.dma_start(k.full_d, m8[:, :]).then_inc(s_full, 16)
                sp.wait_ge(s_full, 16)
                sp.dma_start(full[:, :], k.full_d.rearrange("h (a f) -> (h a) f", f=2)).then_inc(s_full, 16)
                sp.wait_ge(s_ex, 1)
                for h in range(H):
                    sp.dma_start(k.ex_d.rearrange("(a g) (h e) -> h a g e", a=CH, h=H)[h],
                                 st[h * CH:(h + 1) * CH, :, :]).then_inc(s_exd, 16)

            @block.tensor
            def _(pe):
                pe.wait_ge(s_sc, 1)
                for g in range(CG):
                    ins = pe.transpose(pt[g // 4][:, (g % 4) * P:(g % 4 + 1) * P],
                                       sc[:, g, :], k.ident[:, :])
                    if g % 4 == 3 or g == CG - 1:
                        ins.then_inc(s_t, 1)
                pe.wait_ge(s_st, 7)
                for n in range(8):
                    j, half = n // 2, n % 2
                    pe.wait_ge(s_got, 64)
                    if n >= 7:
                        pe.wait_ge(s_bk, n - 6)
                    for h in range(4):
                        hh = half * 4 + h
                        ins = pe.transpose(pt[n % 7][:, h * P:(h + 1) * P], got[:, j, hh * P:(hh + 1) * P],
                                           k.ident[:, :])
                    ins.then_inc(s_b, 1)

            @block.gpsimd
            def _(g):
                g.wait_ge(s_exd, 16 * H)
                for j in range(4):
                    g.indirect_dma_start(got[:, j, :], None, k.ex_d,
                                         bass.IndirectOffsetOnAxis(k.step_tile[:, j:j + 1], 0),
                                         bounds_check=ETP - 1, oob_is_err=True).then_inc(s_got, 16)

            @block.scalar
            def _(a):
                for g in range(7):
                    n = min(4, CG - 4 * g)
                    a.wait_ge(s_t, g + 1)
                    a.activation(st[:, 4 * g:4 * g + n, :],
                                 pt[g][:, 0:n * P].rearrange("p (g e) -> p g e", e=P), ACT.Copy).then_inc(s_st, 1)
                a.wait_ge(s_dif, 1)
                a.activation(st2, top[:, :], ACT.Exp, scale=scale).then_inc(s_ex, 1)
                for n in range(8):
                    j, half = n // 2, n % 2
                    a.wait_ge(s_b, n + 1)
                    a.activation(ex[:, j * P:(j + 1) * P, half * 4:half * 4 + 4].rearrange("p s h -> p h s"),
                                 pt[n % 7][:, :].rearrange("p (h s) -> p h s", h=4), ACT.Copy).then_inc(s_bk, 1)

            @block.vector
            def _(e):
                done = Chain(e, s_v)

                def segment_max(vals, restart, out, n):
                    done(e.tensor_tensor_scan(vals[1], restart[:, 0:n], vals[0], -BIG, ALU.add, ALU.max))
                    done(e.tensor_tensor_scan(out[:, ::-1], restart[:, 1:n + 1][:, ::-1], vals[1][:, ::-1], -BIG,
                                              ALU.add, ALU.max))

                done(e.tensor_copy(sc[:, :, :].rearrange("p g (h a) -> p a g h", h=H),
                                   score[:, :, :].rearrange("p (a g) h -> p a g h", g=CG)))
                e.sem_inc(s_sc, 1)
                e.wait_ge(s_key, 16 * H)
                done(e.memset(new[:, :], -BIG))
                keyf = got[:, :, :].rearrange("p a b -> p (a b)")[:, 0:L]
                done(e.tensor_copy(keyf, key[:, :].bitcast(I32)))
                done(e.tensor_tensor(top[:, 1:L], keyf[:, 1:L], keyf[:, 0:L - 1], ALU.not_equal))
                done(e.tensor_scalar(new[:, 1:L], top[:, 1:L], -BIG, None, ALU.mult))
                e.wait_ge(s_st, 7)
                segment_max((st2, key[:, :]), new, top, L)
                done(e.tensor_copy(ends[:, 0:1], top[:, 0:1]))
                done(e.tensor_copy(ends[:, 1:2], top[:, L - 1:L]))
                done(e.tensor_copy(ends[:, 2:3], keyf[:, 0:1]))
                done(e.tensor_copy(ends[:, 3:4], keyf[:, L - 1:L]))
                e.sem_inc(s_ends, 1)
                done(e.tensor_scalar(far[:, :], keyf, keyf[:, 0:1], -BIG, ALU.not_equal, ALU.mult))
                done(e.tensor_scalar(key[:, :], keyf, keyf[:, L - 1:L], -BIG, ALU.not_equal, ALU.mult))
                e.wait_ge(s_e8, 32)
                done(e.tensor_copy(m8[:, :].rearrange("p (a f) -> p a f", f=2), e8[:, :, 0:2]))
                done(e.tensor_copy(k8[:, :].rearrange("p (a f) -> p a f", f=2), e8[:, :, 2:4]))
                done(e.memset(n8[:, :], -BIG))
                done(e.tensor_tensor(n8[:, 1:2 * CH], k8[:, 1:], k8[:, 0:2 * CH - 1], ALU.not_equal))
                done(e.tensor_scalar(n8[:, 1:2 * CH], n8[:, 1:2 * CH], -BIG, None, ALU.mult))
                segment_max((m8[:, :], k8[:, :]), n8, m8, 2 * CH)
                e.sem_inc(s_m8, 1)
                e.wait_ge(s_full, 32)
                done(e.scalar_tensor_tensor(top[:, :], far[:, :], full[:, 0:1], top[:, :], ALU.add, ALU.max))
                done(e.scalar_tensor_tensor(top[:, :], key[:, :], full[:, 1:2], top[:, :], ALU.add, ALU.max))
                e.tensor_tensor(top[:, :], st2, top[:, :], ALU.subtract).then_inc(s_dif, 1)
                e.wait_ge(s_bk, 8)


def edge_messages(k, ex, acc, v_d, v_idx, v_rows, heads):
    nc = k.nc
    W = D + H
    TURNS = STEPS // U
    with ExitStack() as c:
        vv = k.sb(c, "vv", [P, 2, Q, D])
        msg = k.sb(c, "msg", [P, 2, Q, W])
        pick = k.sb(c, "pick", [P, 2, Q, P])
        idx = k.sb(c, "idx", [P, 2, Q], I32)
        pm = [k.ps(c, f"pm{i}") for i in range(2 * Q)]
        s_first, s_idx, s_msg, s_exc, s_pick, s_mm, s_acc, s_let = [k.sem(x) for x in
            ("msg_first", "idx_ready", "msg_ready", "ex_ready", "pick_ready", "summed", "added", "fetch_let")]
        s_g = [k.sem(f"rows_in{b}") for b in range(2)]
        with k.block() as block:

            @block.gpsimd
            def _(g):
                with g.Fori(0, TURNS) as i:
                    for b in range(2):
                        g.wait_ge(s_idx, i * 2 + b + 1)
                        g.sem_inc(s_let, 1)
                        for r in range(Q):
                            g.indirect_dma_start(vv[:, b, r, :], None, v_d,
                                                 bass.IndirectOffsetOnAxis(idx[:, b, r:r + 1], 0),
                                                 bounds_check=v_rows - 1, oob_is_err=True).then_inc(s_g[b], 16)

            @block.vector
            def _(e):
                e.memset(acc[:, :, :], 0.0).then_inc(s_first, 1)
                e.tensor_copy(idx[:, :, :], v_idx[:, 0:U].rearrange("p (b r) -> p b r", b=2)).then_inc(s_first, 1)
                e.wait_ge(s_first, 2)
                e.sem_inc(s_idx, 2)
                e.sem_inc(s_mm, 2)
                e.sem_inc(s_acc, 1)

                def make(n, b, turns):
                    e.wait_ge(s_mm, n + 1)
                    e.tensor_tensor(pick[:, b, :, :], bc(k.iota[:, :].unsqueeze(1), (P, Q, P)),
                                    bc(k.step_loc[:, bass.ds(n * Q, Q)].unsqueeze(2), (P, Q, P)),
                                    ALU.is_equal).then_inc(s_pick, 1)
                    w = ex[:, bass.ds(n * Q, Q), :]
                    e.tensor_copy(msg[:, b, :, D:], w).then_inc(s_exc, 1)
                    e.wait_ge(s_g[b], turns * (16 * Q))
                    e.tensor_tensor(msg[:, b, :, 0:D].rearrange("p r (h d) -> p r h d", h=heads),
                                    vv[:, b, :, :].rearrange("p r (h d) -> p r h d", h=heads),
                                    bc(w[:, :, 0:heads].unsqueeze(3), (P, Q, heads, D // heads)),
                                    ALU.mult).then_inc(s_msg, 1)

                def next_indices(n, b):
                    e.wait_ge(s_msg, n + 1)
                    e.tensor_copy(idx[:, b, :], v_idx[:, bass.ds(n * Q + 2 * Q, Q)]).then_inc(s_idx, 1)

                def add(n, b, node, r):
                    e.wait_ge(s_acc, n * Q + r + 1)
                    to = acc[:, bass.ds(node[r], 1), :].rearrange("p a w -> p (a w)")
                    e.tensor_tensor(to, to, pm[b * Q + r][:, 0:W], ALU.add).then_inc(s_acc, 1)

                def adds(n, b, node, behind):
                    e.wait_ge(s_mm, n + 3)
                    add(n, b, node, 0)
                    if behind:
                        next_indices(n + 1, 1 - b)
                    for r in range(1, Q):
                        add(n, b, node, r)

                load = registers(k, e, k.step_block, NT - 1, "node")
                make(0, 0, 1)
                next_indices(0, 0)
                node = load(LAG)
                make(1, 1, 1)
                adds(0, 0, node[0:Q], True)
                with e.Fori(1, TURNS) as i:
                    node = load(i * U + (LAG - Q))
                    n = i * 2
                    make(n, 0, i + 1)
                    adds(n - 1, 1, node[0:Q], True)
                    make(n + 1, 1, i + 1)
                    adds(n, 0, node[Q:], True)
                node = load(TURNS * U + (LAG - Q))
                adds(2 * TURNS - 1, 1, node[0:Q], False)
                e.wait_ge(s_acc, STEPS + 1)

            @block.tensor
            def _(pe):
                def turn(i, first):
                    for b in range(2):
                        n = i * 2 + b
                        pe.wait_ge(s_pick, n + 1)
                        pe.wait_ge(s_exc, n + 1)
                        pe.wait_ge(s_msg, n + 1)
                        if not first:
                            pe.wait_ge(s_acc, n * Q - (Q - 1))
                        for r in range(Q):
                            ins = pe.matmul(pm[b * Q + r][:, 0:W], pick[:, b, r, :], msg[:, b, r, :], start=True,
                                            stop=True)
                        ins.then_inc(s_mm, 1)
                turn(0, True)
                with pe.Fori(1, TURNS) as i:
                    turn(i, False)


def reciprocal_sums(k, e, s_v, acc, rden):
    done = Chain(e, s_v)
    done(e.tensor_scalar(rden[:, :, :], acc[:, :, D:], 1e-30, None, ALU.max))
    done(e.reciprocal(rden[:, :, :], rden[:, :, :]))


def finish0(k, acc):
    nc, io = k.nc, k.io
    with ExitStack() as c:
        w = k.sb(c, "wout", [P, 2, D])
        b = k.sb(c, "bout", [P, D])
        rden = k.sb(c, "rden", [P, NT, H])
        hn = k.sb(c, "hn", [P, GROUP, D])
        xn = k.sb(c, "xn", [P, GROUP, D])
        xt = k.sb(c, "xt", [P, GROUP, 2, P])
        pt = [k.ps(c, f"pt{i}") for i in range(2)]
        py = [k.ps(c, f"py{i}") for i in range(2)]
        s_w, s_v, s_a, s_b, s_hn, s_tr, s_xt, s_mm, s_y, s_x = [k.sem(x) for x in
            ("w_loaded", "dve", "normed", "scaled", "h_ready", "turned", "xt_ready", "product", "biased", "x_ready")]
        with k.block() as block:

            @block.sync
            def _(sp):
                sp.dma_start(w[:, :, :], io["W_out"].rearrange("(c p) n -> p c n", p=P)).then_inc(s_w, 16)
                sp.dma_start(b[:, :], row_bc(io["b_out"], P)).then_inc(s_w, 16)

            @block.vector
            def _(e):
                e.wait_ge(s_w, 32)
                reciprocal_sums(k, e, s_v, acc, rden)

                def turn(i, first):
                    for j in range(GROUP):
                        t = i * GROUP + j
                        if not first:
                            e.wait_ge(s_tr, t - GROUP + 1)
                        e.tensor_scalar(xn[:, j, :], tile_of(k.x, t), k.mean[:, bass.ds(t, 1)],
                                        k.rstd[:, bass.ds(t, 1)], ALU.subtract, ALU.mult).then_inc(s_a, 1)
                        e.tensor_tensor(hn[:, j, :].rearrange("p (d h) -> p h d", h=H),
                                        tile_of(acc, t)[:, 0:D].rearrange("p (h d) -> p h d", h=H),
                                        bc(tile_of(rden, t).unsqueeze(2), (P, H, D // H)), ALU.mult).then_inc(s_b, 1)
                        e.wait_ge(s_a, t + 1)
                        e.wait_ge(s_b, t + 1)
                        e.tensor_tensor(hn[:, j, :], hn[:, j, :], xn[:, j, :], ALU.add).then_inc(s_hn, 1)
                    for j in range(GROUP):
                        t = i * GROUP + j
                        e.wait_ge(s_mm, t + 1)
                        e.tensor_tensor(xn[:, j, :], py[j % 2][:, 0:D], b[:, :], ALU.add).then_inc(s_y, 1)
                        e.wait_ge(s_y, t + 1)
                        e.tensor_tensor(tile_of(k.x, t), tile_of(k.x, t), xn[:, j, :], ALU.add).then_inc(s_x, 1)
                turn(0, True)
                with e.Fori(1, NT // GROUP) as i:
                    e.wait_ge(s_x, i * GROUP)
                    turn(i, False)
                e.wait_ge(s_x, NT)

            @block.scalar
            def _(a):
                def turn(i, first):
                    for j in range(GROUP):
                        t = i * GROUP + j
                        a.wait_ge(s_tr, t + 1)
                        if not first:
                            a.wait_ge(s_mm, t - GROUP + 1)
                        a.activation(xt[:, j, :, :], pt[j % 2][:, 0:256].rearrange("p (c n) -> p c n", c=2),
                                     ACT.Copy).then_inc(s_xt, 1)
                turn(0, True)
                with a.Fori(1, NT // GROUP) as i:
                    turn(i, False)

            @block.tensor
            def _(pe):
                pe.wait_ge(s_w, 32)

                def turn(i, first):
                    for j in range(GROUP):
                        t = i * GROUP + j
                        pe.wait_ge(s_hn, t + 1)
                        if not first or j >= 2:
                            pe.wait_ge(s_xt, t - held(j))
                        for h in range(2):
                            ins = pe.transpose(pt[j % 2][:, h * P:(h + 1) * P], hn[:, j, h * P:(h + 1) * P],
                                               k.ident[:, :])
                        ins.then_inc(s_tr, 1)
                    for j in range(GROUP):
                        t = i * GROUP + j
                        pe.wait_ge(s_xt, t + 1)
                        if not first or j >= 2:
                            pe.wait_ge(s_y, t - held(j))
                        for h in range(2):
                            ins = pe.matmul(py[j % 2][:, 0:D], xt[:, j, h, :], w[:, h, :], start=(h == 0), stop=(h == 1))
                        ins.then_inc(s_mm, 1)
                turn(0, True)
                with pe.Fori(1, NT // GROUP) as i:
                    turn(i, False)


def normalize(k, x, out):
    nc = k.nc
    s_v = k.sem("normed")
    with k.block() as block:

        @block.vector
        def _(e):
            with e.Fori(0, NT // GROUP) as i:
                for j in range(GROUP):
                    t = i * GROUP + j
                    e.tensor_scalar(tile_of(out, t), tile_of(x, t), k.mean[:, bass.ds(t, 1)],
                                    k.rstd[:, bass.ds(t, 1)], ALU.subtract, ALU.mult).then_inc(s_v, 1)
            e.wait_ge(s_v, NT)


def columns(k, x, xnt, router, w_router, R, affine):
    nc, io = k.nc, k.io
    with ExitStack() as c:
        wr = k.sb(c, "wr", [P, 2, R])
        gb = k.sb(c, "gb", [P, 2, 2])
        xn = k.sb(c, "xn", [P, GROUP, D])
        xt = k.sb(c, "xt", [P, GROUP, 2, P])
        pt = [k.ps(c, f"pt{i}") for i in range(2)]
        pr = [k.ps(c, f"pr{i}") for i in range(2)]
        s_w, s_xn, s_tr, s_xt, s_mm, s_r, s_cp = [k.sem(x) for x in
            ("w_loaded", "xn_ready", "turned", "xt_ready", "routed", "router_kept", "xt_kept")]
        n_w = 1 + 2 * bool(affine)
        with k.block() as block:

            @block.sync
            def _(sp):
                sp.dma_start(wr[:, :, :], io[w_router].rearrange("(c p) n -> p c n", p=P)).then_inc(s_w, 16)
                if affine:
                    for n, name in enumerate(affine):
                        sp.dma_start(gb[:, n, :], io[name].rearrange("p c -> p c")).then_inc(s_w, 16)

            @block.vector
            def _(e):
                def turn(i, first):
                    for j in range(GROUP):
                        t = i * GROUP + j
                        if not first:
                            e.wait_ge(s_tr, t - GROUP + 1)
                        e.tensor_scalar(xn[:, j, :], tile_of(x, t), k.mean[:, bass.ds(t, 1)],
                                        k.rstd[:, bass.ds(t, 1)], ALU.subtract, ALU.mult).then_inc(s_xn, 1)
                    for j in range(GROUP):
                        t = i * GROUP + j
                        e.wait_ge(s_mm, t + 1)
                        e.tensor_copy(tile_of(router, t), pr[j % 2][:, 0:R]).then_inc(s_r, 1)
                turn(0, True)
                with e.Fori(1, NT // GROUP) as i:
                    turn(i, False)
                e.wait_ge(s_r, NT)

            @block.scalar
            def _(a):
                a.wait_ge(s_w, 16 * n_w)

                def turn(i, first):
                    for j in range(GROUP):
                        t = i * GROUP + j
                        a.wait_ge(s_tr, t + 1)
                        if not first:
                            a.wait_ge(s_mm, t - GROUP + 1)
                        for h in range(2):
                            src = pt[j % 2][:, h * P:(h + 1) * P]
                            for n, to in enumerate((xt[:, j, h, :], xnt[:, h, bass.ds(t * P, P)])):
                                if affine:
                                    ins = a.activation(to, src, ACT.Identity, bias=gb[:, 1, h:h + 1],
                                                       scale=gb[:, 0, h:h + 1])
                                else:
                                    ins = a.activation(to, src, ACT.Copy)
                        ins.then_inc(s_xt, 1)
                turn(0, True)
                with a.Fori(1, NT // GROUP) as i:
                    turn(i, False)

            @block.tensor
            def _(pe):
                pe.wait_ge(s_w, 16 * n_w)

                def turn(i, first):
                    for j in range(GROUP):
                        t = i * GROUP + j
                        pe.wait_ge(s_xn, t + 1)
                        if not first or j >= 2:
                            pe.wait_ge(s_xt, t - held(j))
                        for h in range(2):
                            ins = pe.transpose(pt[j % 2][:, h * P:(h + 1) * P], xn[:, j, h * P:(h + 1) * P],
                                               k.ident[:, :])
                        ins.then_inc(s_tr, 1)
                    for j in range(GROUP):
                        t = i * GROUP + j
                        pe.wait_ge(s_xt, t + 1)
                        if not first or j >= 2:
                            pe.wait_ge(s_r, t - held(j))
                        for h in range(2):
                            ins = pe.matmul(pr[j % 2][:, 0:R], xt[:, j, h, :], wr[:, h, :], start=(h == 0),
                                            stop=(h == 1))
                        ins.then_inc(s_mm, 1)
                turn(0, True)
                with pe.Fori(1, NT // GROUP) as i:
                    turn(i, False)


def top2_gates(k, score, gate, E, b_router=None):
    nc, io = k.nc, k.io
    with ExitStack() as c:
        b = k.sb(c, "b", [P, E])
        work = k.sb(c, "work", [P, NT, E])
        cand = k.sb(c, "cand", [P, NT, E])
        one = [k.sb(c, f"one{i}", [P, NT, E]) for i in range(2)]
        m = [k.sb(c, f"m{i}", [P, NT]) for i in range(2)]
        pick = k.sb(c, "pick", [P, NT])
        ww = [k.sb(c, f"ww{i}", [P, NT]) for i in range(2)]
        s_b, s_v, s_d, s_e = [k.sem(x) for x in ("b_loaded", "dve", "gap_ready", "exp_ready")]
        wide = lambda a: bc(a[:, :].unsqueeze(2), (P, NT, E))
        iota = bc(k.iota[:, 0:E].unsqueeze(1), (P, NT, E))
        with k.block() as block:

            if b_router:
                @block.sync
                def _(sp):
                    sp.dma_start(b[:, :], row_bc(io[b_router], P)).then_inc(s_b, 16)

            @block.vector
            def _(e):
                done = Chain(e, s_v)
                if b_router:
                    e.wait_ge(s_b, 16)
                    done(e.tensor_tensor(score[:, :, :], score[:, :, :], bc(b[:, :].unsqueeze(1), (P, NT, E)), ALU.add))
                done(e.tensor_copy(work[:, :, :], score[:, :, :]))
                for n in range(2):
                    done(e.tensor_reduce(m[n][:, :], work[:, :, :], AX, ALU.max))
                    done(e.tensor_tensor(cand[:, :, :], work[:, :, :], wide(m[n]), ALU.is_lt))
                    done(e.scalar_tensor_tensor(cand[:, :, :], cand[:, :, :], 99.0, iota, ALU.mult, ALU.add))
                    done(e.tensor_reduce(pick[:, :], cand[:, :, :], AX, ALU.min))
                    done(e.tensor_tensor(one[n][:, :, :], cand[:, :, :], wide(pick), ALU.is_equal))
                    if n == 0:
                        done(e.scalar_tensor_tensor(work[:, :, :], one[0][:, :, :], -BIG, work[:, :, :],
                                                    ALU.mult, ALU.add))
                done(e.tensor_tensor(m[1][:, :], m[1][:, :], m[0][:, :], ALU.subtract))
                e.sem_inc(s_d, 1)
                e.wait_ge(s_e, 1)
                done(e.tensor_scalar(ww[0][:, :], ww[1][:, :], 1.0, None, ALU.add))
                done(e.reciprocal(ww[0][:, :], ww[0][:, :]))
                done(e.tensor_tensor(ww[1][:, :], ww[1][:, :], ww[0][:, :], ALU.mult))
                done(e.tensor_tensor(one[0][:, :, :], one[0][:, :, :], wide(ww[0]), ALU.mult))
                done(e.tensor_tensor(one[1][:, :, :], one[1][:, :, :], wide(ww[1]), ALU.mult))
                done(e.tensor_tensor(gate[:, :, :], one[0][:, :, :], one[1][:, :, :], ALU.add))

            @block.scalar
            def _(a):
                a.wait_ge(s_d, 1)
                a.activation(ww[1][:, :], m[1][:, :], ACT.Exp).then_inc(s_e, 1)


def mark_mask(k, block, c, s_cleared, s_neg):
    idx = k.sb(c, "idx", [P, 2], I32)
    zero1 = k.sb(c, "zero1", [P, 1], BF)
    s_i, s_mark, s_let, s_z = [k.sem(x) for x in ("pos_ready", "marked", "scatter_let", "zero_ready")]

    @block.gpsimd
    def _(g):
        g.memset(zero1[:, :], 0.0).then_inc(s_z, 1)
        g.wait_ge(s_z, 1)
        g.wait_ge(s_cleared, 16 * NT)

        def scatter(b):
            g.sem_inc(s_let, 1)
            g.indirect_dma_start(k.mask_d, bass.IndirectOffsetOnAxis(idx[:, b:b + 1], 0), zero1[:, :], None,
                                 bounds_check=NP * NP - 1, oob_is_err=True).then_inc(s_mark, 16)
        for b in range(2):
            g.tensor_copy(idx[:, b:b + 1], k.mask_pos[:, b:b + 1]).then_inc(s_i, 1)
        g.wait_ge(s_i, 2)
        scatter(0)
        with g.Fori(0, GT // 2 - 1) as i:
            for b in range(2):
                g.wait_ge(s_mark, i * 32 + 16 * b + 16)
                scatter(1 - b)
                g.tensor_copy(idx[:, b:b + 1], k.mask_pos[:, bass.ds(i * 2 + b + 2, 1)]).then_inc(s_i, 1)
                g.wait_ge(s_i, i * 2 + b + 3)
        g.wait_ge(s_mark, 16 * (GT - 1))
        scatter(1)
        g.wait_ge(s_mark, 16 * GT)


def experts(k, xnt, gate, E, names, mask=False):
    nc, io = k.nc, k.io
    F = 512
    FC = F // P
    W1, b1, W2, b2 = names
    with ExitStack() as c:
        w1 = k.sb(c, "w1", [P, E, 2, F])
        w2 = k.sb(c, "w2", [P, E, FC, D])
        b1s = k.sb(c, "b1s", [P, E, FC])
        b2s = k.sb(c, "b2s", [P, E, D])
        ht = k.sb(c, "ht", [P, 2, FC, P])
        y = k.sb(c, "y", [P, 2, D])
        ph = [k.ps(c, f"ph{i}") for i in range(2)]
        py = [k.ps(c, f"py{i}") for i in range(2)]
        s_w, s_h, s_g, s_y, s_b, s_x = [k.sem(x) for x in
            ("w_loaded", "hidden", "gelu_ready", "product", "biased", "x_ready")]
        s_neg, s_cleared = k.sem("neg_ready"), k.sem("mask_cleared")
        neg = k.sb(c, "neg", [P, NP // 4], BF)
        with k.block() as block:
            if mask:
                mark_mask(k, block, c, s_cleared, s_neg)

            @block.sync
            def _(sp):
                sp.dma_start(w1[:, :, :, :], io[W1].rearrange("e (c p) f -> p e c f", p=P)).then_inc(s_w, 16)
                sp.dma_start(w2[:, :, :, :], io[W2].rearrange("e (c p) d -> p e c d", p=P)).then_inc(s_w, 16)
                sp.dma_start(b1s[:, :, :], io[b1]).then_inc(s_w, 16)
                sp.dma_start(b2s[:, :, :].rearrange("p e d -> p (e d)"),
                             row_bc(io[b2].rearrange("e d -> (e d)"), P)).then_inc(s_w, 16)
                if mask:
                    sp.wait_ge(s_neg, 1)
                    clear = k.mask_d.rearrange("(t p n f) o -> t p n (f o)", p=P, n=4, f=NP // 4)
                    for t in range(NT):
                        sp.dma_start(clear[t], bc(neg[:, :].unsqueeze(1), (P, 4, NP // 4))).then_inc(s_cleared, 16)

            @block.tensor
            def _(pe):
                pe.wait_ge(s_w, 64)

                def hidden(i, n, first):
                    if not first:
                        pe.wait_ge(s_g, i * E + n - 1)
                    for f in range(FC):
                        for h in range(2):
                            ins = pe.matmul(ph[n % 2][:, f * P:(f + 1) * P], w1[:, n, h, f * P:(f + 1) * P],
                                            xnt[:, h, bass.ds(i * P, P)], start=(h == 0), stop=(h == 1))
                    ins.then_inc(s_h, 1)

                def output(i, n, first):
                    pe.wait_ge(s_g, i * E + n + 1)
                    if not first:
                        pe.wait_ge(s_b, i * E + n - 1)
                    for f in range(FC):
                        ins = pe.matmul(py[n % 2][:, 0:D], ht[:, n % 2, f, :], w2[:, n, f, :], start=(f == 0),
                                        stop=(f == FC - 1))
                    ins.then_inc(s_y, 1)

                def turn(i, first):
                    hidden(i, 0, first)
                    for n in range(E):
                        if n + 1 < E:
                            hidden(i, n + 1, first and n + 1 < 2)
                        output(i, n, first and n < 2)
                turn(0, True)
                with pe.Fori(1, NT) as i:
                    turn(i, False)

            @block.scalar
            def _(a):
                a.wait_ge(s_w, 64)

                def turn(i, first):
                    for n in range(E):
                        a.wait_ge(s_h, i * E + n + 1)
                        if not (first and n < 2):
                            a.wait_ge(s_y, i * E + n - 1)
                        for f in range(FC):
                            ins = a.activation(ht[:, n % 2, f, :], ph[n % 2][:, f * P:(f + 1) * P], ACT.Gelu,
                                               bias=b1s[:, n, f:f + 1])
                        ins.then_inc(s_g, 1)
                turn(0, True)
                with a.Fori(1, NT) as i:
                    turn(i, False)

            @block.vector
            def _(e):
                e.memset(neg[:, :], -BIG).then_inc(s_neg, 1)
                e.wait_ge(s_w, 64)
                e.sem_inc(s_x, 1)
                with e.Fori(0, NT) as i:
                    for n in range(E):
                        e.wait_ge(s_y, i * E + n + 1)
                        e.tensor_tensor(y[:, n % 2, :], py[n % 2][:, 0:D], b2s[:, n, :], ALU.add).then_inc(s_b, 1)
                        e.wait_ge(s_b, i * E + n + 1)
                        e.wait_ge(s_x, i * E + n + 1)
                        e.scalar_tensor_tensor(tile_of(k.x, i), y[:, n % 2, :],
                                               tile_of(gate, i)[:, n:n + 1], tile_of(k.x, i),
                                               ALU.mult, ALU.add).then_inc(s_x, 1)
                e.wait_ge(s_x, NT * E + 1)


def project1(k, qres):
    nc, io = k.nc, k.io
    T, R = 4, 8
    with ExitStack() as c:
        w = k.sb(c, "wkvq", [P, 3, T, 2, D])
        rel = k.sb(c, "rel", [P, 2, 2, R, P])
        pri = k.sb(c, "pri", [P, R, 4])
        xn = k.sb(c, "xn", [P, GROUP, D])
        xm = k.sb(c, "xm", [P, 2, T, 2, P])
        kvt = k.sb(c, "kvt", [P, 2, 4, P])
        stage = k.sb(c, "stage", [P, 2, 2, R, D])
        pt = [k.ps(c, f"pt{i}") for i in range(2)]
        pk = k.ps(c, "pk")
        pq = k.ps(c, "pq")
        po = [k.ps(c, f"po{i}") for i in range(4)]
        s_w, s_z, s_blk, s_v, s_xn, s_tr, s_xm, s_kv, s_q, s_kvt, s_qs = [k.sem(x) for x in
            ("w_loaded", "rel_zero", "rel_loaded", "dve", "xn_ready", "turned", "masked", "kv_ready", "q_ready",
             "kvt_ready", "q_kept")]
        s_o, s_od, s_oa, s_rel = [k.sem(x) for x in ("out_ready", "out_kept_dve", "out_kept_act", "rel_scaled")]
        s_st = [k.sem(f"stored{j}") for j in range(2)]
        kv_to = [x.rearrange("(t p r) d -> p t (r d)", p=P, r=R) for x in (k.kr_d, k.vr_d)]
        with k.block() as block:

            @block.sync
            def _(sp):
                for n, name in enumerate(("k_linears", "v_linears", "q_linears")):
                    sp.dma_start(w[:, n, :, :, :], io[name].rearrange("t (c p) o -> p t c o", p=P)).then_inc(s_w, 16)
                sp.dma_start(pri[:, :, :].rearrange("p r h -> p (r h)"), row_bc(io["pri"], P)).then_inc(s_w, 16)
                sp.wait_ge(s_z, 1)
                for n, name in enumerate(("att_t", "msg")):
                    for h in range(4):
                        o = (h % 2) * 64
                        sp.dma_start(rel[o:o + 64, n, h // 2, :, o:o + 64], io[name][h]).then_inc(s_blk, 16)

                def turn(i, first):
                    for j in range(GROUP):
                        t = i * GROUP + j
                        sp.wait_ge(s_od, (t + 1) * 4)
                        sp.wait_ge(s_oa, (t + 1) * 4)
                        for n in range(2):
                            sp.dma_start(kv_to[n][:, bass.ds(t, 1), :].rearrange("p a f -> p (a f)"),
                                         stage[:, j % 2, n, :, :].rearrange("p r d -> p (r d)")
                                         ).then_inc(s_st[j % 2], 16)
                with sp.Fori(0, NT // GROUP) as i:
                    turn(i, False)
                sp.wait_ge(s_st[0], 32 * 3 * (NT // GROUP))
                sp.wait_ge(s_st[1], 32 * 2 * (NT // GROUP))

            def free_stage(eng, i, j, first):
                uses = (3, 2)[j % 2]
                if not first or j >= 2:
                    eng.wait_ge(s_st[j % 2], i * (32 * uses) + 32 * (j // 2))

            def mask(e, j, t, n):
                return e.scalar_tensor_tensor(
                    xm[:, j % 2, n, :, :], bc(k.ntype[:, bass.ds(t * P, P)].unsqueeze(1), (P, 2, P)), float(n),
                    pt[j % 2][:, 0:2 * P].rearrange("p (c n) -> p c n", c=2), ALU.is_equal, ALU.mult)

            def stage_half(j, m):
                return stage[:, j % 2, m // 4, (m % 2) * 4:(m % 2) * 4 + 4, (m // 2 % 2) * P:(m // 2 % 2 + 1) * P]

            @block.vector
            def _(e):
                done = Chain(e, s_v)
                e.memset(rel[:, :, :, :, :], 0.0).then_inc(s_z, 1)
                e.wait_ge(s_w, 64)
                e.wait_ge(s_blk, 16 * 8)
                done(e.tensor_scalar(pri[:, :, :], pri[:, :, :], 0.125, None, ALU.mult))
                for h in range(4):
                    o = (h % 2) * 64
                    blk = rel[o:o + 64, 0, h // 2, :, o:o + 64]
                    done(e.tensor_tensor(blk, blk, bc(pri[o:o + 64, :, h:h + 1], (64, R, 64)), ALU.mult))
                e.sem_inc(s_rel, 1)

                def norm(i, j, first):
                    t = i * GROUP + j
                    if not first:
                        e.wait_ge(s_tr, t - GROUP + 1)
                    e.tensor_scalar(xn[:, j, :], tile_of(k.x, t), k.mean[:, bass.ds(t, 1)],
                                    k.rstd[:, bass.ds(t, 1)], ALU.subtract, ALU.mult).then_inc(s_xn, 1)

                def turn(i, first):
                    for j in range(GROUP):
                        norm(i, j, first)
                    for j in range(GROUP):
                        t = i * GROUP + j
                        e.wait_ge(s_tr, t + 1)
                        if not first or j >= 2:
                            e.wait_ge(s_q, t - held(j))
                        for n in range(T):
                            ins = mask(e, j, t, n)
                            ins.then_inc(s_xm, 1)
                        free_stage(e, i, j, first)
                        for m in range(0, 8, 2):
                            e.wait_ge(s_o, t * 8 + m + 1)
                            e.tensor_copy(stage_half(j, m), po[m % 4][:, :].rearrange("p (r d) -> p r d", r=4)
                                          ).then_inc(s_od, 1)
                turn(0, True)
                with e.Fori(1, NT // GROUP) as i:
                    turn(i, False)

            @block.scalar
            def _(a):
                def turn(i, first):
                    for j in range(GROUP):
                        t = i * GROUP + j
                        free_stage(a, i, j, first)
                        a.wait_ge(s_kv, t + 1)
                        a.activation(kvt[:, j % 2, :, :], pk[:, :].rearrange("p (m n) -> p m n", m=4),
                                     ACT.Copy).then_inc(s_kvt, 1)
                        a.wait_ge(s_q, t + 1)
                        a.activation(tile_of(qres, t), pq[:, 0:D], ACT.Copy).then_inc(s_qs, 1)
                        for m in range(1, 8, 2):
                            a.wait_ge(s_o, t * 8 + m + 1)
                            a.activation(stage_half(j, m), po[m % 4][:, :].rearrange("p (r d) -> p r d", r=4),
                                         ACT.Copy).then_inc(s_oa, 1)
                turn(0, True)
                with a.Fori(1, NT // GROUP) as i:
                    turn(i, False)

            @block.tensor
            def _(pe):
                pe.wait_ge(s_w, 64)
                pe.wait_ge(s_rel, 1)

                def turned(i, j, first):
                    t = i * GROUP + j
                    pe.wait_ge(s_xn, t + 1)
                    if not first or j >= 2:
                        pe.wait_ge(s_xm, (t - held(j)) * T)
                    for h in range(2):
                        ins = pe.transpose(pt[j % 2][:, h * P:(h + 1) * P], xn[:, j, h * P:(h + 1) * P],
                                           k.ident[:, :])
                    ins.then_inc(s_tr, 1)

                def turn(i, first):
                    turned(i, 0, first)
                    for j in range(GROUP):
                        t = i * GROUP + j
                        if j + 1 < GROUP:
                            turned(i, j + 1, first)
                        pe.wait_ge(s_xm, (t + 1) * T)
                        if not first or j:
                            pe.wait_ge(s_kvt, t)
                            pe.wait_ge(s_qs, t)
                        for m in range(4):
                            for n in range(T):
                                for h in range(2):
                                    ins = pe.matmul(pk[:, m * P:(m + 1) * P],
                                                    w[:, m // 2, n, h, (m % 2) * P:(m % 2 + 1) * P],
                                                    xm[:, j % 2, n, h, :], start=(n == 0 and h == 0),
                                                    stop=(n == T - 1 and h == 1))
                        ins.then_inc(s_kv, 1)
                        for n in range(T):
                            for h in range(2):
                                ins = pe.matmul(pq[:, 0:D], xm[:, j % 2, n, h, :], w[:, 2, n, h, :],
                                                start=(n == 0 and h == 0), stop=(n == T - 1 and h == 1))
                        ins.then_inc(s_q, 1)
                        pe.wait_ge(s_kvt, t + 1)
                        for m in range(8):
                            mine = s_od if m % 2 == 0 else s_oa
                            if m >= 4:
                                pe.wait_ge(mine, t * 4 + m // 2 - 1)
                            elif not first or j:
                                pe.wait_ge(mine, t * 4 - 1 + m // 2)
                            pe.matmul(po[m % 4][:, :], kvt[:, j % 2, m // 2, :],
                                      rel[:, m // 4, m // 2 % 2, (m % 2) * 4:(m % 2) * 4 + 4, :]
                                      .rearrange("p r d -> p (r d)"), start=True, stop=True).then_inc(s_o, 1)
                turn(0, True)
                with pe.Fori(1, NT // GROUP) as i:
                    turn(i, False)


def finish1(k, acc):
    nc, io = k.nc, k.io
    T = 4
    with ExitStack() as c:
        w = k.sb(c, "wa", [P, T, 2, D])
        skip = k.sb(c, "skip", [P, T])
        rden = k.sb(c, "rden", [P, NT, H])
        hn = k.sb(c, "hn", [P, GROUP, D])
        xm = k.sb(c, "xm", [P, GROUP, T, 2, P])
        pt = [k.ps(c, f"pt{i}") for i in range(2)]
        py = [k.ps(c, f"py{i}") for i in range(2)]
        s_w, s_v, s_sig, s_wr, s_hn, s_tr, s_xm, s_mm, s_x = [k.sem(x) for x in
            ("w_loaded", "dve", "sigmoid", "w_ready", "h_ready", "turned", "masked", "product", "x_ready")]
        with k.block() as block:

            @block.sync
            def _(sp):
                sp.dma_start(w[:, :, :, :], io["a_linears"].rearrange("t (c p) o -> p t c o", p=P)).then_inc(s_w, 16)
                sp.dma_start(skip[:, :], row_bc(io["skip"], P)).then_inc(s_w, 16)

            @block.scalar
            def _(a):
                a.wait_ge(s_w, 32)
                a.activation(skip[:, :], skip[:, :], ACT.Sigmoid).then_inc(s_sig, 1)

            @block.vector
            def _(e):
                done = Chain(e, s_v)
                reciprocal_sums(k, e, k.sem("sums"), acc, rden)
                e.wait_ge(s_w, 32)
                e.wait_ge(s_sig, 1)
                for n in range(T):
                    done(e.tensor_scalar(w[:, n, :, :], w[:, n, :, :], skip[:, n:n + 1], None, ALU.mult))
                e.sem_inc(s_wr, 1)

                def turn(i, first):
                    for j in range(GROUP):
                        t = i * GROUP + j
                        if not first:
                            e.wait_ge(s_tr, t - GROUP + 1)
                        e.tensor_tensor(hn[:, j, :].rearrange("p (h d) -> p h d", h=4),
                                        tile_of(acc, t)[:, 0:D].rearrange("p (h d) -> p h d", h=4),
                                        bc(tile_of(rden, t)[:, 0:4].unsqueeze(2), (P, 4, D // 4)),
                                        ALU.mult).then_inc(s_hn, 1)
                    for j in range(GROUP):
                        t = i * GROUP + j
                        e.wait_ge(s_tr, t + 1)
                        if not first:
                            e.wait_ge(s_mm, t - GROUP + 1)
                        for n in range(T):
                            e.scalar_tensor_tensor(
                                xm[:, j, n, :, :], bc(k.ntype[:, bass.ds(t * P, P)].unsqueeze(1), (P, 2, P)), float(n),
                                pt[j % 2][:, 0:2 * P].rearrange("p (c n) -> p c n", c=2), ALU.is_equal,
                                ALU.mult).then_inc(s_xm, 1)
                    for j in range(GROUP):
                        t = i * GROUP + j
                        e.wait_ge(s_mm, t + 1)
                        e.tensor_tensor(tile_of(k.x, t), tile_of(k.x, t), py[j % 2][:, 0:D], ALU.add).then_inc(s_x, 1)
                turn(0, True)
                with e.Fori(1, NT // GROUP) as i:
                    turn(i, False)
                e.wait_ge(s_x, NT)

            @block.tensor
            def _(pe):
                pe.wait_ge(s_wr, 1)

                def turn(i, first):
                    for j in range(GROUP):
                        t = i * GROUP + j
                        pe.wait_ge(s_hn, t + 1)
                        if not first or j >= 2:
                            pe.wait_ge(s_xm, (t - held(j)) * T)
                        for h in range(2):
                            ins = pe.transpose(pt[j % 2][:, h * P:(h + 1) * P], hn[:, j, h * P:(h + 1) * P],
                                               k.ident[:, :])
                        ins.then_inc(s_tr, 1)
                    for j in range(GROUP):
                        t = i * GROUP + j
                        pe.wait_ge(s_xm, (t + 1) * T)
                        if not first or j >= 2:
                            pe.wait_ge(s_x, t - held(j))
                        for n in range(T):
                            for h in range(2):
                                ins = pe.matmul(py[j % 2][:, 0:D], xm[:, j, n, h, :], w[:, n, h, :],
                                                start=(n == 0 and h == 0), stop=(n == T - 1 and h == 1))
                        ins.then_inc(s_mm, 1)
                turn(0, True)
                with pe.Fori(1, NT // GROUP) as i:
                    turn(i, False)


def leaky(e, done, out, x):
    done(e.scalar_tensor_tensor(out, x, 0.2, x, ALU.mult, ALU.max))


def gate_tables(k, h16, gs, gd):
    nc, io = k.nc, k.io
    with ExitStack() as c:
        att = k.sb(c, "att", [P, 2, 16])
        prod = k.sb(c, "prod", [P, 2, NT, 16])
        arow = k.sb(c, "arow", [4, NP])
        every = k.sb(c, "every", [P, 4, NP])
        mask = k.sb(c, "mask", [P, GROUP, NP], BF)
        scr = k.sb(c, "scr", [P, NP], BF)
        mx = k.sb(c, "mx", [P, 2, GROUP * 4])
        most = k.sb(c, "most", [P, NT * 4])
        pt = [k.ps(c, f"pt{i}") for i in range(7)]
        s_w, s_v, s_t, s_tk, s_row, s_all, s_mx, s_cp = [k.sem(x) for x in
            ("w_loaded", "dve", "turned", "row_kept", "row_ready", "row_spread", "maxima", "maxima_kept")]
        s_let = k.sem("mask_let")
        s_as, s_gd, s_out = k.sem("asrc_ready"), k.sem("gd_ready"), k.sem("stored")
        s_m = [k.sem(f"mask_in{j}") for j in range(GROUP)]
        rows = k.mask_d.rearrange("(t p f) o -> p t (f o)", p=P, f=NP)
        with k.block() as block:

            @block.sync
            def _(sp):
                sp.dma_start(att[:, 0, :], row_bc(io["att_src"], P)).then_inc(s_w, 16)
                sp.dma_start(att[:, 1, :], row_bc(io["att_dst"], P)).then_inc(s_w, 16)
                for j in range(GROUP):
                    sp.dma_start(mask[:, j, :], rows[:, j, :]).then_inc(s_m[j], 16)
                sp.wait_ge(s_tk, 7)
                sp.dma_start(k.asrc_d, arow[:, :]).then_inc(s_row, 16)
                sp.wait_ge(s_row, 16)
                sp.dma_start(every[:, :, :].rearrange("p h n -> p (h n)"),
                             row_bc(k.asrc_d.rearrange("h n -> (h n)"), P)).then_inc(s_all, 16)
                sp.dma_start(k.gs_d.rearrange("(t p) f -> p t f", p=P), gs[:, :, :]).then_inc(s_out, 16)
                with sp.Fori(1, NT // GROUP) as i:
                    for j in range(GROUP):
                        sp.wait_ge(s_mx, (i * GROUP + j - GROUP) * 4 + 4)
                        sp.dma_start(mask[:, j, :], rows[:, bass.ds(i * GROUP + j, 1), :].rearrange("p a f -> p (a f)")
                                     ).then_inc(s_m[j], 16)
                sp.wait_ge(s_gd, 1)
                sp.dma_start(k.gd_d.rearrange("(t p) f -> p t f", p=P), gd[:, :, :]).then_inc(s_out, 16)
                sp.wait_ge(s_out, 32)

            @block.tensor
            def _(pe):
                pe.wait_ge(s_as, 1)
                for t in range(NT):
                    ins = pe.transpose(pt[t // 4][0:4, (t % 4) * P:(t % 4 + 1) * P], gs[:, t, 0:4], k.ident[:, :])
                    if t % 4 == 3 or t == NT - 1:
                        ins.then_inc(s_t, 1)

            @block.scalar
            def _(a):
                for g in range(7):
                    n = min(4, NT - 4 * g)
                    a.wait_ge(s_t, g + 1)
                    a.activation(arow[:, g * 4 * P:(g * 4 + n) * P], pt[g][0:4, 0:n * P], ACT.Copy).then_inc(s_tk, 1)

            @block.vector
            def _(e):
                done = Chain(e, s_v)
                e.wait_ge(s_w, 32)
                for n, out in enumerate((gs, gd)):
                    done(e.tensor_tensor(prod[:, n, :, :], h16[:, :, :], bc(att[:, n:n + 1, :], (P, NT, 16)), ALU.mult))
                    done(e.tensor_reduce(out[:, :, 0:4], prod[:, n, :, :].rearrange("p t (h x) -> p t h x", x=4),
                                         AX, ALU.add))
                done(e.tensor_copy(gs[:, :, 4:20], h16[:, :, :]))
                e.sem_inc(s_as, 1)
                e.wait_ge(s_all, 16)
                with e.Fori(0, NT // GROUP) as i:
                    for j in range(GROUP):
                        e.wait_ge(s_m[j], i * 16 + 16)
                        e.sem_inc(s_let, 1)
                        for h in range(4):
                            e.tensor_tensor_reduce(scr[:, :], mask[:, j, :], every[:, h, :], 1.0, -BIG, ALU.add,
                                                   ALU.max, mx[:, 0, j * 4 + h:j * 4 + h + 1]).then_inc(s_mx, 1)
                            e.wait_ge(s_mx, (i * GROUP + j) * 4 + h + 1)
                            e.sem_inc(s_let, 1)
                    e.wait_ge(s_mx, (i + 1) * (GROUP * 4))
                    e.tensor_copy(most[:, bass.ds(i * (GROUP * 4), GROUP * 4)], mx[:, 0, :]).then_inc(s_cp, 1)
                    e.wait_ge(s_cp, i + 1)
                m3 = most[:, :].rearrange("p (t h) -> p t h", h=4)
                done(e.tensor_tensor(m3, m3, gs[:, :, 0:4], ALU.max))
                done(e.tensor_tensor(m3, m3, gd[:, :, 0:4], ALU.add))
                leaky(e, done, gd[:, :, 4:8], m3)
                e.sem_inc(s_gd, 1)


def gate_sums(k, gs, gd, score):
    nc, io = k.nc, k.io
    B = 8
    C = NT * 20
    with ExitStack() as c:
        idx = k.sb(c, "idx", [P, 2, B, 2], I32)
        rs = k.sb(c, "rs", [P, 2, B, 20])
        rd = k.sb(c, "rd", [P, 2, B, 8])
        ev = k.sb(c, "ev", [P, 2, B, 4])
        f = k.sb(c, "f", [P, 2, B, 20])
        lo = k.sb(c, "lo", [P, 2, B, P])
        hi = k.sb(c, "hi", [P, 2, B, NT])
        wide = k.sb(c, "wide", [P, 2, C])
        zero = k.sb(c, "zero", [P, C])
        agg = k.sb(c, "agg", [P, NT, 20])
        own = k.sb(c, "own", [P, NT, 20])
        nrm = k.sb(c, "nrm", [P, NT, 16])
        sq = k.sb(c, "sq", [P, NT, 16])
        m1 = k.sb(c, "m1", [P, NT])
        v1 = k.sb(c, "v1", [P, NT])
        par = k.sb(c, "par", [P, 3, 16])
        pa = k.ps(c, "pa")
        s_w, s_first, s_idx, s_v, s_e, s_ex, s_hot, s_mm, s_own, s_ownx, s_var, s_std = [k.sem(x) for x in
            ("w_loaded", "first", "idx_ready", "dve", "gap_ready", "exp_ready", "wide_ready", "summed", "loop_gap",
             "loop_exp", "var_ready", "std_ready")]
        s_let = k.sem("fetch_let")
        s_g = [k.sem(f"rows_in{b}") for b in range(2)]
        with k.block() as block:

            @block.sync
            def _(sp):
                for n, name in enumerate(("b_gat", "ln_gamma", "ln_beta")):
                    sp.dma_start(par[:, n, :], row_bc(io[name], P)).then_inc(s_w, 16)

            @block.gpsimd
            def _(g):
                with g.Fori(0, GT // (2 * B)) as i:
                    for b in range(2):
                        g.wait_ge(s_idx, i * 2 + b + 1)
                        g.sem_inc(s_let, 1)
                        for j in range(B):
                            g.indirect_dma_start(rd[:, b, j, :], None, k.gd_d,
                                                 bass.IndirectOffsetOnAxis(idx[:, b, j, 0:1], 0),
                                                 bounds_check=NP - 1, oob_is_err=True).then_inc(s_g[b], 16)
                            g.indirect_dma_start(rs[:, b, j, :], None, k.gs_d,
                                                 bass.IndirectOffsetOnAxis(idx[:, b, j, 1:2], 0),
                                                 bounds_check=NP - 1, oob_is_err=True).then_inc(s_g[b], 16)

            @block.scalar
            def _(a):
                a.wait_ge(s_own, 1)
                a.activation(own[:, :, 0:4], own[:, :, 0:4], ACT.Exp).then_inc(s_ownx, 1)
                with a.Fori(0, GT // (2 * B)) as i:
                    for b in range(2):
                        a.wait_ge(s_e, i * 2 + b + 1)
                        a.activation(f[:, b, :, 0:4], ev[:, b, :, :], ACT.Exp).then_inc(s_ex, 1)
                a.wait_ge(s_var, 1)
                a.activation(v1[:, :], v1[:, :], ACT.Sqrt, bias=k.eps[:, 0:1]).then_inc(s_std, 1)

            @block.tensor
            def _(pe):
                pe.wait_ge(s_first, 1)
                pe.matmul(pa[:, 0:C], zero[:, 0:P], zero[:, :], start=True, stop=False, skip_group_check=True)
                with pe.Fori(0, GT // (2 * B)) as i:
                    for b in range(2):
                        for j in range(B):
                            pe.wait_ge(s_hot, (i * 2 + b) * B + j + 1)
                            pe.matmul(pa[:, 0:C], lo[:, b, j, :], wide[:, j % 2, :], start=False, stop=False,
                                      skip_group_check=True).then_inc(s_mm, 1)
                pe.matmul(pa[:, 0:C], zero[:, 0:P], zero[:, :], start=False, stop=True,
                          skip_group_check=True).then_inc(s_mm, 1)

            @block.vector
            def _(e):
                e.memset(zero[:, :], 0.0).then_inc(s_v, 1)
                e.tensor_copy(idx[:, :, :, :], k.gpair[:, 0:2 * B, :].rearrange("p (a b) f -> p a b f", a=2)
                              ).then_inc(s_v, 1)
                done = Chain(e, s_v, start=2)
                done.sync()
                e.sem_inc(s_first, 1)
                e.sem_inc(s_idx, 2)
                e.sem_inc(s_mm, 2 * B)
                done(e.tensor_tensor(own[:, :, 0:4], gs[:, :, 0:4], gd[:, :, 0:4], ALU.add))
                leaky(e, done, own[:, :, 0:4], own[:, :, 0:4])
                done(e.tensor_tensor(own[:, :, 0:4], own[:, :, 0:4], gd[:, :, 4:8], ALU.subtract))
                e.sem_inc(s_own, 1)
                e.wait_ge(s_ownx, 1)
                for x in range(4):
                    done(e.tensor_tensor(own[:, :, 4 + x:20:4], gs[:, :, 4 + x:20:4], own[:, :, 0:4], ALU.mult))
                base = done.n
                with e.Fori(0, GT // (2 * B)) as i:
                    per = 2 * 9
                    loop = Chain(e, s_v, base=i * per + base)
                    for b in range(2):
                        T0 = (i * 2 + b) * B
                        e.wait_ge(s_g[b], i * (32 * B) + 32 * B)
                        loop(e.tensor_tensor(ev[:, b, :, :], rs[:, b, :, 0:4], rd[:, b, :, 0:4], ALU.add))
                        leaky(e, loop, ev[:, b, :, :], ev[:, b, :, :])
                        loop(e.tensor_tensor(ev[:, b, :, :], ev[:, b, :, :], rd[:, b, :, 4:8], ALU.subtract))
                        e.sem_inc(s_e, 1)
                        e.wait_ge(s_mm, T0 + B)
                        loop(e.tensor_tensor(lo[:, b, :, :], bc(k.iota[:, :].unsqueeze(1), (P, B, P)),
                                             bc(k.glo[:, bass.ds(T0, B)].unsqueeze(2), (P, B, P)), ALU.is_equal))
                        loop(e.tensor_tensor(hi[:, b, :, :], bc(k.iota[:, 0:NT].unsqueeze(1), (P, B, NT)),
                                             bc(k.ghi[:, bass.ds(T0, B)].unsqueeze(2), (P, B, NT)), ALU.is_equal))
                        e.wait_ge(s_ex, i * 2 + b + 1)
                        for x in range(4):
                            loop(e.tensor_tensor(f[:, b, :, 4 + x:20:4], rs[:, b, :, 4 + x:20:4], f[:, b, :, 0:4],
                                                 ALU.mult))
                        e.tensor_copy(idx[:, b, :, :], k.gpair[:, bass.ds(T0 + 2 * B, B), :]).then_inc(s_idx, 1)
                        for j in range(B):
                            e.wait_ge(s_mm, T0 + j + 2 * B - 1)
                            e.tensor_tensor(wide[:, j % 2, :].rearrange("p (n f) -> p n f", n=NT),
                                            bc(hi[:, b, j, :].unsqueeze(2), (P, NT, 20)),
                                            bc(f[:, b, j:j + 1, :], (P, NT, 20)), ALU.mult).then_inc(s_hot, 1)
                    assert loop.n == per, loop.n
                done = Chain(e, s_v, start=base + per * (GT // (2 * B)))
                e.wait_ge(s_mm, GT + 2 * B + 1)
                done(e.tensor_tensor(agg[:, :, :], pa[:, 0:C].rearrange("p (n f) -> p n f", n=NT), own[:, :, :], ALU.add))
                done(e.tensor_scalar(own[:, :, 0:4], agg[:, :, 0:4], 1e-16, None, ALU.add))
                done(e.reciprocal(own[:, :, 0:4], own[:, :, 0:4]))
                for x in range(4):
                    done(e.tensor_tensor(nrm[:, :, x::4], agg[:, :, 4 + x:20:4], own[:, :, 0:4], ALU.mult))
                e.wait_ge(s_w, 48)
                done(e.tensor_tensor(nrm[:, :, :], nrm[:, :, :], bc(par[:, 0:1, :], (P, NT, 16)), ALU.add))
                done(e.tensor_reduce(m1[:, :], nrm[:, :, :], AX, ALU.add))
                done(e.tensor_scalar(m1[:, :], m1[:, :], 1.0 / 16, None, ALU.mult))
                done(e.tensor_tensor(nrm[:, :, :], nrm[:, :, :], bc(m1[:, :].unsqueeze(2), (P, NT, 16)), ALU.subtract))
                done(e.tensor_tensor(sq[:, :, :], nrm[:, :, :], nrm[:, :, :], ALU.mult))
                done(e.tensor_reduce(v1[:, :], sq[:, :, :], AX, ALU.add))
                done(e.tensor_scalar(v1[:, :], v1[:, :], 1.0 / 16, None, ALU.mult))
                e.sem_inc(s_var, 1)
                e.wait_ge(s_std, 1)
                done(e.reciprocal(v1[:, :], v1[:, :]))
                done(e.tensor_tensor(nrm[:, :, :], nrm[:, :, :], bc(v1[:, :].unsqueeze(2), (P, NT, 16)), ALU.mult))
                done(e.tensor_tensor(nrm[:, :, :], nrm[:, :, :], bc(par[:, 1:2, :], (P, NT, 16)), ALU.mult))
                done(e.tensor_tensor(nrm[:, :, :], nrm[:, :, :], bc(par[:, 2:3, :], (P, NT, 16)), ALU.add))
                done(e.tensor_reduce(score[:, :, :], nrm[:, :, :].rearrange("p t (h x) -> p t x h", x=4), AX, ALU.add))
                done(e.tensor_scalar(score[:, :, :], score[:, :, :], 0.25, None, ALU.mult))


def store_x(k, to):
    nc = k.nc
    s_o = k.sem("stored")
    with k.block() as block:

        @block.sync
        def _(sp):
            sp.dma_start(to[0:(NT - 1) * P, :].rearrange("(t p) d -> p t d", p=P), k.x[:, 0:NT - 1, :]).then_inc(s_o, 16)
            sp.dma_start(to[(NT - 1) * P:, :], k.x[0:to.shape[0] - (NT - 1) * P, NT - 1, :]).then_inc(s_o, 16)
            sp.wait_ge(s_o, 32)


def build(nc, io, out, dumps=None, upto=99):
    with ExitStack() as ctx:
        k = Kernel(nc, io, out, ctx, dumps)
        setup(k)
        structure(k)
        for layer in range(2):
            ln_stats(k, k.x)
            with ExitStack() as c:
                ex = k.sb(c, "ex", [P, SP_, H])
                with ExitStack() as c2:
                    score = k.sb(c2, "score", [P, ETP, H])
                    with ExitStack() as c3:
                        qres = k.sb(c3, "qres", [P, NT, D])
                        if layer == 0:
                            project0(k, qres)
                            edge_scores(k, score, qres, k.step_src, k.k_d, NP, 8)
                            vargs, scale = (k.v_d, k.step_src, NP, 8), 32 ** -0.5
                        else:
                            project1(k, qres)
                            edge_scores(k, score, qres, k.step_rel, k.kr_d, NP * 8, 4)
                            vargs, scale = (k.vr_d, k.step_rel, NP * 8, 4), 1.0
                    softmax_numerators(k, score, ex, scale)
                acc = k.sb(c, "acc", [P, NT, D + H])
                edge_messages(k, ex, acc, *vargs)
                (finish0, finish1)[layer](k, acc)
            if dumps:
                store_x(k, dumps[2 * layer])
            if upto <= 2 * layer + 1:
                return
            with ExitStack() as c:
                E, R = ((8, 8), (4, 16))[layer]
                gate = k.sb(c, "gate", [P, NT, E])
                ln_stats(k, k.x)
                xnt = k.sb(c, "xnt", [P, 2, NP])
                with ExitStack() as c2:
                    router = k.sb(c2, "router", [P, NT, R])
                    if layer == 0:
                        with ExitStack() as c3:
                            xn = k.sb(c3, "xn", [P, NT, D])
                            normalize(k, k.x, xn)
                            ln_stats(k, xn)
                            columns(k, xn, xnt, router, "Wr", R, ("gamma", "beta"))
                        top2_gates(k, router, gate, E, "br")
                    else:
                        columns(k, k.x, xnt, router, "W_gat", R, None)
                        gs = k.sb(c2, "gs", [P, NT, 20])
                        gd = k.sb(c2, "gd", [P, NT, 8])
                        score = k.sb(c2, "score", [P, NT, E])
                        gate_tables(k, router, gs, gd)
                        gate_sums(k, gs, gd, score)
                        top2_gates(k, score, gate, E)
                experts(k, xnt, gate, E, [f"{x}_{layer}" for x in ("W1", "b1", "W2", "b2")],
                        mask=layer == 0)
            if dumps:
                store_x(k, dumps[2 * layer + 1])
            if upto <= 2 * layer + 2:
                return
        store_x(k, out)


def kernel(x, src, dst, edge_type_8, node_type_4, L0_gnn_W_qkv, L0_gnn_b_qkv, L0_gnn_W_out, L0_gnn_b_out,
           L0_ffn_gamma, L0_ffn_beta, L0_ffn_Wr, L0_ffn_br, L0_ffn_W1, L0_ffn_b1, L0_ffn_W2, L0_ffn_b2,
           L1_gnn_k_linears, L1_gnn_q_linears, L1_gnn_v_linears, L1_gnn_a_linears, L1_gnn_relation_att,
           L1_gnn_relation_msg, L1_gnn_relation_pri, L1_gnn_skip, L1_ffn_W_gat, L1_ffn_att_src, L1_ffn_att_dst,
           L1_ffn_b_gat, L1_ffn_ln_gamma, L1_ffn_ln_beta, L1_ffn_W1, L1_ffn_b1, L1_ffn_W2, L1_ffn_b2,
           L1_ffn_edge_index, _dump=False, _upto=99):
    import concourse.bacc as bacc
    from concourse.bass_utils import run_bass_kernel_spmd

    a = np.ascontiguousarray

    def pad(v, n, fill):
        v = np.asarray(v)
        out = np.full((n,) + v.shape[1:], fill, v.dtype)
        out[:len(v)] = v
        return out

    last = NP - 1
    s, d, r = pad(src, EP, last), pad(dst, EP, last), pad(edge_type_8, EP, 0)
    g = np.asarray(L1_ffn_edge_index)

    def tiles(v, extra=0):
        v = np.asarray(v).reshape(-1, P).T
        return a(np.concatenate([v, np.zeros((P, extra), v.dtype)], 1)) if extra else a(v)

    def by_chunk(v):
        v = np.asarray(v)
        v = v.reshape(v.shape[:-1] + (-1, P))
        return a(np.moveaxis(v, -1, 0))

    data = {
        "x": pad(x, NP, 0), "src_rows": s.reshape(ETP, P), "rel_rows": r.reshape(ETP, P),
        "dst_rows": d.reshape(ETP, P), "dst_t": tiles(d), "dst_flat": d,
        "ntype": pad(node_type_4, NP, 0), "gsrc_t": tiles(g[0], 2 * U), "gdst_t": tiles(g[1], 2 * U),
        "W_qkv": L0_gnn_W_qkv, "b_qkv": L0_gnn_b_qkv, "W_out": L0_gnn_W_out, "b_out": L0_gnn_b_out,
        "gamma": by_chunk(L0_ffn_gamma), "beta": by_chunk(L0_ffn_beta), "Wr": L0_ffn_Wr, "br": L0_ffn_br,
        "W1_0": L0_ffn_W1, "b1_0": by_chunk(L0_ffn_b1), "W2_0": L0_ffn_W2, "b2_0": L0_ffn_b2,
        "k_linears": L1_gnn_k_linears, "q_linears": L1_gnn_q_linears, "v_linears": L1_gnn_v_linears,
        "a_linears": L1_gnn_a_linears,
        "att_t": np.transpose(np.asarray(L1_gnn_relation_att), (1, 3, 0, 2)),
        "msg": np.transpose(np.asarray(L1_gnn_relation_msg), (1, 2, 0, 3)),
        "pri": np.asarray(L1_gnn_relation_pri).reshape(-1), "skip": L1_gnn_skip, "W_gat": L1_ffn_W_gat,
        "att_src": np.asarray(L1_ffn_att_src).reshape(-1), "att_dst": np.asarray(L1_ffn_att_dst).reshape(-1),
        "b_gat": L1_ffn_b_gat, "ln_gamma": L1_ffn_ln_gamma, "ln_beta": L1_ffn_ln_beta,
        "W1_1": L1_ffn_W1, "b1_1": by_chunk(L1_ffn_b1), "W2_1": L1_ffn_W2, "b2_1": L1_ffn_b2,
    }
    nc = bacc.Bacc("TRN2", target_bir_lowering=False, num_devices=1)
    arrays, io = {}, {}
    for name, v in data.items():
        v = a(np.asarray(v))
        arrays["in_" + name] = v
        io[name] = nc.dram_tensor("in_" + name, list(v.shape), mybir.dt.from_np(v.dtype), kind="ExternalInput").ap()
    out = nc.dram_tensor("out", [N, D], F32, kind="ExternalOutput").ap()
    if _dump:
        dumps = [nc.dram_tensor(f"dump{i}", [N, D], F32, kind="ExternalOutput").ap() for i in range(4)]
        build(nc, io, out, dumps, _upto)
        return nc, arrays
    build(nc, io, out)
    res = run_bass_kernel_spmd(nc, [arrays], core_ids=[0])
    return res.results[0]["out"]
```

```python
from contextlib import ExitStack, contextmanager

import numpy as np

import concourse.bass as bass
from concourse import mybir

P = 128
N, D = 3125, 256
NT = 25
NP = NT * P
GROUP = 5
E0 = 50000
ET = 392
ETP = 400
EP = ETP * P
CH, CG = 16, 25
STEPS = ET + NT - 1
SP_ = 512
U = 16
Q = 4
S = U // Q
M = 8
LAG = 8
GE = 32768
GT = GE // P
EARLY_MARKS = 16
H = 8
BIG = 1.0e30
LN_EPS = 1e-5

ALU = mybir.AluOpType
ACT = mybir.ActivationFunctionType
AX = mybir.AxisListType.X
F32, I32, BF = mybir.dt.float32, mybir.dt.int32, mybir.dt.bfloat16


class Chain:

    def __init__(self, eng, sem, start=0, base=None):
        self.eng, self.sem, self.n, self.base = eng, sem, start, base

    def mark(self, ins):
        ins.then_inc(self.sem, 1)
        self.n += 1

    def sync(self):
        self.eng.wait_ge(self.sem, self.n if self.base is None else self.base + self.n)

    def __call__(self, ins):
        self.mark(ins)
        self.sync()


class Kernel:

    def __init__(self, nc, io, ctx):
        self.nc, self.io, self.ctx = nc, io, ctx
        self.nsem = 0
        self.sems = []

    def sem(self, name):
        self.nsem += 1
        self.sems.append(self.nc.alloc_semaphore(name=f"{name}_{self.nsem}"))
        return self.sems[-1]

    @contextmanager
    def block(self):
        with self.nc.Block() as block:
            yield block
        self.nc.clear_and_free_semaphores(self.sems)
        self.nc.all_engine_barrier()
        self.sems = []

    def sb(self, ctx, name, shape, dt=F32):
        self.nsem += 1
        return ctx.enter_context(self.nc.sbuf_tensor(f"{name}_{self.nsem}", shape, dt))

    def ps(self, ctx, name, shape=(P, 512), dt=F32):
        self.nsem += 1
        return ctx.enter_context(self.nc.psum_tensor(f"{name}_{self.nsem}", list(shape), dt))

    def dram(self, name, shape, dt=F32):
        return self.nc.dram_tensor(name, shape, dt, kind="Internal").ap()


def bc(ap, shape):
    return ap.to_broadcast(list(shape))


def row_bc(ap, parts):
    return ap.partition_broadcast(parts)


def setup(k):
    nc, ctx, io = k.nc, k.ctx, k.io
    k.x = k.sb(ctx, "x", [P, NT, D])
    k.ident = k.sb(ctx, "ident", [P, P])
    k.iota = k.sb(ctx, "iota", [P, P])
    k.pcol = k.sb(ctx, "pcol", [P, 1])
    k.gpair = k.sb(ctx, "gpair", [P, GT + 16, 2], I32)
    k.mask_pos = k.sb(ctx, "mask_pos", [P, GT], I32)
    k.glo = k.sb(ctx, "glo", [P, GT])
    k.ghi = k.sb(ctx, "ghi", [P, GT])
    k.mean = k.sb(ctx, "mean", [P, NT])
    k.rstd = k.sb(ctx, "rstd", [P, NT])
    k.shift = k.sb(ctx, "shift", [P, NT])
    k.stats = k.sb(ctx, "stats", [P, NT, 6])
    k.tmp1 = k.sb(ctx, "tmp1", [P, NT])
    k.tmp2 = k.sb(ctx, "tmp2", [P, NT])
    k.eps = k.sb(ctx, "eps", [P, 1])
    k.one = k.sb(ctx, "one", [P, 1])

    k.loc_d = k.dram("loc_d", [SP_, P])
    k.k_d = k.dram("k_d", [NP, D])
    k.v_d = k.dram("v_d", [NP, D])
    k.kr_d = k.dram("kr_d", [NP * 8, D])
    k.vr_d = k.dram("vr_d", [NP * 8, D])
    k.rec_d = k.dram("rec_d", [ETP, 3 * P])
    k.ex_d = k.dram("ex_d", [ETP, H * P])
    k.ends_d = k.dram("ends_d", [P, 4])
    k.full_d = k.dram("full_d", [8, 32])
    k.mask_d = k.dram("mask_d", [NP * NP, 1], BF)
    k.asrc_d = k.dram("asrc_d", [4, NP])
    k.gs_d = k.dram("gs_d", [NP, 20])
    k.gd_d = k.dram("gd_d", [NP, 8])
    k.y_d = k.dram("y_d", [NP, 4, D])


def graph_tables(k, ctx):
    k.step_src = k.sb(ctx, "step_src", [P, SP_], I32)
    k.step_rel = k.sb(ctx, "step_rel", [P, SP_], I32)
    k.step_neg = k.sb(ctx, "step_neg", [P, SP_])
    k.step_tile = k.sb(ctx, "step_tile", [P, 4], I32)
    k.step_block = k.sb(ctx, "step_block", [1, LAG + SP_], I32)
    k.step_etile = k.sb(ctx, "step_etile", [1, LAG + SP_], I32)
    k.ntype = k.sb(ctx, "ntype", [P, NP])


def structure(k, wqkv):
    nc, io = k.nc, k.io
    with ExitStack() as c:
        rows = k.sb(c, "rows", [100, 3, 4, P], I32)
        rec = k.sb(c, "rec", [100, 4, 3, P])
        locr = k.sb(c, "locr", [P, 4, P])
        brow = k.sb(c, "brow", [1, SP_])
        dst0 = k.sb(c, "dst0", [P, ETP], I32)
        gsrc = k.sb(c, "gsrc", [P, GT + 16], I32)
        gdst = k.sb(c, "gdst", [P, GT + 16], I32)
        dstf = k.sb(c, "dstf", [P, ETP])
        low = k.sb(c, "low", [P, NT - 1])
        sum_i = k.sb(c, "sum_i", [NT - 1, 2], I32)
        first = k.sb(c, "first", [NT - 1, 2])
        begun = k.sb(c, "begun", [NT - 1, SP_])
        ones = k.sb(c, "ones", [P, P])
        scr = k.sb(c, "scr", [P, ETP])
        sidx = k.sb(c, "sidx", [P, SP_ + 4])
        blk = k.sb(c, "blk", [P, SP_ + 4])
        got = k.sb(c, "got", [P, 4, 3 * P])
        nt_i = k.sb(c, "nt_i", [P, NP], I32)
        gd_f = k.sb(c, "gd_f", [P, GT])
        gs_f = k.sb(c, "gs_f", [P, GT])
        lo_i = k.sb(c, "lo_i", [P, GT], I32)
        pc = k.ps(c, "pc")
        pt = [k.ps(c, f"pt{i}") for i in range(4)]
        s_load, s_gload, s_const, s_v, s_cnt, s_rec, s_recd = [k.sem(x) for x in
            ("loaded", "gate_loaded", "const_done", "dve", "counts_summed", "rec_ready", "rec_stored")]
        s_bn, s_wqkv = k.sem("statistics"), k.sem("w_loaded")
        s_step, s_got, s_tr, s_loc, s_locd = [k.sem(x) for x in ("steps_ready", "got", "turned", "loc_ready", "loc_stored")]
        with k.block() as block:

            @block.sync
            def _(sp):
                for j, name in enumerate(("src_rows", "rel_rows", "dst_rows")):
                    sp.dma_start(rows[:, j, :, :], io[name].rearrange("(p c) e -> p c e", c=4)).then_inc(s_load, 16)
                sp.dma_start(dst0[:, :], io["dst_t"]).then_inc(s_load, 16)
                sp.dma_start(nt_i[:, :], row_bc(io["ntype"], P)).then_inc(s_load, 16)
                sp.dma_start(gsrc[:, :], io["gsrc_t"]).then_inc(s_gload, 16)
                sp.dma_start(gdst[:, :], io["gdst_t"]).then_inc(s_gload, 16)
                sp.dma_start(k.x[:, :, :], io["x"].rearrange("(t p) d -> p t d", p=P)).then_inc(s_gload, 16)
                sp.dma_start(wqkv[:, :, :], io["W_qkv"].rearrange("(c p) n -> p c n", p=P)).then_inc(s_wqkv, 16)
                sp.wait_ge(s_rec, 1)
                sp.dma_start(k.rec_d.rearrange("(p c) f -> p c f", c=4),
                             rec[:, :, :, :].rearrange("p c j e -> p c (j e)")).then_inc(s_recd, 16)
                sp.wait_ge(s_loc, 1)
                sp.dma_start(k.loc_d.rearrange("(j p) e -> p j e", p=P), locr[:, :, :]).then_inc(s_locd, 16)
                sp.wait_ge(s_locd, 16)
                sp.wait_ge(s_wqkv, 16)

            @block.gpsimd
            def _(g):
                g.memset(k.ident[:, :], 0.0).then_inc(s_const, 1)
                g.wait_ge(s_const, 1)
                g.affine_select(out=k.ident[:, :], in_=k.ident[:, :], compare_op=ALU.not_equal, fill=1.0,
                                base=0, pattern=[[-1, P]], channel_multiplier=1).then_inc(s_const, 1)
                g.iota(k.iota[:, :], [[1, P]], base=0, channel_multiplier=0,
                       allow_small_or_imprecise_dtypes=True).then_inc(s_const, 1)
                g.iota(k.pcol[:, :], [[1, 1]], base=0, channel_multiplier=1,
                       allow_small_or_imprecise_dtypes=True).then_inc(s_const, 1)
                g.iota(sidx[:, 0:SP_], [[1, SP_]], base=0, channel_multiplier=0,
                       allow_small_or_imprecise_dtypes=True).then_inc(s_const, 1)
                g.iota(sidx[:, SP_:], [[P, 4]], base=0, channel_multiplier=1,
                       allow_small_or_imprecise_dtypes=True).then_inc(s_const, 1)
                g.wait_ge(s_step, 1)
                g.wait_ge(s_recd, 16)
                for j in range(4):
                    g.indirect_dma_start(got[:, j, :], None, k.rec_d,
                                         bass.IndirectOffsetOnAxis(k.step_tile[:, j:j + 1], 0),
                                         bounds_check=ETP - 1, oob_is_err=True).then_inc(s_got, 16)

            @block.vector
            def _(e):
                done = Chain(e, s_v)
                done(e.memset(ones[:, :], 1.0))
                done(e.memset(k.eps[:, :], LN_EPS))
                done(e.memset(k.one[:, :], 1.0))
                e.wait_ge(s_load, 16 * 5)
                done(e.tensor_copy(rec[:, :, 0, :], rows[:, 0, :, :]))
                done(e.tensor_copy(rec[:, :, 2, :], rows[:, 2, :, :]))
                done(e.scalar_tensor_tensor(rec[:, :, 1, :], rec[:, :, 0, :], 8.0, rows[:, 1, :, :],
                                            ALU.mult, ALU.add))
                e.sem_inc(s_rec, 1)
                done(e.tensor_copy(k.ntype[:, :], nt_i[:, :]))
                done(e.tensor_copy(dstf[:, :], dst0[:, :]))
                for b in range(NT - 1):
                    done(e.tensor_scalar(scr[:, 0:ET], dstf[:, 0:ET], float(P * (b + 1)), 0.0, ALU.is_lt, ALU.add,
                                         accum_out=low[:, b:b + 1]))
                e.sem_inc(s_cnt, 1)
                e.wait_ge(s_tr, 1)
                done(e.tensor_copy(sum_i[:, 0:1], pc[0:NT - 1, 0:1]))
                done(e.tensor_scalar(sum_i[:, 1:2], sum_i[:, 0:1], P - 1, None, ALU.bitwise_and))
                done(e.tensor_copy(first[:, :], sum_i[:, :]))
                done(e.tensor_tensor(first[:, 0:1], first[:, 0:1], first[:, 1:2], ALU.subtract))
                done(e.tensor_scalar(first[:, 0:1], first[:, 0:1], 1.0 / P, 1.0, ALU.mult, ALU.add))
                done(e.tensor_scalar(first[:, 0:1], first[:, 0:1], float(ET), None, ALU.min))
                e.wait_ge(s_const, 6)
                done(e.tensor_tensor(first[:, 0:1], first[:, 0:1], k.pcol[0:NT - 1, :], ALU.add))
                done(e.tensor_scalar(begun[:, :], sidx[0:NT - 1, 0:SP_], first[:, 0:1], None, ALU.is_ge))
                e.sem_inc(s_cnt, 1)
                e.wait_ge(s_tr, 2)
                done(e.tensor_copy(blk[:, 0:SP_], pt[0][:, :]))
                done(e.tensor_copy(blk[:, SP_:], pc[:, 8:12]))
                done(e.memset(k.step_block[:, :], 0))
                done(e.memset(k.step_etile[:, :], 0))
                done(e.tensor_copy(k.step_block[:, LAG:], blk[0:1, 0:SP_]))
                done(e.tensor_tensor(brow[:, :], sidx[0:1, 0:SP_], blk[0:1, 0:SP_], ALU.subtract))
                done(e.tensor_copy(k.step_etile[:, LAG:], brow[:, :]))
                done(e.tensor_tensor(sidx[:, SP_:], sidx[:, SP_:], blk[:, SP_:], ALU.subtract))
                done(e.tensor_scalar(sidx[:, SP_:], sidx[:, SP_:], float(ETP - 1), None, ALU.min))
                done(e.tensor_copy(k.step_tile[:, :], sidx[:, SP_:]))
                e.sem_inc(s_step, 1)
                e.wait_ge(s_gload, 16 * 3)
                with e.Fori(0, NT // GROUP) as i:
                    for j in range(GROUP):
                        row_stats(k, e, i * GROUP + j, s_bn)
                e.wait_ge(s_bn, NT)
                e.wait_ge(s_got, 64)
                for j in range(4):
                    done(e.scalar_tensor_tensor(locr[:, j, :], bc(blk[:, SP_ + j:SP_ + j + 1], (P, P)), -float(P),
                                                got[:, j, 2 * P:3 * P], ALU.mult, ALU.add))
                e.sem_inc(s_loc, 1)
                for j in range(4):
                    e.wait_ge(s_tr, 3 + j)
                    cols = slice(P * j, P * j + P)
                    done(e.tensor_copy(k.step_src[:, cols], pt[j][:, 0:P]))
                    done(e.tensor_copy(k.step_rel[:, cols], pt[j][:, P:2 * P]))
                    done(e.scalar_tensor_tensor(k.step_neg[:, cols], blk[:, cols], float(P), pt[j][:, 2 * P:3 * P],
                                                ALU.mult, ALU.subtract))
                done(e.tensor_copy(k.gpair[:, :, 0], gdst[:, :]))
                done(e.tensor_copy(k.gpair[:, :, 1], gsrc[:, :]))
                done(e.tensor_scalar(lo_i[:, :], gdst[:, 0:GT], P - 1, None, ALU.bitwise_and))
                done(e.tensor_copy(k.glo[:, :], lo_i[:, :]))
                done(e.tensor_copy(gd_f[:, :], gdst[:, 0:GT]))
                done(e.tensor_tensor(k.ghi[:, :], gd_f[:, :], k.glo[:, :], ALU.subtract))
                done(e.tensor_scalar(k.ghi[:, :], k.ghi[:, :], 1.0 / P, None, ALU.mult))
                done(e.tensor_copy(gs_f[:, :], gsrc[:, 0:GT]))
                done(e.scalar_tensor_tensor(k.mask_pos[:, :], gd_f[:, :], float(NP), gs_f[:, :], ALU.mult, ALU.add))

            @block.tensor
            def _(pe):
                pe.wait_ge(s_cnt, 1)
                pe.matmul(pc[0:NT - 1, 0:1], low[:, :], ones[:, 0:1], start=True, stop=True).then_inc(s_tr, 1)
                pe.wait_ge(s_cnt, 2)
                pe.matmul(pt[0][:, :], ones[0:NT - 1, :], begun[:, 0:SP_], start=True, stop=True)
                for j in range(4):
                    ins = pe.matmul(pc[:, 8 + j:9 + j], begun[:, j * P:(j + 1) * P], ones[0:NT - 1, 0:1], start=True,
                                    stop=True)
                ins.then_inc(s_tr, 1)
                pe.wait_ge(s_const, 2)
                pe.wait_ge(s_got, 64)
                for j in range(4):
                    for r in range(3):
                        ins = pe.transpose(pt[j][:, r * P:(r + 1) * P], got[:, j, r * P:(r + 1) * P], k.ident[:, :])
                    ins.then_inc(s_tr, 1)


def row_stats(k, e, t, done):
    e.bn_stats(k.stats[:, bass.ds(t, 1), :].rearrange("p a b -> p (a b)"), tile_of(k.x, t)).then_inc(done, 1)


def ln_scales(k, twice=False):
    nc = k.nc
    s_v, s_var, s_std = k.sem("ln_dve"), k.sem("ln_var"), k.sem("ln_std")
    with k.block() as block:

        @block.vector
        def _(e):
            done = Chain(e, s_v)
            me, mo = k.stats[:, :, 1], k.stats[:, :, 4]
            ve, vo = k.stats[:, :, 2], k.stats[:, :, 5]
            done(e.tensor_tensor(k.mean[:, :], me, mo, ALU.add))
            done(e.tensor_scalar(k.mean[:, :], k.mean[:, :], 0.5, None, ALU.mult))
            done(e.tensor_tensor(k.tmp1[:, :], me, mo, ALU.subtract))
            done(e.tensor_tensor(k.tmp1[:, :], k.tmp1[:, :], k.tmp1[:, :], ALU.mult))
            done(e.tensor_tensor(k.tmp2[:, :], ve, vo, ALU.add))
            done(e.tensor_scalar(k.tmp2[:, :], k.tmp2[:, :], 1.0 / D, None, ALU.mult))
            done(e.scalar_tensor_tensor(k.tmp1[:, :], k.tmp1[:, :], 0.25, k.tmp2[:, :], ALU.mult, ALU.add))
            e.sem_inc(s_var, 1)
            e.wait_ge(s_std, 1)
            done(e.reciprocal(k.rstd[:, :], k.tmp2[:, :]))
            done(e.scalar_tensor_tensor(k.shift[:, :], k.mean[:, :], -1.0, k.rstd[:, :], ALU.mult, ALU.mult))
            if twice:
                done(e.tensor_tensor(k.tmp1[:, :], k.tmp1[:, :], k.rstd[:, :], ALU.mult))
                done(e.tensor_tensor(k.tmp1[:, :], k.tmp1[:, :], k.rstd[:, :], ALU.mult))
                e.sem_inc(s_var, 1)
                e.wait_ge(s_std, 2)
                done(e.reciprocal(k.tmp2[:, :], k.tmp2[:, :]))
                done(e.tensor_tensor(k.rstd[:, :], k.rstd[:, :], k.tmp2[:, :], ALU.mult))

        @block.scalar
        def _(a):
            for n in range(1 + twice):
                a.wait_ge(s_var, n + 1)
                a.activation(k.tmp2[:, :], k.tmp1[:, :], ACT.Sqrt, bias=k.eps[:, 0:1]).then_inc(s_std, 1)


def tile_of(t3, t, n=1):
    return t3[:, bass.ds(t, n), :].rearrange("p a b -> p (a b)")


def held(j):
    return 0 if j == 0 else 1


def project0(k, qres, w):
    nc, io = k.nc, k.io
    with ExitStack() as c:
        b = k.sb(c, "bqkv", [P, 3 * D])
        xn = k.sb(c, "xn", [P, GROUP, D])
        xt = k.sb(c, "xt", [P, GROUP, 2, P])
        stage = k.sb(c, "stage", [P, GROUP, 2 * D])
        pt = [k.ps(c, f"pt{i}") for i in range(2)]
        pa = [k.ps(c, f"pa{i}") for i in range(2)]
        pb = [k.ps(c, f"pb{i}") for i in range(2)]
        s_w, s_xn, s_tr, s_xt, s_mm, s_out = [k.sem(x) for x in
            ("w_loaded", "xn_ready", "turned", "xt_ready", "qkv_ready", "staged")]
        s_sto = [k.sem(f"stored{j}") for j in range(GROUP)]
        dst = [x.rearrange("(t p) d -> p t d", p=P) for x in (k.k_d, k.v_d)]
        with k.block() as block:

            @block.sync
            def _(sp):
                sp.dma_start(b[:, :], row_bc(io["b_qkv"], P)).then_inc(s_w, 16)
                with sp.Fori(0, NT // GROUP) as i:
                    for j in range(GROUP):
                        sp.wait_ge(s_out, i * GROUP + j + 1)
                        for n in range(2):
                            sp.dma_start(dst[n][:, bass.ds(i * GROUP + j, 1), :].rearrange("p a b -> p (a b)"),
                                         stage[:, j, n * D:(n + 1) * D]).then_inc(s_sto[j], 16)
                for j in range(GROUP):
                    sp.wait_ge(s_sto[j], 32 * (NT // GROUP))

            @block.vector
            def _(e):
                def norm(t, j, first):
                    if not first:
                        e.wait_ge(s_tr, t - GROUP + 1)
                    e.tensor_scalar(xn[:, j, :], tile_of(k.x, t), k.mean[:, bass.ds(t, 1)],
                                    k.rstd[:, bass.ds(t, 1)], ALU.subtract, ALU.mult).then_inc(s_xn, 1)

                def emit(i, j, first):
                    t = i * GROUP + j
                    if first and j == 0:
                        e.wait_ge(s_w, 16)
                    e.wait_ge(s_mm, t + 1)
                    if not first:
                        e.wait_ge(s_sto[j], i * 32)
                    e.tensor_tensor(tile_of(qres, t), pb[j % 2][:, 0:256], b[:, 0:256], ALU.add).then_inc(s_va, 1)
                    e.wait_ge(s_va, t + 1)
                    e.tensor_tensor(stage[:, j, :], pa[j % 2][:, :], b[:, 256:768], ALU.add).then_inc(s_out, 1)

                s_va = k.sem("first_half")

                def turn(i, first, last):
                    for j in range(GROUP):
                        if not last or j + 3 < GROUP:
                            norm(i * GROUP + j + 3, (j + 3) % GROUP, first and j + 3 < GROUP)
                        emit(i, j, first)
                for j in range(3):
                    norm(j, j, True)
                turn(0, True, False)
                with e.Fori(1, NT // GROUP - 1) as i:
                    turn(i, False, False)
                turn(NT // GROUP - 1, False, True)

            @block.scalar
            def _(a):
                def turn(i, first):
                    for j in range(GROUP):
                        t = i * GROUP + j
                        a.wait_ge(s_tr, t + 1)
                        if not first:
                            a.wait_ge(s_mm, t - GROUP + 1)
                        a.activation(xt[:, j, :, :], pt[j % 2][:, 0:256].rearrange("p (c n) -> p c n", c=2),
                                     ACT.Copy).then_inc(s_xt, 1)
                turn(0, True)
                with a.Fori(1, NT // GROUP) as i:
                    turn(i, False)

            @block.tensor
            def _(pe):
                def turned(t, j, first):
                    pe.wait_ge(s_xn, t + 1)
                    if not first or j >= 2:
                        pe.wait_ge(s_xt, t - held(j))
                    for h in range(2):
                        ins = pe.transpose(pt[j % 2][:, h * P:(h + 1) * P], xn[:, j, h * P:(h + 1) * P],
                                           k.ident[:, :])
                    ins.then_inc(s_tr, 1)

                def turn(i, first, last):
                    for j in range(GROUP):
                        t = i * GROUP + j
                        if not last or j + 1 < GROUP:
                            turned(t + 1, (j + 1) % GROUP, first and j + 1 < GROUP)
                        pe.wait_ge(s_xt, t + 1)
                        if not first or j >= 2:
                            pe.wait_ge(s_out, t - held(j))
                        for out, lo, hi in ((pb[j % 2][:, 0:256], 0, 256), (pa[j % 2][:, :], 256, 768)):
                            for h in range(2):
                                ins = pe.matmul(out, xt[:, j, h, :], w[:, h, lo:hi], start=(h == 0), stop=(h == 1))
                        ins.then_inc(s_mm, 1)
                turned(0, 0, True)
                turn(0, True, False)
                with pe.Fori(1, NT // GROUP - 1) as i:
                    turn(i, False, False)
                turn(NT // GROUP - 1, False, True)


def registers(k, eng, table, first, name):
    k.nsem += 1
    regs = [eng.alloc_register(f"{name}{k.nsem}_{j}") for j in range(U)]

    def load(at):
        k.nc.reg_load(regs, table[0:1, bass.ds(at, U)])
        return [eng.snap(r, min_val=0, max_val=first) for r in regs]
    return load


def edge_scores(k, score, qres, idx_all, k_d, k_rows, heads):
    nc = k.nc
    TURNS = STEPS // U
    with ExitStack() as c:
        loc = k.sb(c, "loc", [P, 2, Q * P])
        hot = k.sb(c, "hot", [P, 2, Q * P])
        kv = k.sb(c, "kv", [P, S, Q, D])
        prod = k.sb(c, "prod", [P, 2, Q * D])
        part = k.sb(c, "part", [P, 2, Q, heads])
        idx = k.sb(c, "idx", [P, S, Q], I32)
        pq = [k.ps(c, f"pq{i}", [P, Q * D]) for i in range(2)]
        s_first, s_idx, s_hot, s_q, s_prod, s_part, s_add, s_let = [k.sem(x) for x in
            ("score_first", "idx_ready", "hot_ready", "q_picked", "product", "part_ready", "added", "fetch_let")]
        s_g = [k.sem(f"rows_in{b}") for b in range(S)]
        s_l = [k.sem(f"loc_in{b}") for b in range(2)]
        with k.block() as block:

            @block.gpsimd
            def _(g):
                with g.Fori(0, TURNS) as i:
                    for b in range(S):
                        g.wait_ge(s_idx, i * S + b + 1)
                        g.sem_inc(s_let, 1)
                        for r in range(Q):
                            g.indirect_dma_start(kv[:, b, r, :], None, k_d,
                                                 bass.IndirectOffsetOnAxis(idx[:, b, r:r + 1], 0),
                                                 bounds_check=k_rows - 1, oob_is_err=True).then_inc(s_g[b], 16)

            @block.sync
            def _(sp):
                def fetch(n, b):
                    sp.dma_start(loc[:, b, :], row_bc(k.loc_d.rearrange("s e -> (s e)")[bass.ds(n * (Q * P), Q * P)], P)
                                 ).then_inc(s_l[b], 16)
                for b in range(2):
                    fetch(b, b)
                with sp.Fori(1, STEPS // (2 * Q)) as i:
                    for b in range(2):
                        sp.wait_ge(s_hot, i * 2 + b - 1)
                        fetch(i * 2 + b, b)

            @block.tensor
            def _(pe):
                load = registers(k, pe, k.step_block, NT - 1, "node")
                with pe.Fori(0, TURNS) as i:
                    node = load(i * U + LAG)
                    for j in range(S):
                        n, b = i * S + j, j % 2
                        pe.wait_ge(s_hot, n + 1)
                        pe.wait_ge(s_prod, n + 1)
                        for r in range(Q):
                            ins = pe.matmul(pq[b][:, r * D:(r + 1) * D], hot[:, b, r * P:(r + 1) * P],
                                            tile_of(qres, node[j * Q + r]), start=True, stop=True)
                        ins.then_inc(s_q, 1)

            @block.vector
            def _(e):
                e.memset(score[:, :, :], 0.0).then_inc(s_first, 1)
                e.tensor_copy(idx[:, :, :], idx_all[:, 0:U].rearrange("p (b r) -> p b r", b=S)).then_inc(s_first, 1)
                e.wait_ge(s_first, 2)
                e.sem_inc(s_idx, S)
                for x in (s_q, s_prod, s_part):
                    e.sem_inc(x, 2)
                e.sem_inc(s_add, 1)

                def pick(n, j, i):
                    b = j % 2
                    e.wait_ge(s_l[b], i * (16 * (S // 2)) + 16 * (j // 2 + 1))
                    e.wait_ge(s_q, n + 1)
                    e.tensor_scalar(hot[:, b, :], loc[:, b, :], k.pcol[:, 0:1], None, ALU.is_equal).then_inc(s_hot, 1)

                def multiply(n, j, turns):
                    b = j % 2
                    e.wait_ge(s_q, n + 3)
                    e.wait_ge(s_g[j], turns * (16 * Q))
                    e.wait_ge(s_part, n + 1)
                    e.tensor_tensor(prod[:, b, :], pq[b][:, :], kv[:, j, :, :].rearrange("p r d -> p (r d)"),
                                    ALU.mult).then_inc(s_prod, 1)

                def reduce(n, j):
                    b = j % 2
                    e.wait_ge(s_prod, n + 3)
                    e.tensor_copy(idx[:, j, :], idx_all[:, bass.ds(n * Q + S * Q, Q)]).then_inc(s_idx, 1)
                    e.tensor_reduce(part[:, b, :, :], prod[:, b, :].rearrange("p (r h d) -> p r h d", r=Q, h=heads),
                                    AX, ALU.add).then_inc(s_part, 1)

                def add(n, b, tiles):
                    e.wait_ge(s_part, n + 3)
                    for r in range(Q):
                        to = score[:, bass.ds(tiles[r], 1), 0:heads].rearrange("p a h -> p (a h)")
                        e.wait_ge(s_add, n * Q + r + 1)
                        e.tensor_tensor(to, to, part[:, b, r, :], ALU.add).then_inc(s_add, 1)

                def turn(i, first):
                    tiles = load(i * U)
                    for j in range(S):
                        n = i * S + j
                        pick(n, j, i)
                        if not first or j >= 1:
                            multiply(n - 1, (j - 1) % S, i + (1 if j else 0))
                        if not first or j >= 2:
                            add(n - 2, j % 2, tiles[j * Q:j * Q + Q])
                        if not first or j >= 1:
                            reduce(n - 1, (j - 1) % S)
                load = registers(k, e, k.step_etile, ETP - 1, "etile")
                turn(0, True)
                with e.Fori(1, TURNS) as i:
                    turn(i, False)
                n = S * TURNS
                tiles = load(n * Q)
                multiply(n - 1, S - 1, TURNS)
                add(n - 2, 0, tiles[0:Q])
                reduce(n - 1, S - 1)
                add(n - 1, 1, tiles[Q:2 * Q])
                e.wait_ge(s_add, n * Q + 1)


def softmax_numerators(k, score, ex, acc, scale, vv, idx, v_d, v_idx, v_rows):
    nc, io = k.nc, k.io
    L = CG * P
    with ExitStack() as c:
        room = acc[:, :, :].rearrange("p t w -> p (t w)")
        sc, st = [room[:, n * L:(n + 1) * L].rearrange("p (g e) -> p g e", e=P) for n in range(2)]
        key = k.sb(c, "key", [P, L])
        st2 = st[:, :, :].rearrange("p g e -> p (g e)")
        new = k.sb(c, "new", [P, L + 1], BF)
        top = k.sb(c, "top", [P, L])
        far = k.sb(c, "far", [P, L], BF)
        ends = k.sb(c, "ends", [P, 4])
        full = k.sb(c, "full", [P, 2])
        e8 = k.sb(c, "e8", [8, CH, 4])
        m8 = k.sb(c, "m8", [8, 2 * CH])
        n8 = k.sb(c, "n8", [8, 2 * CH + 1])
        k8 = k.sb(c, "k8", [8, 2 * CH])
        got = k.sb(c, "got", [P, 4, H * P])
        pt = [k.ps(c, f"pt{i}") for i in range(7)]
        s_key, s_t, s_st, s_v, s_ends, s_e8, s_m8, s_full = [k.sem(x) for x in
            ("keys_in", "turned", "st_ready", "dve", "ends_out", "ends_in", "full_ready", "full_in")]
        s_sc = k.sem("scores_sorted")
        s_idx, s_vv = k.sem("idx_ready"), k.sem("v_rows_in")
        s_dif, s_ex, s_exd, s_got, s_b, s_bk = [k.sem(x) for x in
            ("shifted", "exp_ready", "exp_stored", "got", "step_turned", "step_kept")]
        with k.block() as block:

            @block.sync
            def _(sp):
                for h in range(H):
                    sp.dma_start(key[h * CH:(h + 1) * CH, :].bitcast(I32), io["dst_flat"].rearrange("(a f) -> a f", a=CH)
                                 ).then_inc(s_key, 16)
                sp.wait_ge(s_ends, 1)
                sp.dma_start(k.ends_d, ends[:, :]).then_inc(s_e8, 16)
                sp.wait_ge(s_e8, 16)
                sp.dma_start(e8[:, :, :], k.ends_d.rearrange("(h a) f -> h a f", a=CH)).then_inc(s_e8, 16)
                sp.wait_ge(s_m8, 1)
                sp.dma_start(k.full_d, m8[:, :]).then_inc(s_full, 16)
                sp.wait_ge(s_full, 16)
                sp.dma_start(full[:, :], k.full_d.rearrange("h (a f) -> (h a) f", f=2)).then_inc(s_full, 16)
                sp.wait_ge(s_ex, 1)
                for h in range(H):
                    sp.dma_start(k.ex_d.rearrange("(a g) (h e) -> h a g e", a=CH, h=H)[h],
                                 st[h * CH:(h + 1) * CH, :, :]).then_inc(s_exd, 16)

            @block.tensor
            def _(pe):
                pe.wait_ge(s_sc, 1)
                for g in range(CG):
                    ins = pe.transpose(pt[g // 4][:, (g % 4) * P:(g % 4 + 1) * P],
                                       sc[:, g, :], k.ident[:, :])
                    if g % 4 == 3 or g == CG - 1:
                        ins.then_inc(s_t, 1)
                pe.wait_ge(s_st, 7)
                for n in range(8):
                    j, half = n // 2, n % 2
                    pe.wait_ge(s_got, 64)
                    if n >= 7:
                        pe.wait_ge(s_bk, n - 6)
                    for h in range(4):
                        hh = half * 4 + h
                        ins = pe.transpose(pt[n % 7][:, h * P:(h + 1) * P], got[:, j, hh * P:(hh + 1) * P],
                                           k.ident[:, :])
                    ins.then_inc(s_b, 1)

            @block.gpsimd
            def _(g):
                g.wait_ge(s_idx, 1)
                for b in range(M):
                    for r in range(Q):
                        g.indirect_dma_start(vv[:, b, r, :], None, v_d,
                                             bass.IndirectOffsetOnAxis(idx[:, b, r:r + 1], 0),
                                             bounds_check=v_rows - 1, oob_is_err=True).then_inc(s_vv, 16)
                g.wait_ge(s_vv, 16 * Q * M)
                g.wait_ge(s_exd, 16 * H)
                for j in range(4):
                    g.indirect_dma_start(got[:, j, :], None, k.ex_d,
                                         bass.IndirectOffsetOnAxis(k.step_tile[:, j:j + 1], 0),
                                         bounds_check=ETP - 1, oob_is_err=True).then_inc(s_got, 16)

            @block.scalar
            def _(a):
                for g in range(7):
                    n = min(4, CG - 4 * g)
                    a.wait_ge(s_t, g + 1)
                    a.activation(st[:, 4 * g:4 * g + n, :],
                                 pt[g][:, 0:n * P].rearrange("p (g e) -> p g e", e=P), ACT.Copy).then_inc(s_st, 1)
                a.wait_ge(s_dif, 1)
                a.activation(st2, top[:, :], ACT.Exp, scale=scale).then_inc(s_ex, 1)
                for n in range(8):
                    j, half = n // 2, n % 2
                    a.wait_ge(s_b, n + 1)
                    a.activation(ex[:, j * P:(j + 1) * P, half * 4:half * 4 + 4].rearrange("p s h -> p h s"),
                                 pt[n % 7][:, :].rearrange("p (h s) -> p h s", h=4), ACT.Copy).then_inc(s_bk, 1)

            @block.vector
            def _(e):
                done = Chain(e, s_v)
                e.tensor_copy(idx[:, :, :], v_idx[:, 0:Q * M].rearrange("p (b r) -> p b r", b=M)).then_inc(s_idx, 1)
                e.wait_ge(s_idx, 1)

                def segment_max(vals, restart, out, n):
                    done(e.tensor_tensor_scan(vals[1], restart[:, 0:n], vals[0], -BIG, ALU.add, ALU.max))
                    done(e.tensor_tensor_scan(out[:, ::-1], restart[:, 1:n + 1][:, ::-1], vals[1][:, ::-1], -BIG,
                                              ALU.add, ALU.max))

                done(e.tensor_copy(sc[:, :, :].rearrange("p g (h a) -> p a g h", h=H),
                                   score[:, :, :].rearrange("p (a g) h -> p a g h", g=CG)))
                e.sem_inc(s_sc, 1)
                e.wait_ge(s_key, 16 * H)
                done(e.memset(new[:, 0:1], -BIG))
                done(e.memset(new[:, L:], -BIG))
                keyf = got[:, :, :].rearrange("p a b -> p (a b)")[:, 0:L]
                done(e.tensor_copy(keyf, key[:, :].bitcast(I32)))
                done(e.tensor_tensor(top[:, 1:L], keyf[:, 1:L], keyf[:, 0:L - 1], ALU.not_equal))
                done(e.tensor_scalar(new[:, 1:L], top[:, 1:L], -BIG, None, ALU.mult))
                e.wait_ge(s_st, 7)
                segment_max((st2, key[:, :]), new, top, L)
                done(e.tensor_copy(ends[:, 0:1], top[:, 0:1]))
                done(e.tensor_copy(ends[:, 1:2], top[:, L - 1:L]))
                done(e.tensor_copy(ends[:, 2:3], keyf[:, 0:1]))
                done(e.tensor_copy(ends[:, 3:4], keyf[:, L - 1:L]))
                e.sem_inc(s_ends, 1)
                done(e.tensor_scalar(far[:, :], keyf, keyf[:, 0:1], -BIG, ALU.not_equal, ALU.mult))
                done(e.tensor_scalar(key[:, :], keyf, keyf[:, L - 1:L], -BIG, ALU.not_equal, ALU.mult))
                e.wait_ge(s_e8, 32)
                done(e.tensor_copy(m8[:, :].rearrange("p (a f) -> p a f", f=2), e8[:, :, 0:2]))
                done(e.tensor_copy(k8[:, :].rearrange("p (a f) -> p a f", f=2), e8[:, :, 2:4]))
                done(e.memset(n8[:, :], -BIG))
                done(e.tensor_tensor(n8[:, 1:2 * CH], k8[:, 1:], k8[:, 0:2 * CH - 1], ALU.not_equal))
                done(e.tensor_scalar(n8[:, 1:2 * CH], n8[:, 1:2 * CH], -BIG, None, ALU.mult))
                segment_max((m8[:, :], k8[:, :]), n8, m8, 2 * CH)
                e.sem_inc(s_m8, 1)
                e.wait_ge(s_full, 32)
                done(e.scalar_tensor_tensor(top[:, :], far[:, :], full[:, 0:1], top[:, :], ALU.add, ALU.max))
                done(e.scalar_tensor_tensor(top[:, :], key[:, :], full[:, 1:2], top[:, :], ALU.add, ALU.max))
                e.tensor_tensor(top[:, :], st2, top[:, :], ALU.subtract).then_inc(s_dif, 1)
                e.wait_ge(s_bk, 8)


def edge_messages(k, ex, acc, vv, idx, v_d, v_idx, v_rows, heads, clear):
    nc = k.nc
    W = D + H
    TURNS = STEPS // (Q * M)
    with ExitStack() as c:
        msg = k.sb(c, "msg", [P, 2, Q, W])
        gap = k.sb(c, "gap", [P, 2, Q, P])
        pick = k.sb(c, "pick", [P, 2, Q, P])
        pm = [k.ps(c, f"pm{i}") for i in range(2 * Q)]
        s_gap, s_first, s_idx, s_msg, s_exc, s_pick, s_mm, s_acc, s_let = [k.sem(x) for x in
            ("gap_ready", "msg_first", "idx_ready", "msg_ready", "ex_ready", "pick_ready", "summed", "added", "fetch_let")]
        s_g = [k.sem(f"rows_in{b}") for b in range(M)]
        neg = k.sb(c, "neg", [P, NP // 4], BF)
        s_acc2 = k.sem("added_second_half")
        s_neg, s_cleared = k.sem("neg_ready"), k.sem("mask_cleared")
        with k.block() as block:

            if clear:
                @block.sync
                def _(sp):
                    sp.wait_ge(s_neg, 1)
                    fill = k.mask_d.rearrange("(t p n f) o -> t p n (f o)", p=P, n=4, f=NP // 4)
                    for t in range(NT):
                        if t:
                            sp.wait_ge(s_cleared, 16 * t)
                        sp.dma_start(fill[t], bc(neg[:, :].unsqueeze(1), (P, 4, NP // 4))).then_inc(s_cleared, 16)
                    sp.wait_ge(s_cleared, 16 * NT)

            @block.gpsimd
            def _(g):
                with g.Fori(0, TURNS - 1) as i:
                    for b in range(M):
                        g.wait_ge(s_idx, i * M + b + 1)
                        g.sem_inc(s_let, 1)
                        for r in range(Q):
                            g.indirect_dma_start(vv[:, b, r, :], None, v_d,
                                                 bass.IndirectOffsetOnAxis(idx[:, b, r:r + 1], 0),
                                                 bounds_check=v_rows - 1, oob_is_err=True).then_inc(s_g[b], 16)

            @block.scalar
            def _(a):
                with a.Fori(0, TURNS) as i:
                    for j in range(M):
                        n, b = i * M + j, j % 2
                        a.wait_ge(s_pick, n + 1)
                        for r in range(Q):
                            ins = a.activation(gap[:, b, r, :], k.iota[:, :], ACT.Abs,
                                               bias=k.step_neg[:, bass.ds(n * Q + r, 1)])
                        ins.then_inc(s_gap, 1)
                        a.wait_ge(s_gap, n + 1)
                        a.wait_ge(s_mm, n + 1)
                        a.activation(pick[:, b, :, :], gap[:, b, :, :], ACT.Relu, scale=-1.0, bias=k.one[:, 0:1]
                                     ).then_inc(s_pick, 1)

            @block.vector
            def _(e):
                e.memset(neg[:, :], -BIG).then_inc(s_neg, 1)
                e.sem_inc(s_mm, 2)
                e.sem_inc(s_acc, 1)
                e.sem_inc(s_acc2, 1)
                e.sem_inc(s_pick, 2)

                def make(n, j, i, first):
                    b = j % 2
                    e.wait_ge(s_mm, n + 1)
                    w = ex[:, bass.ds(n * Q, Q), :]
                    e.tensor_copy(msg[:, b, :, D:], w).then_inc(s_exc, 1)
                    if not first:
                        e.wait_ge(s_g[j], i * (16 * Q))
                    e.tensor_tensor(msg[:, b, :, 0:D].rearrange("p r (h d) -> p r h d", h=heads),
                                    vv[:, j, :, :].rearrange("p r (h d) -> p r h d", h=heads),
                                    bc(w[:, :, 0:heads].unsqueeze(3), (P, Q, heads, D // heads)),
                                    ALU.mult).then_inc(s_msg, 1)

                def next_indices(n, j):
                    e.wait_ge(s_msg, n + 1)
                    e.tensor_copy(idx[:, j, :], v_idx[:, bass.ds(n * Q + M * Q, Q)]).then_inc(s_idx, 1)

                def adds(n, b, node):
                    e.wait_ge(s_mm, n + 3)
                    for r in range(Q):
                        to = acc[:, bass.ds(node[r], 1), :].rearrange("p a w -> p (a w)")
                        for half, added in ((slice(0, W // 2), s_acc), (slice(W // 2, W), s_acc2)):
                            e.wait_ge(added, n * Q + r + 1)
                            e.tensor_tensor(to[:, half], to[:, half], pm[b * Q + r][:, half], ALU.add
                                            ).then_inc(added, 1)

                def turn(i, first):
                    for j in range(M):
                        n = i * M + j
                        if j % S == 0:
                            node = load(n * Q + (LAG - Q))
                        make(n, j, i, first)
                        if not first or j:
                            at = j % S * Q
                            adds(n - 1, (j - 1) % 2, node[at:at + Q])
                        next_indices(n, j)
                        if first and j == 0:
                            e.memset(acc[:, :, :], 0.0).then_inc(s_first, 1)
                            e.wait_ge(s_first, 1)
                load = registers(k, e, k.step_block, NT - 1, "node")
                turn(0, True)
                with e.Fori(1, TURNS) as i:
                    turn(i, False)
                node = load(TURNS * (Q * M) + (LAG - Q))
                adds(M * TURNS - 1, 1, node[0:Q])
                e.wait_ge(s_acc, STEPS + 1)
                e.wait_ge(s_acc2, STEPS + 1)

            @block.tensor
            def _(pe):
                def turn(i, first):
                    for j in range(M):
                        n, b = i * M + j, j % 2
                        pe.wait_ge(s_pick, n + 3)
                        pe.wait_ge(s_exc, n + 1)
                        pe.wait_ge(s_msg, n + 1)
                        if not first or j >= 2:
                            pe.wait_ge(s_acc2, n * Q - (Q - 1))
                        for r in range(Q):
                            ins = pe.matmul(pm[b * Q + r][:, 0:W], pick[:, b, r, :], msg[:, b, r, :], start=True,
                                            stop=True)
                        ins.then_inc(s_mm, 1)
                turn(0, True)
                with pe.Fori(1, TURNS) as i:
                    turn(i, False)


def reciprocal_sums(k, e, s_v, acc, rden):
    done = Chain(e, s_v)
    done(e.tensor_scalar(rden[:, :, :], acc[:, :, D:], 1e-30, None, ALU.max))
    done(e.reciprocal(rden[:, :, :], rden[:, :, :]))


def finish0(k, acc):
    nc, io = k.nc, k.io
    with ExitStack() as c:
        w = k.sb(c, "wout", [P, 2, D])
        b = k.sb(c, "bout", [P, D])
        rden = k.sb(c, "rden", [P, NT, H])
        hn = k.sb(c, "hn", [P, GROUP, D])
        xn = k.sb(c, "xn", [P, GROUP, D])
        xt = k.sb(c, "xt", [P, GROUP, 2, P])
        y = k.sb(c, "y", [P, GROUP, D])
        pt = [k.ps(c, f"pt{i}") for i in range(2)]
        py = [k.ps(c, f"py{i}") for i in range(2)]
        s_w, s_v, s_a, s_b, s_hn, s_tr, s_xt, s_mm, s_y, s_x = [k.sem(x) for x in
            ("w_loaded", "dve", "normed", "scaled", "h_ready", "turned", "xt_ready", "product", "biased", "x_ready")]
        s_bn = k.sem("statistics")
        with k.block() as block:
            mark_mask(k, block, c, 0, EARLY_MARKS)

            @block.sync
            def _(sp):
                sp.dma_start(w[:, :, :], io["W_out"].rearrange("(c p) n -> p c n", p=P)).then_inc(s_w, 16)
                sp.dma_start(b[:, :], row_bc(io["b_out"], P)).then_inc(s_w, 16)

            @block.vector
            def _(e):
                e.wait_ge(s_w, 32)
                reciprocal_sums(k, e, s_v, acc, rden)

                def scaled(t, j, first):
                    if not first:
                        e.wait_ge(s_tr, t - GROUP + 1)
                    e.tensor_tensor(hn[:, j, :].rearrange("p (d h) -> p h d", h=H),
                                    tile_of(acc, t)[:, 0:D].rearrange("p (h d) -> p h d", h=H),
                                    bc(tile_of(rden, t).unsqueeze(2), (P, H, D // H)), ALU.mult).then_inc(s_b, 1)
                    e.wait_ge(s_a, t + 1)
                    e.wait_ge(s_b, t + 1)
                    e.tensor_tensor(hn[:, j, :], hn[:, j, :], xn[:, j, :], ALU.add).then_inc(s_hn, 1)

                def turn(i, first, last):
                    for j in range(GROUP):
                        t = i * GROUP + j
                        if not last or j + 3 < GROUP:
                            scaled(t + 3, (j + 3) % GROUP, first and j + 3 < GROUP)
                        e.wait_ge(s_mm, t + 1)
                        e.tensor_tensor(y[:, j, :], py[j % 2][:, 0:D], b[:, :], ALU.add).then_inc(s_y, 1)
                        e.wait_ge(s_y, t + 1)
                        e.tensor_tensor(tile_of(k.x, t), tile_of(k.x, t), y[:, j, :], ALU.add).then_inc(s_x, 1)
                        e.wait_ge(s_x, t + 1)
                        row_stats(k, e, t, s_bn)
                for j in range(3):
                    scaled(j, j, True)
                turn(0, True, False)
                with e.Fori(1, NT // GROUP - 1) as i:
                    turn(i, False, False)
                turn(NT // GROUP - 1, False, True)
                e.wait_ge(s_bn, NT)

            @block.scalar
            def _(a):
                def norm(t, j, first):
                    if not first:
                        a.wait_ge(s_hn, t - GROUP + 1)
                    a.activation(xn[:, j, :], tile_of(k.x, t), ACT.Identity, bias=k.shift[:, bass.ds(t, 1)],
                                 scale=k.rstd[:, bass.ds(t, 1)]).then_inc(s_a, 1)

                def turn(i, first, last):
                    for j in range(GROUP):
                        t = i * GROUP + j
                        if not last or j + 4 < GROUP:
                            norm(t + 4, (j + 4) % GROUP, first and j + 4 < GROUP)
                        a.wait_ge(s_tr, t + 1)
                        if not first:
                            a.wait_ge(s_mm, t - GROUP + 1)
                        a.activation(xt[:, j, :, :], pt[j % 2][:, 0:256].rearrange("p (c n) -> p c n", c=2),
                                     ACT.Copy).then_inc(s_xt, 1)
                for j in range(4):
                    norm(j, j, True)
                turn(0, True, False)
                with a.Fori(1, NT // GROUP - 1) as i:
                    turn(i, False, False)
                turn(NT // GROUP - 1, False, True)

            @block.tensor
            def _(pe):
                pe.wait_ge(s_w, 32)

                def turned(t, j, first):
                    pe.wait_ge(s_hn, t + 1)
                    if not first or j >= 2:
                        pe.wait_ge(s_xt, t - held(j))
                    for h in range(2):
                        ins = pe.transpose(pt[j % 2][:, h * P:(h + 1) * P], hn[:, j, h * P:(h + 1) * P],
                                           k.ident[:, :])
                    ins.then_inc(s_tr, 1)

                def turn(i, first, last):
                    for j in range(GROUP):
                        t = i * GROUP + j
                        if not last or j + 1 < GROUP:
                            turned(t + 1, (j + 1) % GROUP, first and j + 1 < GROUP)
                        pe.wait_ge(s_xt, t + 1)
                        if not first or j >= 2:
                            pe.wait_ge(s_y, t - held(j))
                        for h in range(2):
                            ins = pe.matmul(py[j % 2][:, 0:D], xt[:, j, h, :], w[:, h, :], start=(h == 0), stop=(h == 1))
                        ins.then_inc(s_mm, 1)
                turned(0, 0, True)
                turn(0, True, False)
                with pe.Fori(1, NT // GROUP - 1) as i:
                    turn(i, False, False)
                turn(NT // GROUP - 1, False, True)


def columns(k, xnt, router, w_router, R, affine, ahead=()):
    nc, io = k.nc, k.io
    with ExitStack() as c:
        wr = k.sb(c, "wr", [P, 2, R])
        gb = k.sb(c, "gb", [P, 2, 2])
        xn = k.sb(c, "xn", [P, GROUP, D])
        xt = k.sb(c, "xt", [P, GROUP, 2, P])
        pt = [k.ps(c, f"pt{i}") for i in range(2)]
        pr = [k.ps(c, f"pr{i}") for i in range(2)]
        s_w, s_xn, s_tr, s_xt, s_mm, s_r, s_xk = [k.sem(x) for x in
            ("w_loaded", "xn_ready", "turned", "xt_ready", "routed", "router_kept", "xnt_kept")]
        n_w = 1 + 2 * bool(affine)
        s_ahead = k.sem("loaded_ahead")
        with k.block() as block:

            @block.sync
            def _(sp):
                sp.dma_start(wr[:, :, :], io[w_router].rearrange("(c p) n -> p c n", p=P)).then_inc(s_w, 16)
                if affine:
                    for n, name in enumerate(affine):
                        sp.dma_start(gb[:, n, :], io[name]).then_inc(s_w, 16)
                for to, src in ahead:
                    sp.dma_start(to, src).then_inc(s_ahead, 16)
                if ahead:
                    sp.wait_ge(s_ahead, 16 * len(ahead))

            @block.vector
            def _(e):
                def norm(t, j, first):
                    if not first:
                        e.wait_ge(s_tr, t - GROUP + 1)
                    e.tensor_scalar(xn[:, j, :], tile_of(k.x, t), k.mean[:, bass.ds(t, 1)],
                                    k.rstd[:, bass.ds(t, 1)], ALU.subtract, ALU.mult).then_inc(s_xn, 1)

                def keep(t, j):
                    e.wait_ge(s_xt, t + 1)
                    e.tensor_copy(xnt[:, :, bass.ds(t * P, P)], xt[:, j, :, :]).then_inc(s_xk, 1)

                def turn(i, first, last):
                    for j in range(GROUP):
                        t = i * GROUP + j
                        if not last or j + 1 < GROUP:
                            keep(t + 1, (j + 1) % GROUP)
                        if not last or j + 3 < GROUP:
                            norm(t + 3, (j + 3) % GROUP, first and j + 3 < GROUP)
                        e.wait_ge(s_mm, t + 1)
                        e.tensor_copy(tile_of(router, t), pr[j % 2][:, 0:R]).then_inc(s_r, 1)
                for j in range(3):
                    norm(j, j, True)
                keep(0, 0)
                turn(0, True, False)
                with e.Fori(1, NT // GROUP - 1) as i:
                    turn(i, False, False)
                turn(NT // GROUP - 1, False, True)
                e.wait_ge(s_r, NT)
                e.wait_ge(s_xk, NT)

            @block.scalar
            def _(a):
                a.wait_ge(s_w, 16 * n_w)

                def turn(i, first):
                    for j in range(GROUP):
                        t = i * GROUP + j
                        a.wait_ge(s_tr, t + 1)
                        if not first:
                            a.wait_ge(s_mm, t - GROUP + 1)
                            a.wait_ge(s_xk, t - GROUP + 1)
                        for h in range(2):
                            src = pt[j % 2][:, h * P:(h + 1) * P]
                            if affine:
                                ins = a.activation(xt[:, j, h, :], src, ACT.Identity, bias=gb[:, 1, h:h + 1],
                                                   scale=gb[:, 0, h:h + 1])
                            else:
                                ins = a.activation(xt[:, j, h, :], src, ACT.Copy)
                        ins.then_inc(s_xt, 1)
                turn(0, True)
                with a.Fori(1, NT // GROUP) as i:
                    turn(i, False)

            @block.tensor
            def _(pe):
                pe.wait_ge(s_w, 16 * n_w)

                def turned(t, j, first):
                    pe.wait_ge(s_xn, t + 1)
                    if not first or j >= 2:
                        pe.wait_ge(s_xt, t - held(j))
                    for h in range(2):
                        ins = pe.transpose(pt[j % 2][:, h * P:(h + 1) * P], xn[:, j, h * P:(h + 1) * P],
                                           k.ident[:, :])
                    ins.then_inc(s_tr, 1)

                def turn(i, first, last):
                    for j in range(GROUP):
                        t = i * GROUP + j
                        if not last or j + 1 < GROUP:
                            turned(t + 1, (j + 1) % GROUP, first and j + 1 < GROUP)
                        pe.wait_ge(s_xt, t + 1)
                        if not first or j >= 2:
                            pe.wait_ge(s_r, t - held(j))
                        for h in range(2):
                            ins = pe.matmul(pr[j % 2][:, 0:R], xt[:, j, h, :], wr[:, h, :], start=(h == 0),
                                            stop=(h == 1))
                        ins.then_inc(s_mm, 1)
                turned(0, 0, True)
                turn(0, True, False)
                with pe.Fori(1, NT // GROUP - 1) as i:
                    turn(i, False, False)
                turn(NT // GROUP - 1, False, True)


def top2_gates(k, score, gate, E, b_router=None):
    nc, io = k.nc, k.io
    with ExitStack() as c:
        b = k.sb(c, "b", [P, E])
        work = k.sb(c, "work", [P, NT, E])
        cand = k.sb(c, "cand", [P, NT, E])
        one = [k.sb(c, f"one{i}", [P, NT, E]) for i in range(2)]
        m = [k.sb(c, f"m{i}", [P, NT]) for i in range(2)]
        pick = k.sb(c, "pick", [P, NT])
        ww = [k.sb(c, f"ww{i}", [P, NT]) for i in range(2)]
        s_b, s_v, s_d, s_e = [k.sem(x) for x in ("b_loaded", "dve", "gap_ready", "exp_ready")]
        wide = lambda a: bc(a[:, :].unsqueeze(2), (P, NT, E))
        iota = bc(k.iota[:, 0:E].unsqueeze(1), (P, NT, E))
        with k.block() as block:

            if b_router:
                @block.sync
                def _(sp):
                    sp.dma_start(b[:, :], row_bc(io[b_router], P)).then_inc(s_b, 16)

            @block.vector
            def _(e):
                done = Chain(e, s_v)
                if b_router:
                    e.wait_ge(s_b, 16)
                    done(e.tensor_tensor(score[:, :, :], score[:, :, :], bc(b[:, :].unsqueeze(1), (P, NT, E)), ALU.add))
                done(e.tensor_copy(work[:, :, :], score[:, :, :]))
                for n in range(2):
                    done(e.tensor_reduce(m[n][:, :], work[:, :, :], AX, ALU.max))
                    done(e.tensor_tensor(cand[:, :, :], work[:, :, :], wide(m[n]), ALU.is_lt))
                    done(e.scalar_tensor_tensor(cand[:, :, :], cand[:, :, :], 99.0, iota, ALU.mult, ALU.add))
                    done(e.tensor_reduce(pick[:, :], cand[:, :, :], AX, ALU.min))
                    done(e.tensor_tensor(one[n][:, :, :], cand[:, :, :], wide(pick), ALU.is_equal))
                    if n == 0:
                        done(e.scalar_tensor_tensor(work[:, :, :], one[0][:, :, :], -BIG, work[:, :, :],
                                                    ALU.mult, ALU.add))
                done(e.tensor_tensor(m[1][:, :], m[1][:, :], m[0][:, :], ALU.subtract))
                e.sem_inc(s_d, 1)
                e.wait_ge(s_e, 1)
                done(e.tensor_scalar(ww[0][:, :], ww[1][:, :], 1.0, None, ALU.add))
                done(e.reciprocal(ww[0][:, :], ww[0][:, :]))
                done(e.tensor_tensor(ww[1][:, :], ww[1][:, :], ww[0][:, :], ALU.mult))
                done(e.tensor_tensor(one[0][:, :, :], one[0][:, :, :], wide(ww[0]), ALU.mult))
                done(e.tensor_tensor(one[1][:, :, :], one[1][:, :, :], wide(ww[1]), ALU.mult))
                done(e.tensor_tensor(gate[:, :, :], one[0][:, :, :], one[1][:, :, :], ALU.add))

            @block.scalar
            def _(a):
                a.wait_ge(s_d, 1)
                a.activation(ww[1][:, :], m[1][:, :], ACT.Exp).then_inc(s_e, 1)


def mark_mask(k, block, c, lo, hi):
    idx = k.sb(c, "idx", [P, 2], I32)
    zero1 = k.sb(c, "zero1", [P, 1], BF)
    s_i, s_mark, s_let, s_z = [k.sem(x) for x in ("pos_ready", "marked", "scatter_let", "zero_ready")]

    @block.gpsimd
    def _(g):
        g.memset(zero1[:, :], 0.0).then_inc(s_z, 1)
        g.wait_ge(s_z, 1)

        def scatter(b):
            g.sem_inc(s_let, 1)
            g.indirect_dma_start(k.mask_d, bass.IndirectOffsetOnAxis(idx[:, b:b + 1], 0), zero1[:, :], None,
                                 bounds_check=NP * NP - 1, oob_is_err=True).then_inc(s_mark, 16)
        for b in range(2):
            g.tensor_copy(idx[:, b:b + 1], k.mask_pos[:, lo + b:lo + b + 1]).then_inc(s_i, 1)
        g.wait_ge(s_i, 2)
        scatter(0)
        with g.Fori(0, (hi - lo) // 2 - 1) as i:
            for b in range(2):
                g.wait_ge(s_mark, i * 32 + 16 * b + 16)
                scatter(1 - b)
                g.tensor_copy(idx[:, b:b + 1], k.mask_pos[:, bass.ds(i * 2 + (lo + b + 2), 1)]).then_inc(s_i, 1)
                g.wait_ge(s_i, i * 2 + b + 3)
        g.wait_ge(s_mark, 16 * (hi - lo - 1))
        scatter(1)
        g.wait_ge(s_mark, 16 * (hi - lo))


def experts(k, xnt, gate, w1, w2, E, ahead):
    nc, io = k.nc, k.io
    F = 512
    FC = F // P
    with ExitStack() as c:
        b1s = k.sb(c, "b1s", [P, E, FC])
        b2s = k.sb(c, "b2s", [P, E, D])
        ht = k.sb(c, "ht", [P, 2, FC, P])
        y = k.sb(c, "y", [P, 2, D])
        ph = [k.ps(c, f"ph{i}") for i in range(2)]
        py = [k.ps(c, f"py{i}") for i in range(2)]
        s_w, s_h, s_g, s_y, s_b, s_x = [k.sem(x) for x in
            ("w_loaded", "hidden", "gelu_ready", "product", "biased", "x_ready")]
        s_bn, s_ahead = k.sem("statistics"), k.sem("loaded_ahead")
        with k.block() as block:
            mark_mask(k, block, c, EARLY_MARKS, GT)

            @block.sync
            def _(sp):
                sp.dma_start(b1s[:, :, :], io["b1_0"]).then_inc(s_w, 16)
                sp.dma_start(b2s[:, :, :].rearrange("p e d -> p (e d)"),
                             row_bc(io["b2_0"].rearrange("e d -> (e d)"), P)).then_inc(s_w, 16)
                for to, src in ahead:
                    sp.dma_start(to, src).then_inc(s_ahead, 16)
                sp.wait_ge(s_ahead, 16 * len(ahead))

            @block.tensor
            def _(pe):
                def hidden(i, n, first):
                    if not first:
                        pe.wait_ge(s_g, i * E + n - 1)
                    for f in range(FC):
                        for h in range(2):
                            ins = pe.matmul(ph[n % 2][:, f * P:(f + 1) * P], w1[:, n, h, f * P:(f + 1) * P],
                                            xnt[:, h, bass.ds(i * P, P)], start=(h == 0), stop=(h == 1))
                    ins.then_inc(s_h, 1)

                def output(i, n, first):
                    pe.wait_ge(s_g, i * E + n + 1)
                    if not first:
                        pe.wait_ge(s_b, i * E + n - 1)
                    for f in range(FC):
                        ins = pe.matmul(py[n % 2][:, 0:D], ht[:, n % 2, f, :], w2[:, n, f, :], start=(f == 0),
                                        stop=(f == FC - 1))
                    ins.then_inc(s_y, 1)

                def turn(i, first):
                    hidden(i, 0, first)
                    for n in range(E):
                        if n + 1 < E:
                            hidden(i, n + 1, first and n + 1 < 2)
                        output(i, n, first and n < 2)
                turn(0, True)
                with pe.Fori(1, NT) as i:
                    turn(i, False)

            @block.scalar
            def _(a):
                a.wait_ge(s_w, 32)

                def turn(i, first):
                    for n in range(E):
                        a.wait_ge(s_h, i * E + n + 1)
                        if not (first and n < 2):
                            a.wait_ge(s_y, i * E + n - 1)
                        for f in range(FC):
                            ins = a.activation(ht[:, n % 2, f, :], ph[n % 2][:, f * P:(f + 1) * P], ACT.Gelu,
                                               bias=b1s[:, n, f:f + 1])
                        ins.then_inc(s_g, 1)
                turn(0, True)
                with a.Fori(1, NT) as i:
                    turn(i, False)

            @block.vector
            def _(e):
                e.wait_ge(s_w, 32)
                e.sem_inc(s_x, 1)
                with e.Fori(0, NT) as i:
                    for n in range(E):
                        e.wait_ge(s_y, i * E + n + 1)
                        e.tensor_tensor(y[:, n % 2, :], py[n % 2][:, 0:D], b2s[:, n, :], ALU.add).then_inc(s_b, 1)
                        e.wait_ge(s_b, i * E + n + 1)
                        e.wait_ge(s_x, i * E + n + 1)
                        e.scalar_tensor_tensor(tile_of(k.x, i), y[:, n % 2, :],
                                               tile_of(gate, i)[:, n:n + 1], tile_of(k.x, i),
                                               ALU.mult, ALU.add).then_inc(s_x, 1)
                    e.wait_ge(s_x, i * E + (E + 1))
                    row_stats(k, e, i, s_bn)
                e.wait_ge(s_bn, NT)


def project1(k, qres, w):
    nc, io = k.nc, k.io
    T, R = 4, 8
    with ExitStack() as c:
        rel = k.sb(c, "rel", [P, 2, 2, R, 64])
        pri = k.sb(c, "pri", [P, R, 4])
        xn = k.sb(c, "xn", [P, GROUP, D])
        xm = k.sb(c, "xm", [P, GROUP, T, 2, P])
        kvt = k.sb(c, "kvt", [P, 2, 4, P])
        stage = k.sb(c, "stage", [P, 2, 2, R, D])
        pt = [k.ps(c, f"pt{i}") for i in range(2)]
        pk = k.ps(c, "pk")
        pq = k.ps(c, "pq")
        po = [k.ps(c, f"po{i}") for i in range(4)]
        s_w, s_blk, s_v, s_xn, s_tr, s_xm, s_kv, s_q, s_kvt, s_qs = [k.sem(x) for x in
            ("w_loaded", "rel_loaded", "dve", "xn_ready", "turned", "masked", "kv_ready", "q_ready",
             "kvt_ready", "q_kept")]
        s_o, s_od, s_oa, s_rel = [k.sem(x) for x in ("out_ready", "out_kept_dve", "out_kept_act", "rel_scaled")]
        s_st = [k.sem(f"stored{j}") for j in range(2)]
        kv_to = [x.rearrange("(t p r) d -> p t (r d)", p=P, r=R) for x in (k.kr_d, k.vr_d)]
        with k.block() as block:

            @block.sync
            def _(sp):
                sp.dma_start(pri[:, :, :].rearrange("p r h -> p (r h)"), row_bc(io["pri"], P)).then_inc(s_w, 16)
                for n, name in enumerate(("att_t", "msg")):
                    for h in range(4):
                        o = (h % 2) * 64
                        sp.dma_start(rel[o:o + 64, n, h // 2, :, :], io[name][h]).then_inc(s_blk, 16)

                def turn(i, first):
                    for j in range(GROUP):
                        t = i * GROUP + j
                        sp.wait_ge(s_od, (t + 1) * 4)
                        sp.wait_ge(s_oa, (t + 1) * 4)
                        for n in range(2):
                            sp.dma_start(kv_to[n][:, bass.ds(t, 1), :].rearrange("p a f -> p (a f)"),
                                         stage[:, j % 2, n, :, :].rearrange("p r d -> p (r d)")
                                         ).then_inc(s_st[j % 2], 16)
                with sp.Fori(0, NT // GROUP) as i:
                    turn(i, False)
                sp.wait_ge(s_st[0], 32 * 3 * (NT // GROUP))
                sp.wait_ge(s_st[1], 32 * 2 * (NT // GROUP))

            def free_stage(eng, i, j, first):
                uses = (3, 2)[j % 2]
                if not first or j >= 2:
                    eng.wait_ge(s_st[j % 2], i * (32 * uses) + 32 * (j // 2))

            def mask(e, j, t, n):
                return e.scalar_tensor_tensor(
                    xm[:, j, n, :, :], bc(k.ntype[:, bass.ds(t * P, P)].unsqueeze(1), (P, 2, P)), float(n),
                    pt[j % 2][:, 0:2 * P].rearrange("p (c n) -> p c n", c=2), ALU.is_equal, ALU.mult)

            def stage_head(j, m):
                return stage[:, j % 2, m // 4, :, (m % 4) * 64:(m % 4 + 1) * 64]

            @block.vector
            def _(e):
                done = Chain(e, s_v)
                def norm(t, j, first):
                    if not first:
                        e.wait_ge(s_tr, t - GROUP + 1)
                    e.tensor_scalar(xn[:, j, :], tile_of(k.x, t), k.mean[:, bass.ds(t, 1)],
                                    k.rstd[:, bass.ds(t, 1)], ALU.subtract, ALU.mult).then_inc(s_xn, 1)

                def masks(t, j, first):
                    e.wait_ge(s_tr, t + 1)
                    if not first:
                        e.wait_ge(s_q, t - GROUP + 1)
                    for n in range(T):
                        mask(e, j, t, n).then_inc(s_xm, 1)

                def turn(i, first, last):
                    for j in range(GROUP):
                        t = i * GROUP + j
                        if not last or j + 1 < GROUP:
                            masks(t + 1, (j + 1) % GROUP, first and j + 1 < GROUP)
                        if not last or j + 3 < GROUP:
                            norm(t + 3, (j + 3) % GROUP, first and j + 3 < GROUP)
                        free_stage(e, i, j, first)
                        for m in range(0, 8, 2):
                            e.wait_ge(s_o, t * 8 + m + 1)
                            e.tensor_copy(stage_head(j, m), po[m % 4][:, :].rearrange("p (r d) -> p r d", r=R)
                                          ).then_inc(s_od, 1)
                for j in range(3):
                    norm(j, j, True)
                masks(0, 0, True)
                e.wait_ge(s_w, 16)
                e.wait_ge(s_blk, 16 * 8)
                done(e.tensor_scalar(pri[:, :, :], pri[:, :, :], 0.125, None, ALU.mult))
                for h in range(4):
                    o = (h % 2) * 64
                    blk = rel[o:o + 64, 0, h // 2, :, :]
                    done(e.tensor_tensor(blk, blk, bc(pri[o:o + 64, :, h:h + 1], (64, R, 64)), ALU.mult))
                e.sem_inc(s_rel, 1)
                turn(0, True, False)
                with e.Fori(1, NT // GROUP - 1) as i:
                    turn(i, False, False)
                turn(NT // GROUP - 1, False, True)

            @block.scalar
            def _(a):
                def turn(i, first):
                    for j in range(GROUP):
                        t = i * GROUP + j
                        free_stage(a, i, j, first)
                        a.wait_ge(s_kv, t + 1)
                        a.activation(kvt[:, j % 2, :, :], pk[:, :].rearrange("p (m n) -> p m n", m=4),
                                     ACT.Copy).then_inc(s_kvt, 1)
                        a.wait_ge(s_q, t + 1)
                        a.activation(tile_of(qres, t), pq[:, 0:D], ACT.Copy).then_inc(s_qs, 1)
                        for m in range(1, 8, 2):
                            a.wait_ge(s_o, t * 8 + m + 1)
                            a.activation(stage_head(j, m), po[m % 4][:, :].rearrange("p (r d) -> p r d", r=R),
                                         ACT.Copy).then_inc(s_oa, 1)
                turn(0, True)
                with a.Fori(1, NT // GROUP) as i:
                    turn(i, False)

            @block.tensor
            def _(pe):
                def turned(t, j, first):
                    pe.wait_ge(s_xn, t + 1)
                    if not first or j >= 2:
                        pe.wait_ge(s_xm, (t - held(j)) * T)
                    for h in range(2):
                        ins = pe.transpose(pt[j % 2][:, h * P:(h + 1) * P], xn[:, j, h * P:(h + 1) * P],
                                           k.ident[:, :])
                    ins.then_inc(s_tr, 1)

                def turn(i, first, last):
                    for j in range(GROUP):
                        t = i * GROUP + j
                        if not last or j + 1 < GROUP:
                            turned(t + 1, (j + 1) % GROUP, first and j + 1 < GROUP)
                        pe.wait_ge(s_xm, (t + 1) * T)
                        if not first or j:
                            pe.wait_ge(s_kvt, t)
                            pe.wait_ge(s_qs, t)
                        for m in range(4):
                            for n in range(T):
                                for h in range(2):
                                    ins = pe.matmul(pk[:, m * P:(m + 1) * P],
                                                    w[:, m // 2, n, h, (m % 2) * P:(m % 2 + 1) * P],
                                                    xm[:, j, n, h, :], start=(n == 0 and h == 0),
                                                    stop=(n == T - 1 and h == 1))
                        ins.then_inc(s_kv, 1)
                        for n in range(T):
                            for h in range(2):
                                ins = pe.matmul(pq[:, 0:D], xm[:, j, n, h, :], w[:, 2, n, h, :],
                                                start=(n == 0 and h == 0), stop=(n == T - 1 and h == 1))
                        ins.then_inc(s_q, 1)
                        if first and j == 0:
                            pe.wait_ge(s_rel, 1)
                        pe.wait_ge(s_kvt, t + 1)
                        for m in range(8):
                            if m % 2 == 0 and (m >= 4 or not first or j):
                                for kept in (s_od, s_oa):
                                    pe.wait_ge(kept, t * 4 - 1 + m // 2)
                            mine = slice((m % 2) * 64, (m % 2 + 1) * 64)
                            pe.matmul(po[m % 4][:, :], kvt[mine, j % 2, m // 2, :],
                                      rel[mine, m // 4, m // 2 % 2, :, :].rearrange("p r d -> p (r d)"),
                                      start=True, stop=True).then_inc(s_o, 1)
                turned(0, 0, True)
                turn(0, True, False)
                with pe.Fori(1, NT // GROUP - 1) as i:
                    turn(i, False, False)
                turn(NT // GROUP - 1, False, True)


def finish1(k, acc):
    nc, io = k.nc, k.io
    T = 4
    with ExitStack() as c:
        w = k.sb(c, "wa", [P, T, 2, D])
        skip = k.sb(c, "skip", [P, T])
        rden = k.sb(c, "rden", [P, NT, H])
        hn = k.sb(c, "hn", [P, GROUP, D])
        xm = k.sb(c, "xm", [P, GROUP, T, 2, P])
        pt = [k.ps(c, f"pt{i}") for i in range(2)]
        py = [k.ps(c, f"py{i}") for i in range(2)]
        s_w, s_v, s_sig, s_wr, s_hn, s_tr, s_xm, s_mm, s_x = [k.sem(x) for x in
            ("w_loaded", "dve", "sigmoid", "w_ready", "h_ready", "turned", "masked", "product", "x_ready")]
        s_bn = k.sem("statistics")
        with k.block() as block:

            @block.sync
            def _(sp):
                sp.dma_start(w[:, :, :, :], io["a_linears"].rearrange("t (c p) o -> p t c o", p=P)).then_inc(s_w, 16)
                sp.dma_start(skip[:, :], row_bc(io["skip"], P)).then_inc(s_w, 16)

            @block.scalar
            def _(a):
                a.wait_ge(s_w, 32)
                a.activation(skip[:, :], skip[:, :], ACT.Sigmoid).then_inc(s_sig, 1)

            @block.vector
            def _(e):
                done = Chain(e, s_v)
                reciprocal_sums(k, e, k.sem("sums"), acc, rden)
                e.wait_ge(s_w, 32)
                e.wait_ge(s_sig, 1)
                for n in range(T):
                    done(e.tensor_scalar(w[:, n, :, :], w[:, n, :, :], skip[:, n:n + 1], None, ALU.mult))
                e.sem_inc(s_wr, 1)

                def scaled(t, j, first):
                    if not first:
                        e.wait_ge(s_tr, t - GROUP + 1)
                    e.tensor_tensor(hn[:, j, :].rearrange("p (h d) -> p h d", h=4),
                                    tile_of(acc, t)[:, 0:D].rearrange("p (h d) -> p h d", h=4),
                                    bc(tile_of(rden, t)[:, 0:4].unsqueeze(2), (P, 4, D // 4)),
                                    ALU.mult).then_inc(s_hn, 1)

                def masks(t, j, first):
                    e.wait_ge(s_tr, t + 1)
                    if not first:
                        e.wait_ge(s_mm, t - GROUP + 1)
                    for n in range(T):
                        e.scalar_tensor_tensor(
                            xm[:, j, n, :, :], bc(k.ntype[:, bass.ds(t * P, P)].unsqueeze(1), (P, 2, P)), float(n),
                            pt[j % 2][:, 0:2 * P].rearrange("p (c n) -> p c n", c=2), ALU.is_equal,
                            ALU.mult).then_inc(s_xm, 1)

                def turn(i, first, last):
                    for j in range(GROUP):
                        t = i * GROUP + j
                        if not last or j + 1 < GROUP:
                            masks(t + 1, (j + 1) % GROUP, first and j + 1 < GROUP)
                        if not last or j + 3 < GROUP:
                            scaled(t + 3, (j + 3) % GROUP, first and j + 3 < GROUP)
                        e.wait_ge(s_mm, t + 1)
                        e.tensor_tensor(tile_of(k.x, t), tile_of(k.x, t), py[j % 2][:, 0:D], ALU.add).then_inc(s_x, 1)
                        e.wait_ge(s_x, t + 1)
                        row_stats(k, e, t, s_bn)
                for j in range(3):
                    scaled(j, j, True)
                masks(0, 0, True)
                turn(0, True, False)
                with e.Fori(1, NT // GROUP - 1) as i:
                    turn(i, False, False)
                turn(NT // GROUP - 1, False, True)
                e.wait_ge(s_bn, NT)

            @block.tensor
            def _(pe):
                pe.wait_ge(s_wr, 1)

                def turned(t, j, first):
                    pe.wait_ge(s_hn, t + 1)
                    if not first or j >= 2:
                        pe.wait_ge(s_xm, (t - held(j)) * T)
                    for h in range(2):
                        ins = pe.transpose(pt[j % 2][:, h * P:(h + 1) * P], hn[:, j, h * P:(h + 1) * P],
                                           k.ident[:, :])
                    ins.then_inc(s_tr, 1)

                def turn(i, first, last):
                    for j in range(GROUP):
                        t = i * GROUP + j
                        if not last or j + 1 < GROUP:
                            turned(t + 1, (j + 1) % GROUP, first and j + 1 < GROUP)
                        pe.wait_ge(s_xm, (t + 1) * T)
                        if not first or j >= 2:
                            pe.wait_ge(s_x, t - held(j))
                        for n in range(T):
                            for h in range(2):
                                ins = pe.matmul(py[j % 2][:, 0:D], xm[:, j, n, h, :], w[:, n, h, :],
                                                start=(n == 0 and h == 0), stop=(n == T - 1 and h == 1))
                        ins.then_inc(s_mm, 1)
                turned(0, 0, True)
                turn(0, True, False)
                with pe.Fori(1, NT // GROUP - 1) as i:
                    turn(i, False, False)
                turn(NT // GROUP - 1, False, True)


def leaky(e, done, out, x):
    done(e.scalar_tensor_tensor(out, x, 0.2, x, ALU.mult, ALU.max))


def gate_tables(k, h16, gs, gd, rs_all, xnt):
    nc, io = k.nc, k.io
    E, F = 4, 512
    FC = F // P
    B = 8
    with ExitStack() as c:
        att = k.sb(c, "att", [P, 2, 16])
        prod = k.sb(c, "prod", [P, 2, NT, 16])
        arow = k.sb(c, "arow", [4, NP])
        every = k.sb(c, "every", [P, 4, NP])
        mask = k.sb(c, "mask", [P, 2, NP], BF)
        scr = k.sb(c, "scr", [P, NP], BF)
        mx = k.sb(c, "mx", [P, 2, 4])
        most = k.sb(c, "most", [P, (NT + 1) * 4])
        w1 = k.sb(c, "w1", [P, 2, 2, F])
        w2 = k.sb(c, "w2", [P, 2, FC, D])
        b1s = k.sb(c, "b1s", [P, E, FC])
        ht = k.sb(c, "ht", [P, 2, FC, P])
        y = k.sb(c, "y", [P, 2, D])
        idx = k.sb(c, "idx", [P, 2, B], I32)
        rs = k.sb(c, "rs", [P, 2, B, 20])
        pt = [k.ps(c, f"pt{i}") for i in range(4)]
        ph = [k.ps(c, f"ph{i}") for i in range(2)]
        py = [k.ps(c, f"py{i}") for i in range(2)]
        s_w, s_v, s_t, s_tk, s_row, s_mx, s_cp = [k.sem(x) for x in
            ("w_loaded", "dve", "turned", "row_kept", "row_ready", "maxima", "maxima_kept")]
        s_let, s_fetch, s_gs = k.sem("mask_let"), k.sem("fetch_let"), k.sem("gs_stored")
        s_as, s_gd, s_out = k.sem("asrc_ready"), k.sem("gd_ready"), k.sem("stored")
        s_b1, s_h, s_g, s_y, s_yk = [k.sem(x) for x in ("b1_loaded", "hidden", "gelu_ready", "product", "y_kept")]
        s_idx, s_rk = k.sem("idx_ready"), k.sem("rows_kept")
        s_all = [k.sem(f"row_spread{h}") for h in range(4)]
        s_m = [k.sem(f"mask_in{j}") for j in range(2)]
        s_we = [k.sem(f"expert_in{j}") for j in range(2)]
        s_st = [k.sem(f"y_stored{j}") for j in range(2)]
        s_rows = [k.sem(f"rows_in{j}") for j in range(2)]
        rows = k.mask_d.rearrange("(t p f) o -> p t (f o)", p=P, f=NP)
        y_to = k.y_d.rearrange("(t p) e d -> e p t d", p=P)

        def fetch_expert(eng, n):
            eng.dma_start(w1[:, n % 2, :, :], io["W1_1"].rearrange("e (c p) f -> e p c f", p=P)[n]
                          ).then_inc(s_we[n % 2], 16)
            eng.dma_start(w2[:, n % 2, :, :], io["W2_1"].rearrange("e (c p) d -> e p c d", p=P)[n]
                          ).then_inc(s_we[n % 2], 16)

        with k.block() as block:

            @block.sync
            def _(sp):
                sp.dma_start(att[:, 0, :], row_bc(io["att_src"], P)).then_inc(s_w, 16)
                sp.dma_start(att[:, 1, :], row_bc(io["att_dst"], P)).then_inc(s_w, 16)
                sp.dma_start(b1s[:, :, :], io["b1_1"]).then_inc(s_b1, 16)
                fetch_expert(sp, 0)
                for j in range(2):
                    sp.dma_start(mask[:, j, :], rows[:, j, :]).then_inc(s_m[j], 16)
                fetch_expert(sp, 1)
                sp.wait_ge(s_tk, 7)
                sp.dma_start(k.asrc_d, arow[:, :]).then_inc(s_row, 16)
                sp.dma_start(k.gs_d.rearrange("(t p) f -> p t f", p=P), gs[:, :, :]).then_inc(s_gs, 16)
                sp.wait_ge(s_row, 16)
                for h in range(4):
                    sp.dma_start(every[:, h, :], row_bc(k.asrc_d[h], P)).then_inc(s_all[h], 16)

                def fetch_mask(t, j):
                    sp.wait_ge(s_mx, (t - 1) * 4)
                    sp.dma_start(mask[:, j, :], rows[:, bass.ds(t, 1), :].rearrange("p a f -> p (a f)")
                                 ).then_inc(s_m[j], 16)
                with sp.Fori(1, NT // 2) as i:
                    for j in range(2):
                        fetch_mask(i * 2 + j, j)
                fetch_mask(NT - 1, 0)
                sp.wait_ge(s_gd, 1)
                sp.dma_start(k.gd_d.rearrange("(t p) f -> p t f", p=P), gd[:, :, :]).then_inc(s_out, 16)
                sp.wait_ge(s_out, 16)

            @block.gpsimd
            def _(g):
                g.sem_inc(s_rk, 2)
                g.wait_ge(s_gs, 16)
                g.sem_inc(s_fetch, 1)

                def fetch(n, b, i):
                    g.wait_ge(s_rk, n + 1)
                    g.tensor_copy(idx[:, b, :], k.gpair[:, bass.ds(n * B, B), 1]).then_inc(s_idx, 1)
                    g.wait_ge(s_idx, n + 1)
                    g.sem_inc(s_fetch, 1)
                    for j in range(B):
                        g.indirect_dma_start(rs[:, b, j, :], None, k.gs_d,
                                             bass.IndirectOffsetOnAxis(idx[:, b, j:j + 1], 0),
                                             bounds_check=NP - 1, oob_is_err=True).then_inc(s_rows[b], 16)

                def keep(n, b, turns):
                    g.wait_ge(s_rows[b], turns * (16 * B))
                    g.tensor_copy(rs_all[:, bass.ds(n * B, B), :], rs[:, b, :, :]).then_inc(s_rk, 1)
                fetch(0, 0, 0)
                with g.Fori(0, GT // (2 * B) - 1) as i:
                    fetch(i * 2 + 1, 1, i)
                    keep(i * 2, 0, i + 1)
                    fetch(i * 2 + 2, 0, i)
                    keep(i * 2 + 1, 1, i + 1)
                n = GT // B - 2
                fetch(n + 1, 1, n // 2)
                keep(n, 0, n // 2 + 1)
                keep(n + 1, 1, n // 2 + 1)
                g.wait_ge(s_rk, GT // B + 2)

            @block.tensor
            def _(pe):
                pe.wait_ge(s_as, 1)
                for t in range(NT):
                    if t % 4 == 0 and t // 4 >= 4:
                        pe.wait_ge(s_tk, t // 4 - 3)
                    ins = pe.transpose(pt[t // 4 % 4][0:4, (t % 4) * P:(t % 4 + 1) * P], gs[:, t, 0:4], k.ident[:, :])
                    if t % 4 == 3 or t == NT - 1:
                        ins.then_inc(s_t, 1)

                def hidden(m, b, n, t):
                    pe.wait_ge(s_g, m)
                    for f in range(FC):
                        for h in range(2):
                            ins = pe.matmul(ph[b][:, f * P:(f + 1) * P], w1[:, n % 2, h, f * P:(f + 1) * P],
                                            xnt[:, h, bass.ds(t * P, P)], start=(h == 0), stop=(h == 1))
                    ins.then_inc(s_h, 1)

                def output(m, b, n):
                    pe.wait_ge(s_g, m + 2)
                    pe.wait_ge(s_yk, m + 1)
                    for f in range(FC):
                        ins = pe.matmul(py[b][:, 0:D], ht[:, b, f, :], w2[:, n % 2, f, :], start=(f == 0),
                                        stop=(f == FC - 1))
                    ins.then_inc(s_y, 1)
                pe.sem_inc(s_y, 2)
                pe.wait_ge(s_we[0], 32)
                for f in range(FC):
                    for h in range(2):
                        ins = pe.matmul(ph[0][:, f * P:(f + 1) * P], w1[:, 0, h, f * P:(f + 1) * P],
                                        xnt[:, h, 0:P], start=(h == 0), stop=(h == 1))
                ins.then_inc(s_h, 1)
                for n in range(E):
                    with pe.Fori(0, NT // 2) as i:
                        for u in range(2):
                            m, b = i * 2 + (n * NT + u), (n * NT + u) % 2
                            hidden(m + 1, 1 - b, n, i * 2 + (u + 1))
                            output(m, b, n)
                    m = n * NT + NT - 1
                    if n + 1 < E:
                        pe.wait_ge(s_we[(n + 1) % 2], 32 * ((n + 1) // 2 + 1))
                        hidden(m + 1, (m + 1) % 2, n + 1, 0)
                    output(m, m % 2, n)

            @block.scalar
            def _(a):
                a.sem_inc(s_g, 1)
                a.sem_inc(s_yk, 2)
                for b in range(2):
                    a.sem_inc(s_st[b], 16)
                for g in range(7):
                    n = min(4, NT - 4 * g)
                    a.wait_ge(s_t, g + 1)
                    a.activation(arow[:, g * 4 * P:(g * 4 + n) * P], pt[g % 4][0:4, 0:n * P], ACT.Copy
                                 ).then_inc(s_tk, 1)
                a.wait_ge(s_b1, 16)

                def gelu(m, b, n):
                    a.wait_ge(s_h, m + 1)
                    a.wait_ge(s_y, m + 1)
                    for f in range(FC):
                        ins = a.activation(ht[:, b, f, :], ph[b][:, f * P:(f + 1) * P], ACT.Gelu,
                                           bias=b1s[:, n, f:f + 1])
                    ins.then_inc(s_g, 1)

                def keep(m, b, uses, n, t):
                    a.wait_ge(s_y, m + 3)
                    a.wait_ge(s_st[b], uses * 16 + 16)
                    a.activation(y[:, b, :], py[b][:, 0:D], ACT.Copy).then_inc(s_yk, 1)
                    a.wait_ge(s_yk, m + 3)
                    a.dma_start(y_to[n][:, bass.ds(t, 1), :].rearrange("p a d -> p (a d)"), y[:, b, :]
                                ).then_inc(s_st[b], 16)
                gelu(0, 0, 0)
                for n in range(E):
                    with a.Fori(0, NT // 2) as i:
                        for u in range(2):
                            m, b = i * 2 + (n * NT + u), (n * NT + u) % 2
                            gelu(m + 1, 1 - b, n)
                            keep(m, b, i + (n * NT + u) // 2, n, i * 2 + u)
                    m = n * NT + NT - 1
                    if n + 1 < E:
                        gelu(m + 1, (m + 1) % 2, n + 1)
                    keep(m, m % 2, m // 2, n, NT - 1)
                    if n + 2 < E:
                        fetch_expert(a, n + 2)
                for b in range(2):
                    a.wait_ge(s_st[b], 16 + 16 * (E * NT // 2))

            @block.vector
            def _(e):
                done = Chain(e, s_v)
                e.wait_ge(s_w, 32)
                for n, out in enumerate((gs, gd)):
                    done(e.tensor_tensor(prod[:, n, :, :], h16[:, :, :], bc(att[:, n:n + 1, :], (P, NT, 16)), ALU.mult))
                    done(e.tensor_reduce(out[:, :, 0:4], prod[:, n, :, :].rearrange("p t (h x) -> p t h x", x=4),
                                         AX, ALU.add))
                done(e.tensor_copy(gs[:, :, 4:20], h16[:, :, :]))
                e.sem_inc(s_as, 1)
                e.sem_inc(s_cp, 2)

                def maxima(t, j, turns, first=False):
                    e.wait_ge(s_m[j], turns * 16)
                    e.wait_ge(s_cp, t + 1)
                    e.sem_inc(s_let, 1)
                    for h in range(4):
                        if first:
                            e.wait_ge(s_all[h], 16)
                            e.sem_inc(s_let, 1)
                        e.tensor_tensor_reduce(scr[:, 0:N], mask[:, j, 0:N], every[:, h, 0:N], 1.0, -BIG, ALU.add,
                                               ALU.max, mx[:, j, h:h + 1]).then_inc(s_mx, 1)
                        e.wait_ge(s_mx, t * 4 + h + 1)
                        e.sem_inc(s_let, 1)
                    e.tensor_copy(most[:, bass.ds(t * 4, 4)], mx[:, j, :]).then_inc(s_cp, 1)
                maxima(0, 0, 1, first=True)
                with e.Fori(0, NT // 2) as i:
                    maxima(i * 2 + 1, 1, i + 1)
                    maxima(i * 2 + 2, 0, i + 2)
                e.wait_ge(s_cp, NT + 2)
                m3 = most[:, 0:NT * 4].rearrange("p (t h) -> p t h", h=4)
                done(e.tensor_tensor(m3, m3, gs[:, :, 0:4], ALU.max))
                done(e.tensor_tensor(m3, m3, gd[:, :, 0:4], ALU.add))
                leaky(e, done, gd[:, :, 4:8], m3)
                e.sem_inc(s_gd, 1)


def gate_sums(k, gs, gd, rs_all, yall, score):
    nc, io = k.nc, k.io
    B = 8
    C = NT * 20
    F = 4
    with ExitStack() as c:
        idx = k.sb(c, "idx", [P, F, B], I32)
        b2s = k.sb(c, "b2s", [P, 4, D])
        rd = k.sb(c, "rd", [P, F, B, 8])
        ev = k.sb(c, "ev", [P, 2, B, 4])
        f = k.sb(c, "f", [P, 2, B, 20])
        lo = k.sb(c, "lo", [P, 2, B, P])
        hi = k.sb(c, "hi", [P, 2, B, NT])
        wide = k.sb(c, "wide", [P, 4, C])
        zero = k.sb(c, "zero", [P, C])
        agg = k.sb(c, "agg", [P, NT, 20])
        own = k.sb(c, "own", [P, NT, 20])
        nrm = k.sb(c, "nrm", [P, NT, 16])
        sq = k.sb(c, "sq", [P, NT, 16])
        m1 = k.sb(c, "m1", [P, NT])
        v1 = k.sb(c, "v1", [P, NT])
        par = k.sb(c, "par", [P, 3, 16])
        pa = k.ps(c, "pa")
        s_w, s_first, s_idx, s_v, s_e, s_ex, s_hot, s_mm, s_own, s_ownx, s_var, s_std = [k.sem(x) for x in
            ("w_loaded", "first", "idx_ready", "dve", "gap_ready", "exp_ready", "wide_ready", "summed", "loop_gap",
             "loop_exp", "var_ready", "std_ready")]
        s_let, s_yb = k.sem("fetch_let"), k.sem("y_biased")
        s_yin = [k.sem(f"y_in{j}") for j in range(NT // GROUP)]
        s_g = [k.sem(f"rows_in{b}") for b in range(F)]
        with k.block() as block:

            @block.sync
            def _(sp):
                for n, name in enumerate(("b_gat", "ln_gamma", "ln_beta")):
                    sp.dma_start(par[:, n, :], row_bc(io[name], P)).then_inc(s_w, 16)
                sp.dma_start(b2s[:, :, :].rearrange("p e d -> p (e d)"),
                             row_bc(io["b2_1"].rearrange("e d -> (e d)"), P)).then_inc(s_w, 16)
                y_from = k.y_d.rearrange("(t p) e d -> p t e d", p=P)
                for j in range(NT // GROUP):
                    ts = slice(j * GROUP, (j + 1) * GROUP)
                    sp.dma_start(yall[:, ts, :, :], y_from[:, ts, :, :]).then_inc(s_yin[j], 16)

            @block.gpsimd
            def _(g):
                with g.Fori(0, GT // (F * B)) as i:
                    for b in range(F):
                        g.wait_ge(s_idx, i * F + b + 1)
                        g.sem_inc(s_let, 1)
                        for j in range(B):
                            g.indirect_dma_start(rd[:, b, j, :], None, k.gd_d,
                                                 bass.IndirectOffsetOnAxis(idx[:, b, j:j + 1], 0),
                                                 bounds_check=NP - 1, oob_is_err=True).then_inc(s_g[b], 16)
                g.wait_ge(s_w, 64)
                for j in range(NT // GROUP):
                    g.wait_ge(s_yin[j], 16)
                    ts = slice(j * GROUP, (j + 1) * GROUP)
                    g.tensor_tensor(yall[:, ts, :, :], yall[:, ts, :, :], bc(b2s[:, :, :].unsqueeze(1), (P, GROUP, 4, D)),
                                    ALU.add).then_inc(s_yb, 1)
                g.wait_ge(s_yb, NT // GROUP)

            @block.scalar
            def _(a):
                a.wait_ge(s_own, 1)
                a.activation(own[:, :, 0:4], own[:, :, 0:4], ACT.Exp).then_inc(s_ownx, 1)
                with a.Fori(0, GT // (2 * B)) as i:
                    for b in range(2):
                        a.wait_ge(s_e, i * 2 + b + 1)
                        a.activation(f[:, b, :, 0:4], ev[:, b, :, :], ACT.Exp).then_inc(s_ex, 1)
                a.wait_ge(s_var, 1)
                a.activation(v1[:, :], v1[:, :], ACT.Sqrt, bias=k.eps[:, 0:1]).then_inc(s_std, 1)

            @block.tensor
            def _(pe):
                pe.wait_ge(s_first, 1)
                pe.matmul(pa[:, 0:C], zero[:, 0:P], zero[:, :], start=True, stop=False, skip_group_check=True)
                with pe.Fori(0, GT // (2 * B)) as i:
                    for b in range(2):
                        for j in range(B):
                            pe.wait_ge(s_hot, (i * 2 + b) * B + j + 1)
                            pe.matmul(pa[:, 0:C], lo[:, b, j, :], wide[:, j % 4, :], start=False, stop=False,
                                      skip_group_check=True).then_inc(s_mm, 1)
                pe.matmul(pa[:, 0:C], zero[:, 0:P], zero[:, :], start=False, stop=True,
                          skip_group_check=True).then_inc(s_mm, 1)

            @block.vector
            def _(e):
                e.memset(zero[:, :], 0.0).then_inc(s_v, 1)
                e.tensor_copy(idx[:, :, :], k.gpair[:, 0:F * B, 0].rearrange("p (a b) -> p a b", a=F)
                              ).then_inc(s_v, 1)
                done = Chain(e, s_v, start=2)
                done.sync()
                e.sem_inc(s_first, 1)
                e.sem_inc(s_idx, F)
                e.sem_inc(s_mm, 2 * B)
                done(e.tensor_tensor(own[:, :, 0:4], gs[:, :, 0:4], gd[:, :, 0:4], ALU.add))
                leaky(e, done, own[:, :, 0:4], own[:, :, 0:4])
                done(e.tensor_tensor(own[:, :, 0:4], own[:, :, 0:4], gd[:, :, 4:8], ALU.subtract))
                e.sem_inc(s_own, 1)
                e.wait_ge(s_ownx, 1)
                for x in range(4):
                    done(e.tensor_tensor(own[:, :, 4 + x:20:4], gs[:, :, 4 + x:20:4], own[:, :, 0:4], ALU.mult))
                base = done.n

                def gaps(n, j, turns, then, more=True):
                    b = j % 2
                    rs = rs_all[:, bass.ds(n * B, B), 0:4]
                    e.wait_ge(s_g[j], turns * (16 * B))
                    e.wait_ge(s_ex, n + 1)
                    then(e.tensor_tensor(ev[:, b, :, :], rs, rd[:, j, :, 0:4], ALU.add))
                    leaky(e, then, ev[:, b, :, :], ev[:, b, :, :])
                    then(e.tensor_tensor(ev[:, b, :, :], ev[:, b, :, :], rd[:, j, :, 4:8], ALU.subtract))
                    e.sem_inc(s_e, 1)
                    if more:
                        e.tensor_copy(idx[:, j, :], k.gpair[:, bass.ds(n * B + F * B, B), 0]).then_inc(s_idx, 1)

                def digits(n, b, then):
                    T0 = n * B
                    e.wait_ge(s_mm, T0 + B)
                    then(e.tensor_tensor(lo[:, b, :, :], bc(k.iota[:, :].unsqueeze(1), (P, B, P)),
                                         bc(k.glo[:, bass.ds(T0, B)].unsqueeze(2), (P, B, P)), ALU.is_equal))
                    then(e.tensor_tensor(hi[:, b, :, :], bc(k.iota[:, 0:NT].unsqueeze(1), (P, B, NT)),
                                         bc(k.ghi[:, bass.ds(T0, B)].unsqueeze(2), (P, B, NT)), ALU.is_equal))

                def weigh(n, b, then):
                    rs = rs_all[:, bass.ds(n * B, B), :]
                    e.wait_ge(s_ex, n + 3)
                    for x in range(4):
                        then(e.tensor_tensor(f[:, b, :, 4 + x:20:4], rs[:, :, 4 + x:20:4], f[:, b, :, 0:4], ALU.mult))

                def spread(n, b, j):
                    e.wait_ge(s_mm, n * B + (j + 2 * B - 3))
                    e.tensor_tensor(wide[:, j % 4, :].rearrange("p (n f) -> p n f", n=NT),
                                    bc(hi[:, b, j, :].unsqueeze(2), (P, NT, 20)),
                                    bc(f[:, b, j:j + 1, :], (P, NT, 20)), ALU.mult).then_inc(s_hot, 1)
                e.sem_inc(s_ex, 2)
                gaps(0, 0, 1, done)
                digits(0, 0, done)
                base, per = done.n, 9 * F

                def turn(i, then, last):
                    for j in range(F):
                        n, b = i * F + j, j % 2
                        more = not last or j + 1 < F
                        if more:
                            gaps(n + 1, (j + 1) % F, i + (2 if j + 1 == F else 1), then, more=not last)
                        weigh(n, b, then)
                        for r in range(B // 2):
                            spread(n, b, r)
                        if more:
                            digits(n + 1, 1 - b, then)
                        for r in range(B // 2, B):
                            spread(n, b, r)
                turns = GT // (F * B)
                with e.Fori(0, turns - 1) as i:
                    loop = Chain(e, s_v, base=i * per + base)
                    turn(i, loop, False)
                    assert loop.n == per, loop.n
                done = Chain(e, s_v, start=base + per * (turns - 1))
                turn(turns - 1, done, True)
                e.wait_ge(s_mm, GT + 2 * B + 1)
                done(e.tensor_tensor(agg[:, :, :], pa[:, 0:C].rearrange("p (n f) -> p n f", n=NT), own[:, :, :], ALU.add))
                done(e.tensor_scalar(own[:, :, 0:4], agg[:, :, 0:4], 1e-16, None, ALU.add))
                done(e.reciprocal(own[:, :, 0:4], own[:, :, 0:4]))
                for x in range(4):
                    done(e.tensor_tensor(nrm[:, :, x::4], agg[:, :, 4 + x:20:4], own[:, :, 0:4], ALU.mult))
                e.wait_ge(s_w, 64)
                done(e.tensor_tensor(nrm[:, :, :], nrm[:, :, :], bc(par[:, 0:1, :], (P, NT, 16)), ALU.add))
                done(e.tensor_reduce(m1[:, :], nrm[:, :, :], AX, ALU.add))
                done(e.tensor_scalar(m1[:, :], m1[:, :], 1.0 / 16, None, ALU.mult))
                done(e.tensor_tensor(nrm[:, :, :], nrm[:, :, :], bc(m1[:, :].unsqueeze(2), (P, NT, 16)), ALU.subtract))
                done(e.tensor_tensor(sq[:, :, :], nrm[:, :, :], nrm[:, :, :], ALU.mult))
                done(e.tensor_reduce(v1[:, :], sq[:, :, :], AX, ALU.add))
                done(e.tensor_scalar(v1[:, :], v1[:, :], 1.0 / 16, None, ALU.mult))
                e.sem_inc(s_var, 1)
                e.wait_ge(s_std, 1)
                done(e.reciprocal(v1[:, :], v1[:, :]))
                done(e.tensor_tensor(nrm[:, :, :], nrm[:, :, :], bc(v1[:, :].unsqueeze(2), (P, NT, 16)), ALU.mult))
                done(e.tensor_tensor(nrm[:, :, :], nrm[:, :, :], bc(par[:, 1:2, :], (P, NT, 16)), ALU.mult))
                done(e.tensor_tensor(nrm[:, :, :], nrm[:, :, :], bc(par[:, 2:3, :], (P, NT, 16)), ALU.add))
                done(e.tensor_reduce(score[:, :, :], nrm[:, :, :].rearrange("p t (h x) -> p t x h", x=4), AX, ALU.add))
                done(e.tensor_scalar(score[:, :, :], score[:, :, :], 0.25, None, ALU.mult))


def combine(k, yall, gate, to):
    E = 4
    s_x, s_o = [k.sem(f"x_ready{g}") for g in range(NT // GROUP)], k.sem("stored")
    s_scaled = k.sem("scaled")
    with k.block() as block:

        @block.vector
        def _(e):
            for t in range(0, 3 * GROUP, GROUP):
                for n in range(E):
                    for j in range(GROUP):
                        if n:
                            e.wait_ge(s_x[t // GROUP], (n - 1) * GROUP + j + 1)
                        e.scalar_tensor_tensor(k.x[:, t + j, :], yall[:, t + j, n, :], gate[:, t + j, n:n + 1],
                                               k.x[:, t + j, :], ALU.mult, ALU.add).then_inc(s_x[t // GROUP], 1)

        @block.scalar
        def _(a):
            for t in range(3 * GROUP, NT, GROUP):
                for n in range(E):
                    for j in range(t, t + GROUP):
                        ins = a.activation(yall[:, j, n, :], yall[:, j, n, :], ACT.Copy, scale=gate[:, j, n:n + 1])
                    ins.then_inc(s_scaled, 1)

        @block.gpsimd
        def _(g):
            for t in range(3 * GROUP, NT, GROUP):
                for n in range(E):
                    g.wait_ge(s_scaled, (t // GROUP - 3) * E + n + 1)
                    if n:
                        g.wait_ge(s_x[t // GROUP], n * GROUP)
                    to = k.x[:, t:t + GROUP, :]
                    g.tensor_tensor(to, to, yall[:, t:t + GROUP, n, :], ALU.add).then_inc(s_x[t // GROUP], GROUP)

        @block.sync
        def _(sp):
            full = to[0:(NT - 1) * P, :].rearrange("(t p) d -> p t d", p=P)
            for t in (GROUP * g for g in (0, 3, 1, 2, 4)):
                sp.wait_ge(s_x[t // GROUP], GROUP * E)
                n = min(t + GROUP, NT - 1)
                sp.dma_start(full[:, t:n, :], k.x[:, t:n, :]).then_inc(s_o, 16)
            sp.dma_start(to[(NT - 1) * P:, :], k.x[0:to.shape[0] - (NT - 1) * P, NT - 1, :]).then_inc(s_o, 16)
            sp.wait_ge(s_o, 16 * (NT // GROUP + 1))


def build(nc, io, out):
    with ExitStack() as ctx:
        k = Kernel(nc, io, ctx)
        setup(k)
        with ExitStack() as graph:
            graph_tables(k, graph)
            k.acc = k.sb(graph, "acc", [P, NT, D + H])
            with ExitStack() as c:
                w = k.sb(c, "wqkv", [P, 2, 3 * D])
                structure(k, w)
                ln_scales(k)
                project0(k, k.acc[:, :, 0:D], w)
            attention(k, 0)
            with ExitStack() as c:
                w = k.sb(c, "wkvq", [P, 3, 4, 2, D])
                mix0(k, [(w[:, n, :, :, :], io[name].rearrange("t (c p) o -> p t c o", p=P))
                         for n, name in enumerate(("k_linears", "v_linears", "q_linears"))])
                ln_scales(k)
                project1(k, k.acc[:, :, 0:D], w)
            attention(k, 1)
        mix1(k, out)


def attention(k, layer):
    heads, rows, scale = ((8, NP, 32 ** -0.5), (4, NP * 8, 1.0))[layer]
    k_d, v_d = ((k.k_d, k.v_d), (k.kr_d, k.vr_d))[layer]
    steps = (k.step_src, k.step_rel)[layer]
    acc = k.acc
    with ExitStack() as c:
        ex = k.sb(c, "ex", [P, SP_, H])
        vv = k.sb(c, "vv", [P, M, Q, D])
        idx = k.sb(c, "idx", [P, M, Q], I32)
        with ExitStack() as c2:
            score = k.sb(c2, "score", [P, ETP, H])
            edge_scores(k, score, acc[:, :, 0:D], steps, k_d, rows, heads)
            softmax_numerators(k, score, ex, acc, scale, vv, idx, v_d, steps, rows)
        edge_messages(k, ex, acc, vv, idx, v_d, steps, rows, heads, clear=layer == 0)
        (finish0, finish1)[layer](k, acc)


def mix0(k, ahead):
    with ExitStack() as c:
        w1 = k.sb(c, "w1", [P, 8, 2, 512])
        w2 = k.sb(c, "w2", [P, 8, 4, D])
        gate = k.sb(c, "gate", [P, NT, 8])
        ln_scales(k, twice=True)
        xnt = k.acc[:, :, :].rearrange("p t w -> p (t w)")[:, 0:2 * NP].rearrange("p (c n) -> p c n", c=2)
        with ExitStack() as c2:
            router = k.sb(c2, "router", [P, NT, 8])
            columns(k, xnt, router, "Wr", 8, ("gamma", "beta"),
                    [(w1[:, :, :, :], k.io["W1_0"].rearrange("e (c p) f -> p e c f", p=P)),
                     (w2[:, :, :, :], k.io["W2_0"].rearrange("e (c p) d -> p e c d", p=P))])
            top2_gates(k, router, gate, 8, "br")
        experts(k, xnt, gate, w1, w2, 8, ahead)


def mix1(k, out):
    with ExitStack() as c:
        gate = k.sb(c, "gate", [P, NT, 4])
        score = k.sb(c, "score", [P, NT, 4])
        gs = k.sb(c, "gs", [P, NT, 20])
        gd = k.sb(c, "gd", [P, NT, 8])
        rs_all = k.sb(c, "rs_all", [P, GT, 20])
        ln_scales(k)
        with ExitStack() as c2:
            xnt = k.sb(c2, "xnt", [P, 2, NP])
            router = k.sb(c2, "router", [P, NT, 16])
            columns(k, xnt, router, "W_gat", 16, None)
            gate_tables(k, router, gs, gd, rs_all, xnt)
        yall = k.sb(c, "yall", [P, NT, 4, D])
        gate_sums(k, gs, gd, rs_all, yall, score)
        top2_gates(k, score, gate, 4)
        combine(k, yall, gate, out)


def kernel(x, src, dst, edge_type_8, node_type_4, L0_gnn_W_qkv, L0_gnn_b_qkv, L0_gnn_W_out, L0_gnn_b_out,
           L0_ffn_gamma, L0_ffn_beta, L0_ffn_Wr, L0_ffn_br, L0_ffn_W1, L0_ffn_b1, L0_ffn_W2, L0_ffn_b2,
           L1_gnn_k_linears, L1_gnn_q_linears, L1_gnn_v_linears, L1_gnn_a_linears, L1_gnn_relation_att,
           L1_gnn_relation_msg, L1_gnn_relation_pri, L1_gnn_skip, L1_ffn_W_gat, L1_ffn_att_src, L1_ffn_att_dst,
           L1_ffn_b_gat, L1_ffn_ln_gamma, L1_ffn_ln_beta, L1_ffn_W1, L1_ffn_b1, L1_ffn_W2, L1_ffn_b2,
           L1_ffn_edge_index):
    import concourse.bacc as bacc
    from concourse.bass_utils import run_bass_kernel_spmd

    a = np.ascontiguousarray

    def pad(v, n, fill):
        v = np.asarray(v)
        out = np.full((n,) + v.shape[1:], fill, v.dtype)
        out[:len(v)] = v
        return out

    last = NP - 1
    s, d, r = pad(src, EP, last), pad(dst, EP, last), pad(edge_type_8, EP, 0)
    g = np.asarray(L1_ffn_edge_index)

    def tiles(v, extra=0):
        v = np.asarray(v).reshape(-1, P).T
        return a(np.concatenate([v, np.zeros((P, extra), v.dtype)], 1)) if extra else a(v)

    def by_chunk(v):
        v = np.asarray(v)
        v = v.reshape(v.shape[:-1] + (-1, P))
        return a(np.moveaxis(v, -1, 0))

    data = {
        "x": pad(x, NP, 0), "src_rows": s.reshape(ETP, P), "rel_rows": r.reshape(ETP, P),
        "dst_rows": d.reshape(ETP, P), "dst_t": tiles(d), "dst_flat": d,
        "ntype": pad(node_type_4, NP, 0), "gsrc_t": tiles(g[0], 16), "gdst_t": tiles(g[1], 16),
        "W_qkv": L0_gnn_W_qkv, "b_qkv": L0_gnn_b_qkv, "W_out": L0_gnn_W_out, "b_out": L0_gnn_b_out,
        "gamma": by_chunk(L0_ffn_gamma), "beta": by_chunk(L0_ffn_beta), "Wr": L0_ffn_Wr, "br": L0_ffn_br,
        "W1_0": L0_ffn_W1, "b1_0": by_chunk(L0_ffn_b1), "W2_0": L0_ffn_W2, "b2_0": L0_ffn_b2,
        "k_linears": L1_gnn_k_linears, "q_linears": L1_gnn_q_linears, "v_linears": L1_gnn_v_linears,
        "a_linears": L1_gnn_a_linears,
        "att_t": np.transpose(np.asarray(L1_gnn_relation_att), (1, 3, 0, 2)),
        "msg": np.transpose(np.asarray(L1_gnn_relation_msg), (1, 2, 0, 3)),
        "pri": np.asarray(L1_gnn_relation_pri).reshape(-1), "skip": L1_gnn_skip, "W_gat": L1_ffn_W_gat,
        "att_src": np.asarray(L1_ffn_att_src).reshape(-1), "att_dst": np.asarray(L1_ffn_att_dst).reshape(-1),
        "b_gat": L1_ffn_b_gat, "ln_gamma": L1_ffn_ln_gamma, "ln_beta": L1_ffn_ln_beta,
        "W1_1": L1_ffn_W1, "b1_1": by_chunk(L1_ffn_b1), "W2_1": L1_ffn_W2, "b2_1": L1_ffn_b2,
    }
    nc = bacc.Bacc("TRN2", target_bir_lowering=False, num_devices=1)
    arrays, io = {}, {}
    for name, v in data.items():
        v = a(np.asarray(v))
        arrays["in_" + name] = v
        io[name] = nc.dram_tensor("in_" + name, list(v.shape), mybir.dt.from_np(v.dtype), kind="ExternalInput").ap()
    out = nc.dram_tensor("out", [N, D], F32, kind="ExternalOutput").ap()
    build(nc, io, out)
    res = run_bass_kernel_spmd(nc, [arrays], core_ids=[0])
    return res.results[0]["out"]
```
